# Optimizing a Trainium2 kernel written in Bass

```python
import numpy as np
import jax
import jax.numpy as jnp

def _softmax(x, axis=-1):
    return jax.nn.softmax(x, axis=axis)

def _gelu(x):
    return jax.nn.gelu(x, approximate=True)

def _silu(x):
    return jax.nn.silu(x)

def _sigmoid(x):
    return jax.nn.sigmoid(x)

def _layernorm(x, axis=-1, eps=1e-05):
    m = jnp.mean(x, axis=axis, keepdims=True)
    v = jnp.var(x, axis=axis, keepdims=True)
    return (x - m) / jnp.sqrt(v + eps)

def _scatter_add(tgt, idx, src, axis=0):
    return tgt.at[idx].add(src)

def _segment_sum(src, seg, n):
    return jax.ops.segment_sum(src, seg, n)
kernel_name = 'mk_xattn_seq_d4_seqx_r8_bd66a8'

def setup_inputs(seed: int=0):
    np.random.seed(seed)
    _w = jnp.asarray

    def _rec_inputs():
        import jax
        import jax.numpy as jnp
        _rk = jax.random.key(seed)
        x = -0.0005146 + 1 * jax.random.normal(jax.random.fold_in(_rk, 1), (2, 256, 256), jnp.float32)
        _lenS = 256 - jax.random.randint(jax.random.fold_in(_rk, 7), (2,), 0, max(1, 256 // 4) + 1, jnp.int32)
        _lenS2 = 512 - jax.random.randint(jax.random.fold_in(_rk, 8), (2,), 0, max(1, 512 // 4) + 1, jnp.int32)
        _ctx_2048P = jax.random.normal(jax.random.fold_in(_rk, 11), (2, 16, 256), jnp.float32)
        _ctx_2048c = jax.random.dirichlet(jax.random.fold_in(_rk, 511), 0.3 * jnp.ones((16,), jnp.float32), (2, 512))
        _ctx_2048t = jnp.einsum('bsk,bkd->bsd', _ctx_2048c, _ctx_2048P)
        _ctx_2048t = _ctx_2048t * jax.lax.rsqrt(jnp.mean(jnp.square(_ctx_2048t)) + 1e-12) * 0.953939
        ctx_2048 = -0.000392918 + 0.999932 * (_ctx_2048t + 0.3 * jax.random.normal(jax.random.fold_in(_rk, 611), (2, 512, 256), jnp.float32))
        _validS = jnp.arange(256)[None, :] < _lenS[:, None]
        _validS2 = jnp.arange(512)[None, :] < _lenS2[:, None]
        _causal = jnp.tril(jnp.ones((256, 256), dtype=bool))
        mask_BxS2_ik0 = jnp.where(jnp.broadcast_to(_validS2[:, :], (2, 512)), 0, 1).astype(jnp.int32)
        mask_BxS2_bf1 = jnp.ones((2, 512), dtype=bool)
        return (x, ctx_2048, mask_BxS2_ik0, mask_BxS2_bf1)
    x, ctx_2048, mask_BxS2_ik0, mask_BxS2_bf1 = _rec_inputs()

    def _L0_xattn_setup():
        import jax, jax.numpy as jnp
        import numpy as np
        B, P, K, H, NH = (4, 256, 32, 256, 16)
        DH = H // NH
        EPS = 1e-06

        def rmsnorm(x, w):
            var = jnp.mean(jnp.square(x), axis=-1, keepdims=True)
            return x * jax.lax.rsqrt(var + EPS) * w
        key = jax.random.key(seed)
        ks = jax.random.split(key, 12)
        s = 0.02
        return {'x': jax.random.normal(ks[0], (B, P, H), jnp.float32), 'latents': jax.random.normal(ks[1], (B, K, H), jnp.float32), 'attention_mask': jax.random.randint(ks[2], (B, P), 0, 2, jnp.int32), 'q_w': s * jax.random.normal(ks[3], (H, H), jnp.float32), 'q_b': jnp.zeros((H,), jnp.float32), 'kv_w': s * jax.random.normal(ks[4], (H, 2 * H), jnp.float32), 'kv_b': jnp.zeros((2 * H,), jnp.float32), 'out_w': s * jax.random.normal(ks[5], (H, H), jnp.float32), 'out_b': jnp.zeros((H,), jnp.float32), 'postnorm_w': jnp.ones((H,), jnp.float32), 'mlp_w1': s * jax.random.normal(ks[6], (H, 4 * H), jnp.float32), 'mlp_b1': jnp.zeros((4 * H,), jnp.float32), 'mlp_w2': s * jax.random.normal(ks[7], (4 * H, H), jnp.float32), 'mlp_b2': jnp.zeros((H,), jnp.float32)}
    _L0_xattn_all = _L0_xattn_setup()
    _L0_xattn_in = {k: v for k, v in _L0_xattn_all.items() if k in ('q_w', 'q_b', 'kv_w', 'kv_b', 'out_w', 'out_b', 'postnorm_w', 'mlp_w1', 'mlp_b1', 'mlp_w2', 'mlp_b2')}
    del _L0_xattn_all

    def _L1_xattn_setup():
        import jax, jax.numpy as jnp
        import numpy as np
        B, Q, S1, S2 = (4, 32, 256, 256)
        D, H, K, F = (256, 16, 128, 1024)
        LN_EPS = 1e-05

        def _layer_norm(x, scale, offset):
            mu = jnp.mean(x, axis=-1, keepdims=True)
            var = jnp.var(x, axis=-1, keepdims=True)
            return (x - mu) * jax.lax.rsqrt(var + LN_EPS) * scale + offset

        def _cross_attention(q_in, kv_in, wq, bq, wk, bk, wv, bv, wo, bo, bias_k, bias_v):
            b, q_len, _ = q_in.shape
            t = kv_in.shape[1]
            qh = (q_in @ wq + bq).reshape(b, q_len, H, K)
            kh = (kv_in @ wk + bk).reshape(b, t, H, K)
            vh = (kv_in @ wv + bv).reshape(b, t, H, K)
            kh = jnp.concatenate([kh, jnp.broadcast_to(bias_k, (b, 1, H, K))], axis=1)
            vh = jnp.concatenate([vh, jnp.broadcast_to(bias_v, (b, 1, H, K))], axis=1)
            scale = jnp.sqrt(jnp.asarray(K, q_in.dtype))
            logits = jnp.einsum('bqhk,bthk->bhqt', qh, kh) / scale
            weights = jax.nn.softmax(logits, axis=-1)
            ctx = jnp.einsum('bhqt,bthk->bqhk', weights, vh).reshape(b, q_len, H * K)
            return ctx @ wo + bo

        def _forward(x, xf_1, xf_2, ln1_scale, ln1_offset, wq1, bq1, wk1, bk1, wv1, bv1, wo1, bo1, bias_k1, bias_v1, ln2_scale, ln2_offset, wq2, bq2, wk2, bk2, wv2, bv2, wo2, bo2, bias_k2, bias_v2, ln_mlp_scale, ln_mlp_offset, w_fc1, b_fc1, w_fc2, b_fc2):
            res = x
            h = _layer_norm(x, ln1_scale, ln1_offset)
            x = res + _cross_attention(h, xf_1, wq1, bq1, wk1, bk1, wv1, bv1, wo1, bo1, bias_k1, bias_v1)
            res = x
            h = _layer_norm(x, ln2_scale, ln2_offset)
            x = res + _cross_attention(h, xf_2, wq2, bq2, wk2, bk2, wv2, bv2, wo2, bo2, bias_k2, bias_v2)
            h = _layer_norm(x, ln_mlp_scale, ln_mlp_offset)
            h = jax.nn.gelu(h @ w_fc1 + b_fc1, approximate=False) @ w_fc2 + b_fc2
            return x + h
        key = jax.random.key(seed)
        ks = iter(jax.random.split(key, 64))

        def rn(shape, s=0.02):
            return jax.random.normal(next(ks), shape, jnp.float32) * s
        inp = {'x': rn((B, Q, D), 1.0), 'xf_1': rn((B, S1, D), 1.0), 'xf_2': rn((B, S2, D), 1.0)}
        for i in (1, 2):
            inp[f'ln{i}_scale'] = jnp.ones((D,), jnp.float32)
            inp[f'ln{i}_offset'] = jnp.zeros((D,), jnp.float32)
            inp[f'wq{i}'] = rn((D, H * K))
            inp[f'bq{i}'] = jnp.zeros((H * K,), jnp.float32)
            inp[f'wk{i}'] = rn((D, H * K))
            inp[f'bk{i}'] = jnp.zeros((H * K,), jnp.float32)
            inp[f'wv{i}'] = rn((D, H * K))
            inp[f'bv{i}'] = jnp.zeros((H * K,), jnp.float32)
            inp[f'wo{i}'] = rn((H * K, D))
            inp[f'bo{i}'] = jnp.zeros((D,), jnp.float32)
            inp[f'bias_k{i}'] = rn((1, 1, H, K))
            inp[f'bias_v{i}'] = rn((1, 1, H, K))
        inp['ln_mlp_scale'] = jnp.ones((D,), jnp.float32)
        inp['ln_mlp_offset'] = jnp.zeros((D,), jnp.float32)
        inp['w_fc1'] = rn((D, F))
        inp['b_fc1'] = jnp.zeros((F,), jnp.float32)
        inp['w_fc2'] = rn((F, D))
        inp['b_fc2'] = jnp.zeros((D,), jnp.float32)
        return inp
    _L1_xattn_all = _L1_xattn_setup()
    _L1_xattn_in = {k: v for k, v in _L1_xattn_all.items() if k in ('ln1_scale', 'ln1_offset', 'wq1', 'bq1', 'wk1', 'bk1', 'wv1', 'bv1', 'wo1', 'bo1', 'bias_k1', 'bias_v1', 'ln2_scale', 'ln2_offset', 'wq2', 'bq2', 'wk2', 'bk2', 'wv2', 'bv2', 'wo2', 'bo2', 'bias_k2', 'bias_v2', 'ln_mlp_scale', 'ln_mlp_offset', 'w_fc1', 'b_fc1', 'w_fc2', 'b_fc2')}
    del _L1_xattn_all

    def _L2_xattn_setup():
        import jax, jax.numpy as jnp
        import numpy as np
        HIDDEN = 256
        HEADS = 16
        HEAD_DIM = HIDDEN // HEADS
        LN_EPS = 1e-05
        GATE_INIT = 0.5

        def _layer_norm(x, gamma, beta):
            mu = jnp.mean(x, axis=-1, keepdims=True)
            var = jnp.mean(jnp.square(x - mu), axis=-1, keepdims=True)
            return (x - mu) * jax.lax.rsqrt(var + LN_EPS) * gamma + beta
        key = jax.random.key(seed)
        ks = jax.random.split(key, 8)
        B, T_TEXT, T_AUDIO = (4, 256, 1500)
        s = 0.02
        return {'hidden_states': jax.random.normal(ks[0], (B, T_TEXT, HIDDEN), jnp.float32), 'audio_kv': jax.random.normal(ks[1], (B, T_AUDIO, HIDDEN), jnp.float32), 'audio_attention_mask': jnp.ones((B, T_AUDIO), dtype=bool), 'Wq': jax.random.normal(ks[2], (HIDDEN, HIDDEN), jnp.float32) * s, 'Wk': jax.random.normal(ks[3], (HIDDEN, HIDDEN), jnp.float32) * s, 'Wv': jax.random.normal(ks[4], (HIDDEN, HIDDEN), jnp.float32) * s, 'Wo': jax.random.normal(ks[5], (HIDDEN, HIDDEN), jnp.float32) * s, 'ln_gamma': jnp.ones((HIDDEN,), jnp.float32), 'ln_beta': jnp.zeros((HIDDEN,), jnp.float32), 'gate': jnp.array([GATE_INIT], jnp.float32)}
    _L2_xattn_all = _L2_xattn_setup()
    _L2_xattn_in = {k: v for k, v in _L2_xattn_all.items() if k in ('Wq', 'Wk', 'Wv', 'Wo', 'ln_gamma', 'ln_beta', 'gate')}
    del _L2_xattn_all

    def _L3_xattn_setup():
        import jax, jax.numpy as jnp
        import numpy as np
        D = 256
        H = 16
        HD = D // H
        INNER = 4 * D
        EPS = 1e-05

        def layer_norm(x, w, b):
            mu = jnp.mean(x, axis=-1, keepdims=True)
            var = jnp.mean(jnp.square(x - mu), axis=-1, keepdims=True)
            return (x - mu) * jax.lax.rsqrt(var + EPS) * w + b
        key = jax.random.key(seed)
        ks = jax.random.split(key, 12)
        B, LQ, LK = (4, 128, 256)
        std = 0.02
        inp = {'hidden_states': jax.random.normal(ks[0], (B, LQ, D), jnp.float32), 'encoder_hidden_states': jax.random.normal(ks[1], (B, LK, D), jnp.float32), 'encoder_attention_mask': jnp.ones((B, LK), dtype=bool), 'ln1_w': jnp.ones((D,), jnp.float32), 'ln1_b': jnp.zeros((D,), jnp.float32), 'q_w': jax.random.normal(ks[2], (D, D), jnp.float32) * std, 'q_b': jnp.zeros((D,), jnp.float32), 'k_w': jax.random.normal(ks[3], (D, D), jnp.float32) * std, 'k_b': jnp.zeros((D,), jnp.float32), 'v_w': jax.random.normal(ks[4], (D, D), jnp.float32) * std, 'v_b': jnp.zeros((D,), jnp.float32), 'cproj_w': jax.random.normal(ks[5], (D, D), jnp.float32) * std, 'cproj_b': jnp.zeros((D,), jnp.float32), 'ln2_w': jnp.ones((D,), jnp.float32), 'ln2_b': jnp.zeros((D,), jnp.float32), 'fc_w': jax.random.normal(ks[6], (D, INNER), jnp.float32) * std, 'fc_b': jnp.zeros((INNER,), jnp.float32), 'proj_w': jax.random.normal(ks[7], (INNER, D), jnp.float32) * std, 'proj_b': jnp.zeros((D,), jnp.float32)}
        return inp
    _L3_xattn_all = _L3_xattn_setup()
    _L3_xattn_in = {k: v for k, v in _L3_xattn_all.items() if k in ('ln1_w', 'ln1_b', 'q_w', 'q_b', 'k_w', 'k_b', 'v_w', 'v_b', 'cproj_w', 'cproj_b', 'ln2_w', 'ln2_b', 'fc_w', 'fc_b', 'proj_w', 'proj_b')}
    del _L3_xattn_all
    return {'x': x, 'ctx_2048': ctx_2048, 'mask_BxS2_ik0': mask_BxS2_ik0, 'mask_BxS2_bf1': mask_BxS2_bf1, 'L0_xattn_q_w': _L0_xattn_in['q_w'], 'L0_xattn_q_b': _L0_xattn_in['q_b'], 'L0_xattn_kv_w': _L0_xattn_in['kv_w'], 'L0_xattn_kv_b': _L0_xattn_in['kv_b'], 'L0_xattn_out_w': _L0_xattn_in['out_w'], 'L0_xattn_out_b': _L0_xattn_in['out_b'], 'L0_xattn_postnorm_w': _L0_xattn_in['postnorm_w'], 'L0_xattn_mlp_w1': _L0_xattn_in['mlp_w1'], 'L0_xattn_mlp_b1': _L0_xattn_in['mlp_b1'], 'L0_xattn_mlp_w2': _L0_xattn_in['mlp_w2'], 'L0_xattn_mlp_b2': _L0_xattn_in['mlp_b2'], 'L1_xattn_ln1_scale': _L1_xattn_in['ln1_scale'], 'L1_xattn_ln1_offset': _L1_xattn_in['ln1_offset'], 'L1_xattn_wq1': _L1_xattn_in['wq1'], 'L1_xattn_bq1': _L1_xattn_in['bq1'], 'L1_xattn_wk1': _L1_xattn_in['wk1'], 'L1_xattn_bk1': _L1_xattn_in['bk1'], 'L1_xattn_wv1': _L1_xattn_in['wv1'], 'L1_xattn_bv1': _L1_xattn_in['bv1'], 'L1_xattn_wo1': _L1_xattn_in['wo1'], 'L1_xattn_bo1': _L1_xattn_in['bo1'], 'L1_xattn_bias_k1': _L1_xattn_in['bias_k1'], 'L1_xattn_bias_v1': _L1_xattn_in['bias_v1'], 'L1_xattn_ln2_scale': _L1_xattn_in['ln2_scale'], 'L1_xattn_ln2_offset': _L1_xattn_in['ln2_offset'], 'L1_xattn_wq2': _L1_xattn_in['wq2'], 'L1_xattn_bq2': _L1_xattn_in['bq2'], 'L1_xattn_wk2': _L1_xattn_in['wk2'], 'L1_xattn_bk2': _L1_xattn_in['bk2'], 'L1_xattn_wv2': _L1_xattn_in['wv2'], 'L1_xattn_bv2': _L1_xattn_in['bv2'], 'L1_xattn_wo2': _L1_xattn_in['wo2'], 'L1_xattn_bo2': _L1_xattn_in['bo2'], 'L1_xattn_bias_k2': _L1_xattn_in['bias_k2'], 'L1_xattn_bias_v2': _L1_xattn_in['bias_v2'], 'L1_xattn_ln_mlp_scale': _L1_xattn_in['ln_mlp_scale'], 'L1_xattn_ln_mlp_offset': _L1_xattn_in['ln_mlp_offset'], 'L1_xattn_w_fc1': _L1_xattn_in['w_fc1'], 'L1_xattn_b_fc1': _L1_xattn_in['b_fc1'], 'L1_xattn_w_fc2': _L1_xattn_in['w_fc2'], 'L1_xattn_b_fc2': _L1_xattn_in['b_fc2'], 'L2_xattn_Wq': _L2_xattn_in['Wq'], 'L2_xattn_Wk': _L2_xattn_in['Wk'], 'L2_xattn_Wv': _L2_xattn_in['Wv'], 'L2_xattn_Wo': _L2_xattn_in['Wo'], 'L2_xattn_ln_gamma': _L2_xattn_in['ln_gamma'], 'L2_xattn_ln_beta': _L2_xattn_in['ln_beta'], 'L2_xattn_gate': _L2_xattn_in['gate'], 'L3_xattn_ln1_w': _L3_xattn_in['ln1_w'], 'L3_xattn_ln1_b': _L3_xattn_in['ln1_b'], 'L3_xattn_q_w': _L3_xattn_in['q_w'], 'L3_xattn_q_b': _L3_xattn_in['q_b'], 'L3_xattn_k_w': _L3_xattn_in['k_w'], 'L3_xattn_k_b': _L3_xattn_in['k_b'], 'L3_xattn_v_w': _L3_xattn_in['v_w'], 'L3_xattn_v_b': _L3_xattn_in['v_b'], 'L3_xattn_cproj_w': _L3_xattn_in['cproj_w'], 'L3_xattn_cproj_b': _L3_xattn_in['cproj_b'], 'L3_xattn_ln2_w': _L3_xattn_in['ln2_w'], 'L3_xattn_ln2_b': _L3_xattn_in['ln2_b'], 'L3_xattn_fc_w': _L3_xattn_in['fc_w'], 'L3_xattn_fc_b': _L3_xattn_in['fc_b'], 'L3_xattn_proj_w': _L3_xattn_in['proj_w'], 'L3_xattn_proj_b': _L3_xattn_in['proj_b']}

def reference(x, ctx_2048, mask_BxS2_ik0, mask_BxS2_bf1, L0_xattn_q_w, L0_xattn_q_b, L0_xattn_kv_w, L0_xattn_kv_b, L0_xattn_out_w, L0_xattn_out_b, L0_xattn_postnorm_w, L0_xattn_mlp_w1, L0_xattn_mlp_b1, L0_xattn_mlp_w2, L0_xattn_mlp_b2, L1_xattn_ln1_scale, L1_xattn_ln1_offset, L1_xattn_wq1, L1_xattn_bq1, L1_xattn_wk1, L1_xattn_bk1, L1_xattn_wv1, L1_xattn_bv1, L1_xattn_wo1, L1_xattn_bo1, L1_xattn_bias_k1, L1_xattn_bias_v1, L1_xattn_ln2_scale, L1_xattn_ln2_offset, L1_xattn_wq2, L1_xattn_bq2, L1_xattn_wk2, L1_xattn_bk2, L1_xattn_wv2, L1_xattn_bv2, L1_xattn_wo2, L1_xattn_bo2, L1_xattn_bias_k2, L1_xattn_bias_v2, L1_xattn_ln_mlp_scale, L1_xattn_ln_mlp_offset, L1_xattn_w_fc1, L1_xattn_b_fc1, L1_xattn_w_fc2, L1_xattn_b_fc2, L2_xattn_Wq, L2_xattn_Wk, L2_xattn_Wv, L2_xattn_Wo, L2_xattn_ln_gamma, L2_xattn_ln_beta, L2_xattn_gate, L3_xattn_ln1_w, L3_xattn_ln1_b, L3_xattn_q_w, L3_xattn_q_b, L3_xattn_k_w, L3_xattn_k_b, L3_xattn_v_w, L3_xattn_v_b, L3_xattn_cproj_w, L3_xattn_cproj_b, L3_xattn_ln2_w, L3_xattn_ln2_b, L3_xattn_fc_w, L3_xattn_fc_b, L3_xattn_proj_w, L3_xattn_proj_b):
    import jax
    import jax.numpy as jnp

    def _L0_xattn_ref(x, latents, attention_mask, q_w, q_b, kv_w, kv_b, out_w, out_b, postnorm_w, mlp_w1, mlp_b1, mlp_w2, mlp_b2):
        import jax, jax.numpy as jnp
        import numpy as np
        B, P, K, H, NH = (4, 256, 32, 256, 16)
        DH = H // NH
        EPS = 1e-06

        def rmsnorm(x, w):
            var = jnp.mean(jnp.square(x), axis=-1, keepdims=True)
            return x * jax.lax.rsqrt(var + EPS) * w
        b, p, _ = x.shape
        k_len = latents.shape[1]
        residual = latents
        h = jnp.concatenate([x, latents], axis=1)
        q = (latents @ q_w + q_b).reshape(b, k_len, NH, DH)
        kv = (h @ kv_w + kv_b).reshape(b, p + k_len, NH, DH, 2)
        kmat, v = (kv[..., 0], kv[..., 1])
        attn = jnp.einsum('bkhd,bnhd->bhkn', q, kmat) / DH
        full_mask = jnp.concatenate([attention_mask.astype(bool), jnp.ones((b, k_len), bool)], axis=-1)
        attn = jnp.where(full_mask[:, None, None, :], attn, -jnp.inf)
        attn = jax.nn.softmax(attn.astype(jnp.float32), axis=-1).astype(q.dtype)
        attn_out = jnp.einsum('bhkn,bnhd->bkhd', attn, v).reshape(b, k_len, H)
        attn_out = attn_out @ out_w + out_b + residual
        out = rmsnorm(attn_out, postnorm_w)
        out = jax.nn.gelu(out @ mlp_w1 + mlp_b1) @ mlp_w2 + mlp_b2
        return out + residual

    def _L1_xattn_ref(x, xf_1, xf_2, ln1_scale, ln1_offset, wq1, bq1, wk1, bk1, wv1, bv1, wo1, bo1, bias_k1, bias_v1, ln2_scale, ln2_offset, wq2, bq2, wk2, bk2, wv2, bv2, wo2, bo2, bias_k2, bias_v2, ln_mlp_scale, ln_mlp_offset, w_fc1, b_fc1, w_fc2, b_fc2):
        import jax, jax.numpy as jnp
        import numpy as np
        B, Q, S1, S2 = (4, 32, 256, 256)
        D, H, K, F = (256, 16, 128, 1024)
        LN_EPS = 1e-05

        def _layer_norm(x, scale, offset):
            mu = jnp.mean(x, axis=-1, keepdims=True)
            var = jnp.var(x, axis=-1, keepdims=True)
            return (x - mu) * jax.lax.rsqrt(var + LN_EPS) * scale + offset

        def _cross_attention(q_in, kv_in, wq, bq, wk, bk, wv, bv, wo, bo, bias_k, bias_v):
            b, q_len, _ = q_in.shape
            t = kv_in.shape[1]
            qh = (q_in @ wq + bq).reshape(b, q_len, H, K)
            kh = (kv_in @ wk + bk).reshape(b, t, H, K)
            vh = (kv_in @ wv + bv).reshape(b, t, H, K)
            kh = jnp.concatenate([kh, jnp.broadcast_to(bias_k, (b, 1, H, K))], axis=1)
            vh = jnp.concatenate([vh, jnp.broadcast_to(bias_v, (b, 1, H, K))], axis=1)
            scale = jnp.sqrt(jnp.asarray(K, q_in.dtype))
            logits = jnp.einsum('bqhk,bthk->bhqt', qh, kh) / scale
            weights = jax.nn.softmax(logits, axis=-1)
            ctx = jnp.einsum('bhqt,bthk->bqhk', weights, vh).reshape(b, q_len, H * K)
            return ctx @ wo + bo

        def _forward(x, xf_1, xf_2, ln1_scale, ln1_offset, wq1, bq1, wk1, bk1, wv1, bv1, wo1, bo1, bias_k1, bias_v1, ln2_scale, ln2_offset, wq2, bq2, wk2, bk2, wv2, bv2, wo2, bo2, bias_k2, bias_v2, ln_mlp_scale, ln_mlp_offset, w_fc1, b_fc1, w_fc2, b_fc2):
            res = x
            h = _layer_norm(x, ln1_scale, ln1_offset)
            x = res + _cross_attention(h, xf_1, wq1, bq1, wk1, bk1, wv1, bv1, wo1, bo1, bias_k1, bias_v1)
            res = x
            h = _layer_norm(x, ln2_scale, ln2_offset)
            x = res + _cross_attention(h, xf_2, wq2, bq2, wk2, bk2, wv2, bv2, wo2, bo2, bias_k2, bias_v2)
            h = _layer_norm(x, ln_mlp_scale, ln_mlp_offset)
            h = jax.nn.gelu(h @ w_fc1 + b_fc1, approximate=False) @ w_fc2 + b_fc2
            return x + h
        return _forward(x, xf_1, xf_2, ln1_scale, ln1_offset, wq1, bq1, wk1, bk1, wv1, bv1, wo1, bo1, bias_k1, bias_v1, ln2_scale, ln2_offset, wq2, bq2, wk2, bk2, wv2, bv2, wo2, bo2, bias_k2, bias_v2, ln_mlp_scale, ln_mlp_offset, w_fc1, b_fc1, w_fc2, b_fc2)

    def _L2_xattn_ref(hidden_states, audio_kv, audio_attention_mask, Wq, Wk, Wv, Wo, ln_gamma, ln_beta, gate):
        import jax, jax.numpy as jnp
        import numpy as np
        HIDDEN = 256
        HEADS = 16
        HEAD_DIM = HIDDEN // HEADS
        LN_EPS = 1e-05
        GATE_INIT = 0.5

        def _layer_norm(x, gamma, beta):
            mu = jnp.mean(x, axis=-1, keepdims=True)
            var = jnp.mean(jnp.square(x - mu), axis=-1, keepdims=True)
            return (x - mu) * jax.lax.rsqrt(var + LN_EPS) * gamma + beta
        B, Tt, D = hidden_states.shape
        Ta = audio_kv.shape[1]
        scale = HEAD_DIM ** (-0.5)
        a = _layer_norm(audio_kv, ln_gamma, ln_beta)
        Q = (hidden_states @ Wq.T).reshape(B, Tt, HEADS, HEAD_DIM).transpose(0, 2, 1, 3)
        K = (a @ Wk.T).reshape(B, Ta, HEADS, HEAD_DIM).transpose(0, 2, 1, 3)
        V = (a @ Wv.T).reshape(B, Ta, HEADS, HEAD_DIM).transpose(0, 2, 1, 3)
        scores = jnp.einsum('bhtd,bhsd->bhts', Q, K) * scale
        mask = audio_attention_mask[:, None, None, :]
        scores = jnp.where(mask, scores, jnp.float32(-jnp.inf))
        attn = jax.nn.softmax(scores, axis=-1)
        out = jnp.einsum('bhts,bhsd->bhtd', attn, V)
        out = out.transpose(0, 2, 1, 3).reshape(B, Tt, D)
        out = out @ Wo.T
        return hidden_states + jnp.tanh(gate) * out

    def _L3_xattn_ref(hidden_states, encoder_hidden_states, encoder_attention_mask, ln1_w, ln1_b, q_w, q_b, k_w, k_b, v_w, v_b, cproj_w, cproj_b, ln2_w, ln2_b, fc_w, fc_b, proj_w, proj_b):
        import jax, jax.numpy as jnp
        import numpy as np
        D = 256
        H = 16
        HD = D // H
        INNER = 4 * D
        EPS = 1e-05

        def layer_norm(x, w, b):
            mu = jnp.mean(x, axis=-1, keepdims=True)
            var = jnp.mean(jnp.square(x - mu), axis=-1, keepdims=True)
            return (x - mu) * jax.lax.rsqrt(var + EPS) * w + b
        B, LQ, _ = hidden_states.shape
        LK = encoder_hidden_states.shape[1]
        residual = hidden_states
        x = layer_norm(hidden_states, ln1_w, ln1_b)
        q = (x @ q_w + q_b).reshape(B, LQ, H, HD).transpose(0, 2, 1, 3)
        k = (encoder_hidden_states @ k_w + k_b).reshape(B, LK, H, HD).transpose(0, 2, 1, 3)
        v = (encoder_hidden_states @ v_w + v_b).reshape(B, LK, H, HD).transpose(0, 2, 1, 3)
        scale = 1.0 / np.sqrt(HD).astype(np.float32)
        scores = jnp.einsum('bhqd,bhkd->bhqk', q, k) * scale
        mask = encoder_attention_mask[:, None, None, :]
        mask_value = jnp.finfo(scores.dtype).min
        scores = jnp.where(mask, scores, mask_value)
        attn = jax.nn.softmax(scores, axis=-1)
        out = jnp.einsum('bhqk,bhkd->bhqd', attn, v)
        out = out.transpose(0, 2, 1, 3).reshape(B, LQ, D)
        out = out @ cproj_w + cproj_b
        hidden = out + residual
        residual = hidden
        y = layer_norm(hidden, ln2_w, ln2_b)
        y = jax.nn.gelu(y @ fc_w + fc_b, approximate=True)
        y = y @ proj_w + proj_b
        return residual + y
    x = _L0_xattn_ref(ctx_2048, x, mask_BxS2_ik0, L0_xattn_q_w, L0_xattn_q_b, L0_xattn_kv_w, L0_xattn_kv_b, L0_xattn_out_w, L0_xattn_out_b, L0_xattn_postnorm_w, L0_xattn_mlp_w1, L0_xattn_mlp_b1, L0_xattn_mlp_w2, L0_xattn_mlp_b2)
    x = _L1_xattn_ref(x, ctx_2048, ctx_2048, L1_xattn_ln1_scale, L1_xattn_ln1_offset, L1_xattn_wq1, L1_xattn_bq1, L1_xattn_wk1, L1_xattn_bk1, L1_xattn_wv1, L1_xattn_bv1, L1_xattn_wo1, L1_xattn_bo1, L1_xattn_bias_k1, L1_xattn_bias_v1, L1_xattn_ln2_scale, L1_xattn_ln2_offset, L1_xattn_wq2, L1_xattn_bq2, L1_xattn_wk2, L1_xattn_bk2, L1_xattn_wv2, L1_xattn_bv2, L1_xattn_wo2, L1_xattn_bo2, L1_xattn_bias_k2, L1_xattn_bias_v2, L1_xattn_ln_mlp_scale, L1_xattn_ln_mlp_offset, L1_xattn_w_fc1, L1_xattn_b_fc1, L1_xattn_w_fc2, L1_xattn_b_fc2)
    x = _L2_xattn_ref(x, ctx_2048, mask_BxS2_bf1, L2_xattn_Wq, L2_xattn_Wk, L2_xattn_Wv, L2_xattn_Wo, L2_xattn_ln_gamma, L2_xattn_ln_beta, L2_xattn_gate)
    x = _L3_xattn_ref(x, ctx_2048, mask_BxS2_bf1, L3_xattn_ln1_w, L3_xattn_ln1_b, L3_xattn_q_w, L3_xattn_q_b, L3_xattn_k_w, L3_xattn_k_b, L3_xattn_v_w, L3_xattn_v_b, L3_xattn_cproj_w, L3_xattn_cproj_b, L3_xattn_ln2_w, L3_xattn_ln2_b, L3_xattn_fc_w, L3_xattn_fc_b, L3_xattn_proj_w, L3_xattn_proj_b)
    return x

_drawn_inputs = setup_inputs


def setup_inputs(seed=0):
    import zlib

    import numpy as np

    out = dict(_drawn_inputs(seed))
    spreads = {'L0_xattn_q_b': (0.0, 0.8),
     'L0_xattn_kv_b': (0.0, 0.8),
     'L0_xattn_out_b': (0.0, 0.703),
     'L0_xattn_postnorm_w': (1.0, 0.6),
     'L0_xattn_mlp_b1': (0.0, 0.1),
     'L0_xattn_mlp_b2': (0.0, 0.1),
     'L1_xattn_ln1_scale': (1.0, 0.6),
     'L1_xattn_ln1_offset': (0.0, 0.8),
     'L1_xattn_bq1': (0.0, 0.8),
     'L1_xattn_bk1': (0.0, 2.0),
     'L1_xattn_bv1': (0.0, 0.1),
     'L1_xattn_bo1': (0.0, 0.1),
     'L1_xattn_ln2_scale': (1.0, 0.6),
     'L1_xattn_ln2_offset': (0.0, 0.8),
     'L1_xattn_bq2': (0.0, 0.8),
     'L1_xattn_bk2': (0.0, 2.0),
     'L1_xattn_bv2': (0.0, 0.1),
     'L1_xattn_bo2': (0.0, 0.1),
     'L1_xattn_ln_mlp_scale': (1.0, 0.6),
     'L1_xattn_ln_mlp_offset': (0.0, 0.699),
     'L1_xattn_b_fc1': (0.0, 0.1),
     'L1_xattn_b_fc2': (0.0, 0.1),
     'L2_xattn_ln_gamma': (1.0, 0.6),
     'L2_xattn_ln_beta': (0.0, 0.8),
     'L3_xattn_ln1_w': (1.0, 0.6),
     'L3_xattn_ln1_b': (0.0, 0.8),
     'L3_xattn_q_b': (0.0, 0.8),
     'L3_xattn_k_b': (0.0, 2.0),
     'L3_xattn_v_b': (0.0, 0.28),
     'L3_xattn_cproj_b': (0.0, 0.1),
     'L3_xattn_ln2_w': (1.0, 0.6),
     'L3_xattn_ln2_b': (0.0, 0.716),
     'L3_xattn_fc_b': (0.0, 0.268),
     'L3_xattn_proj_b': (0.0, 0.1)}
    factors = {'L0_xattn_q_w': 8.0,
     'L0_xattn_kv_w': 8.0,
     'L0_xattn_out_w': 8.0,
     'L1_xattn_wq1': 8.0,
     'L1_xattn_wk1': 8.0,
     'L1_xattn_bias_k1': 64.0,
     'L1_xattn_bias_v1': 64.0,
     'L1_xattn_wq2': 8.0,
     'L1_xattn_wk2': 8.0,
     'L1_xattn_bias_k2': 64.0,
     'L1_xattn_bias_v2': 64.0,
     'L2_xattn_Wq': 8.0,
     'L2_xattn_Wk': 8.0,
     'L3_xattn_q_w': 8.0,
     'L3_xattn_k_w': 8.0}
    for name, (base, spread) in spreads.items():
        noise = np.random.default_rng([zlib.crc32(name.encode()), seed]).standard_normal(out[name].shape)
        drawn = base * np.exp(spread * noise) if base else spread * noise
        out[name] = jnp.asarray(drawn.astype(out[name].dtype))
    for name, factor in factors.items():
        out[name] = (out[name] * factor).astype(out[name].dtype)
    return out
```

```python
from contextlib import ExitStack

import numpy as np

import concourse.bass as bass
from concourse import mybir

F32 = mybir.dt.float32
F32R = mybir.dt.float32r
I32 = mybir.dt.int32
U8 = mybir.dt.uint8
ALU = mybir.AluOpType
ACT = mybir.ActivationFunctionType
AX = mybir.AxisListType

P = 128
B = 2
Q = 256
S = 512
D = 256
KT = D // P
ROWS = B * Q
RT = ROWS // P
CT = B * S // P
H = 16
DN = D // H
DW = 128
F = 1024
FT = F // P
PAIRS = H // 2
MASKED = -float(2 ** 100)
BANKS = 8


def raw(ap):
    return ap.bitcast(F32)


class Ring:

    def __init__(self, banks, sem, name, regular):
        self.banks = banks
        self.n = len(banks)
        self.full = sem(f"{name}_full")
        self.hi_done = sem(f"{name}_hi_done")
        self.free = [sem(f"{name}_free{i}") for i in range(self.n)]
        self.regular = regular

    def bank(self, job):
        return self.banks[job % self.n]

    def wait_bank(self, pe, job, late=0):
        if self.regular or job >= self.n:
            pe.wait_ge(self.free[job % self.n], job // self.n + late)

    def wait_evacuated(self, engine, job, late=0):
        engine.wait_ge(self.free[job % self.n], job // self.n + 1 + late)

    def freed_by(self, job):
        return self.free[job % self.n]


def product3(nc, out, lhs, rhs, start, stop, loose=False):
    (lh, ll), (rh, rl) = lhs, rhs
    nc.tensor.matmul(out, lh, rh, start=start, stop=False, skip_group_check=loose)
    nc.tensor.matmul(out, lh, rl, start=False, stop=False, skip_group_check=loose)
    return nc.tensor.matmul(out, ll, rh, start=False, stop=stop, skip_group_check=loose)


def both(pair, index):
    return tuple(t[index] for t in pair)


class Chain:

    def __init__(self, engine, done):
        self.engine, self.done, self.count = engine, done, 0

    def __call__(self, instruction):
        self.count += 1
        instruction.then_inc(self.done, 1)
        self.engine.wait_ge(self.done, self.count)


def row_statistics(nc, link, rows, tiles, stats, moments, shifted, eps, centred):
    for t in range(tiles):
        last = nc.vector.bn_stats(stats[:, t, :], rows[:, t, :])
        if t == tiles - 1:
            link(last)
    for t in range(tiles):
        last = nc.vector.bn_aggr(moments[:, t, :], stats[:, t, :])
        if t == tiles - 1:
            link(last)
    if not centred:
        link(nc.vector.tensor_tensor(shifted[:, 0:tiles], moments[:, 0:tiles, 0], moments[:, 0:tiles, 0], ALU.mult))
        link(nc.vector.tensor_tensor(shifted[:, 0:tiles], shifted[:, 0:tiles], moments[:, 0:tiles, 1], ALU.add))
        return nc.vector.tensor_scalar(shifted[:, 0:tiles], shifted[:, 0:tiles], eps, None, ALU.add)
    return nc.vector.tensor_scalar(shifted[:, 0:tiles], moments[:, 0:tiles, 1], eps, None, ALU.add)


class Phase:

    def __init__(self, nc, name):
        self.nc, self.name, self.ctx, self.sems = nc, name, ExitStack(), []

    def __enter__(self):
        self.ctx.__enter__()
        return self

    def __exit__(self, *error):
        self.ctx.__exit__(*error)
        if self.sems and not error[0]:
            self.nc.clear_and_free_semaphores(self.sems)
            self.nc.all_engine_barrier()

    def sb(self, name, shape, dt=F32):
        return self.ctx.enter_context(self.nc.sbuf_tensor(f"{self.name}_{name}", shape, dt))

    def hilo(self, name, shape):
        return self.sb(name + "_hi", shape, F32R), self.sb(name + "_lo", shape, F32R)

    def psum(self, n):
        return [self.ctx.enter_context(self.nc.psum_tensor(f"{self.name}_bank{i}", [P, 512], F32)) for i in range(n)]

    def sem(self, name):
        self.sems.append(self.nc.alloc_semaphore(f"{self.name}_{name}"))
        return self.sems[-1]

    def ring(self, banks, regular=False):
        return Ring(banks, self.sem, "ring", regular)

    def block(self):
        return self.ctx.enter_context(self.nc.Block())


def transpose_context(nc, io, keep):
    with Phase(nc, "prep") as ph:
        ctx_rows = ph.sb("ctx_rows", [P, CT, D])
        ring = ph.ring(ph.psum(4))
        loaded, cleared, ident_ready = ph.sem("loaded"), ph.sem("cleared"), ph.sem("ident_ready")
        block = ph.block()
        jobs = [(keep["ctxT"], ctx_rows, kt, 4 * g) for kt in range(KT) for g in range(CT // 4)]
        jobs += [(keep["latT"], keep["x"], kt, 0) for kt in range(KT)]

        @block.sync
        def _(sp):
            sp.dma_start(ctx_rows[:, :, :], io["ctx_2048"].rearrange("b (t p) d -> p (b t) d", p=P)).then_inc(loaded, 16)
            sp.dma_start(keep["x"][:, :, :], io["x"].rearrange("b (t p) d -> p (b t) d", p=P)).then_inc(loaded, 16)

        @block.gpsimd
        def _(pool):
            nc.gpsimd.memset(keep["ident"][:, :], 0.0).then_inc(cleared, 1)
            pool.wait_ge(cleared, 1)
            nc.gpsimd.affine_select(out=keep["ident"][:, :], in_=keep["ident"][:, :], compare_op=ALU.not_equal, fill=1.0,
                                    base=0, pattern=[[-1, P]], channel_multiplier=1).then_inc(ident_ready, 1)

        @block.tensor
        def _(pe):
            pe.wait_ge(loaded, 32)
            pe.wait_ge(ident_ready, 1)
            for job, (_, rows, kt, t0) in enumerate(jobs):
                ring.wait_bank(pe, job)
                for t in range(4):
                    last = nc.tensor.transpose(ring.bank(job)[:, t * P:(t + 1) * P],
                                               rows[:, t0 + t, kt * P:(kt + 1) * P], keep["ident"][:, :])
                last.then_inc(ring.full, 1)

        @block.scalar
        def _(act):
            for job, (to, _, kt, t0) in enumerate(jobs):
                act.wait_ge(ring.full, job + 1)
                nc.scalar.copy(to[0][:, kt, t0 * P:t0 * P + 512], ring.bank(job)[:, :]).then_inc(ring.hi_done, 1)

        @block.vector
        def _(dve):
            for job, (to, _, kt, t0) in enumerate(jobs):
                dve.wait_ge(ring.hi_done, job + 1)
                nc.vector.tensor_tensor(to[1][:, kt, t0 * P:t0 * P + 512], ring.bank(job)[:, :],
                                        raw(to[0][:, kt, t0 * P:t0 * P + 512]), ALU.subtract).then_inc(ring.freed_by(job), 1)


def narrow_attention(nc, io, keep, cfg):
    name, nk, queries, sources = cfg["name"], cfg["nk"], cfg["queries"], cfg["keys"]
    nkt = nk // P
    extra = nk - S
    quads = H // 4
    units = B * quads
    with Phase(nc, name) as ph:
        w = ph.hilo("w", [P, 5, 512])
        bias = ph.sb("bias", [P, 8])
        out_bias = ph.sb("out_bias", [P, D])
        gate = ph.sb("gate", [P, 1])
        mask_raw = ph.sb("mask_raw", [1, B * S], cfg["mask_dtype"])
        mask_row = ph.sb("mask_row", [1, B, nk], F32R)
        qT = ph.hilo("qT", [P, KT, ROWS])
        kT = ph.hilo("kT", [P, KT, B * nk])
        v = ph.sb("v", [P, B * nkt, H * 32])
        k_stack = [ph.sb(f"k_stack{i}", [P, 2, nk], F32R) for i in range(2)]
        q_stack = [ph.sb(f"q_stack{i}", [P, 4, Q], F32R) for i in range(2)]
        probs = ph.sb("probs", [P, 4, nk])
        probsT = ph.sb("probsT", [P, 6, 2 * nkt * P])
        stage = probsT[:, :, :].rearrange("p s n -> p (s n)")[:, 0:5 * 512].rearrange("p (i n) -> p i n", i=5)
        neg_max, row_sum, inverse = ph.sb("neg_max", [P, 4]), ph.sb("row_sum", [P, 4]), ph.sb("inverse", [P, 4])
        attended = ph.hilo("attended", [P, quads, ROWS])
        banks = ph.psum(4)
        scores = [ph.ctx.enter_context(nc.psum_tensor(f"{name}_scores{i}", [P, 1024], F32)) for i in range(2)]
        ring = ph.ring(banks)
        loaded, small_loaded = [ph.sem(f"loaded{i}") for i in range(5)], ph.sem("small_loaded")
        q_scaled, w_hi, w_lo = ph.sem("q_scaled"), ph.sem("w_hi"), ph.sem("w_lo")
        zeroed, cleared, mask_ready, gate_ready, resid_ready = ph.sem("zeroed"), ph.sem("cleared"), ph.sem("mask_ready"), ph.sem("gate_ready"), ph.sem("resid_ready")
        stack_loaded = [ph.sem(f"stack_loaded{i}") for i in range(2)]
        scores_full, max_done, exp_done = ph.sem("scores_full"), ph.sem("max_done"), ph.sem("exp_done")
        inverse_done, normed, dve_done, bias_ready = ph.sem("inverse_done"), ph.sem("normed"), ph.sem("dve_done"), ph.sem("bias_ready")
        block = ph.block()

        wq, wk, wv = ([t[:, i, :].rearrange("p (k n) -> p k n", k=KT) for t in w] for i in range(3))
        wo = [t[:, 3:5, :].rearrange("p s (g n) -> p (s g) n", g=2) for t in w]

        q_jobs = [(mt,) for mt in range(KT)]
        k_jobs = [(mt, b, c0, n) for mt in range(KT) for b in range(B) for c0, n in ([(0, S)] + ([(S, extra)] if extra else []))]
        v_jobs = [(b, 2 * i) for b in range(B) for i in range(nkt // 2)]
        k0 = len(q_jobs)
        v0 = k0 + len(k_jobs)
        u0 = v0 + len(v_jobs)
        tj = 2 * nkt // 4
        HEADS = units * 4

        def key_source(part, kt, b, c0, n):
            src, per = (sources[0], S) if c0 < S else (sources[1], extra)
            at = b * per + (c0 if c0 < S else c0 - S)
            return src[part][:, kt, at:at + n]

        order = []
        for g in range(HEADS + 1):
            unit, j = divmod(g, 4)
            if g:
                order += [("T", g - 1, c) for c in range(tj)]
            if j == 2 and unit >= 1:
                order.insert(len(order) - tj, ("V", unit - 1, 0))
        order.append(("V", units - 1, 0))
        job_of = {what: u0 + i for i, what in enumerate(order)}
        o0 = u0 + len(order)
        by_act = lambda g, c: (c + (g if tj % 2 else 0)) % 2 == 0
        unit_copies = lambda unit: [job_of["T", 4 * unit + j, c] for j in range(4) for c in range(tj)]

        @block.sync
        def _(sp):
            for i in range(5):
                sp.dma_start(stage[:, i, :], io[cfg["w"]][:, i, :]).then_inc(loaded[i], 16)
                if i == 0:
                    sp.dma_start(bias[:, :], io[cfg["bias"]]).then_inc(small_loaded, 16)
                    sp.dma_start(mask_raw[:, :], io[cfg["mask"]]).then_inc(small_loaded, 16)
                    sp.dma_start(gate[:, :], io[cfg["gate"]].partition_broadcast(P)).then_inc(small_loaded, 16)
                    sp.dma_start(out_bias[:, :], io[cfg["out_bias"]].partition_broadcast(P)).then_inc(small_loaded, 16)
            sp.wait_ge(cleared, 4)
            sp.wait_ge(mask_ready, 1)
            ring.wait_evacuated(sp, v0 - 1)
            if v0 >= 2:
                ring.wait_evacuated(sp, v0 - 2)
            for u in range(units):
                b, quad = divmod(u, quads)
                r = u % 2
                if u >= 2:
                    sp.wait_ge(scores_full, 8 * (u - 1))
                for j in range(4):
                    h = 4 * quad + j
                    a, pt, src, kt = h % 2, j // 2, 16 * (h % 8), h // 8
                    for c, (kp, qp) in enumerate(((0, 0), (0, 1), (1, 0))):
                        row = 64 * a + 16 * c
                        sp.dma_start(raw(k_stack[r][row:row + 16, pt, :]),
                                     raw(kT[kp][src:src + 16, kt, b * nk:(b + 1) * nk])).then_inc(stack_loaded[r], 16)
                        sp.dma_start(raw(q_stack[r][row:row + 16, j, :]),
                                     raw(qT[qp][src:src + 16, kt, b * Q:(b + 1) * Q])).then_inc(stack_loaded[r], 16)
                    row = 64 * a + 48
                    sp.dma_start(raw(k_stack[r][row:row + 1, pt, :]), raw(mask_row[0:1, b, :])).then_inc(stack_loaded[r], 16)
        stack_dmas = 28

        @block.gpsimd
        def _(pool):
            for r in range(2):
                nc.gpsimd.memset(raw(k_stack[r][:, :, :]), 0.0)
                nc.gpsimd.memset(raw(q_stack[r][:, :, :]), 0.0).then_inc(zeroed, 1)
            nc.gpsimd.memset(raw(mask_row[:, :, :]), 0.0)
            nc.gpsimd.memset(v[:, :, :], 0.0).then_inc(zeroed, 1)
            pool.wait_ge(zeroed, 3)
            for r in range(2):
                for a in range(2):
                    nc.gpsimd.memset(raw(q_stack[r][64 * a + 32:64 * a + 64, a:4:2, :]), 1.0).then_inc(cleared, 1)
            for m in range(2 * HEADS):
                pool.wait_ge(inverse_done, m + 1)
                nc.gpsimd.tensor_scalar(probs[:, m % 4, :], probs[:, m % 4, :], inverse[:, m % 4:m % 4 + 1], 1.0,
                                        ALU.mult, ALU.mult).then_inc(normed, 1)

        @block.tensor
        def _(pe):
            for job, (mt,) in enumerate(q_jobs):
                pe.wait_ge(w_lo, 1)
                ring.wait_bank(pe, job)
                for kt in range(KT):
                    last = product3(nc, ring.bank(job)[:, :], [t[:, kt, mt * P:(mt + 1) * P] for t in wq],
                                    [t[:, kt, :] for t in queries], kt == 0, kt == KT - 1)
                last.then_inc(ring.full, 1)
            for i, (mt, b, c0, n) in enumerate(k_jobs):
                job = k0 + i
                pe.wait_ge(w_lo, 2)
                ring.wait_bank(pe, job)
                for kt in range(KT):
                    last = product3(nc, ring.bank(job)[:, 0:n], [t[:, kt, mt * P:(mt + 1) * P] for t in wk],
                                    [key_source(part, kt, b, c0, n) for part in range(2)], kt == 0, kt == KT - 1)
                last.then_inc(ring.full, 1)
            for i, (b, t0) in enumerate(v_jobs):
                job = v0 + i
                pe.wait_ge(w_lo, 3)
                ring.wait_bank(pe, job)
                for t in range(2):
                    for kt in range(KT):
                        last = product3(nc, ring.bank(job)[:, t * D:(t + 1) * D],
                                        [key_source(part, kt, b, (t0 + t) * P, P) for part in range(2)],
                                        [t_[:, kt, :] for t_ in wv], kt == 0, kt == KT - 1)
                last.then_inc(ring.full, 1)

            def transpose_head(g):
                pe.wait_ge(normed, 2 * g + 2)
                for c in range(tj):
                    job = job_of["T", g, c]
                    ring.wait_bank(pe, job)
                    for i in range(4):
                        qt, kt = divmod(4 * c + i, nkt)
                        last = nc.tensor.transpose(ring.bank(job)[:, i * P:(i + 1) * P],
                                                   probs[:, (2 * g + qt) % 4, kt * P:(kt + 1) * P], keep["ident"][:, :])
                    last.then_inc(ring.full, 1)

            def product_v(unit):
                job = job_of["V", unit, 0]
                ring.wait_bank(pe, job)
                b, quad = divmod(unit, quads)
                for back in range(ring.n):
                    ring.wait_evacuated(pe, unit_copies(unit)[-1 - back])
                for kt in range(nkt):
                    for j in range(4):
                        g = 4 * unit + j
                        moving = probsT[:, g % 6, :].rearrange("p (t k n) -> p t k n", t=2, k=nkt)[:, :, kt, :]
                        last = nc.tensor.matmul(ring.bank(job)[32 * j:32 * j + 32, 0:Q],
                                                v[:, b * nkt + kt, 32 * (4 * quad + j):32 * (4 * quad + j) + 32],
                                                moving, start=kt == 0, stop=kt == nkt - 1)
                last.then_inc(ring.full, 1)

            for g in range(HEADS + 1):
                unit, j = divmod(g, 4)
                if g < HEADS:
                    r = unit % 2
                    if j == 0:
                        pe.wait_ge(stack_loaded[r], 16 * stack_dmas * (unit // 2 + 1))
                    for qt in range(2):
                        m = 2 * g + qt
                        if m >= 2:
                            pe.wait_ge(exp_done, m - 1)
                        for c0, n in [(0, S)] + ([(S, extra)] if extra else []):
                            last = nc.tensor.matmul(scores[m % 2][:, c0:c0 + n], q_stack[r][:, j, qt * P:(qt + 1) * P],
                                                    k_stack[r][:, j // 2, c0:c0 + n], start=True, stop=True)
                        last.then_inc(scores_full, 1)
                if j == 2 and unit >= 1:
                    product_v(unit - 1)
                if g:
                    transpose_head(g - 1)
            product_v(units - 1)

            ring.wait_evacuated(pe, job_of["V", units - 1, 0])
            pe.wait_ge(w_lo, 5)
            for t in range(RT):
                job = o0 + t
                ring.wait_bank(pe, job)
                for quad in range(quads):
                    last = product3(nc, ring.bank(job)[:, 0:D], [x[:, quad, t * P:(t + 1) * P] for x in attended],
                                    [x[:, quad, :] for x in wo], quad == 0, quad == quads - 1)
                last.then_inc(ring.full, 1)

        @block.scalar
        def _(act):
            act.wait_ge(q_scaled, 1)
            for i in range(5):
                act.wait_ge(loaded[i], 16)
                nc.scalar.copy(w[0][:, i, :], stage[:, i, :]).then_inc(w_hi, 1)
            act.wait_ge(small_loaded, 64)
            if cfg["gated"]:
                nc.scalar.activation(gate[:, :], gate[:, :], ACT.Tanh).then_inc(gate_ready, 1)
            act.wait_ge(bias_ready, 1)
            for job in range(len(q_jobs)):
                act.wait_ge(ring.full, job + 1)
                nc.scalar.activation(qT[0][:, job, :], ring.bank(job)[:, :], ACT.Identity,
                                     bias=bias[:, job:job + 1]).then_inc(ring.hi_done, 1)
            for i, (mt, b, c0, n) in enumerate(k_jobs):
                job = k0 + i
                act.wait_ge(ring.full, job + 1)
                nc.scalar.activation(kT[0][:, mt, b * nk + c0:b * nk + c0 + n], ring.bank(job)[:, 0:n], ACT.Identity,
                                     bias=bias[:, 2 + mt:3 + mt]).then_inc(ring.hi_done, 1)
            act.wait_ge(cleared, 4)
            for i, (b, t0) in enumerate(v_jobs):
                job = v0 + i
                act.wait_ge(ring.full, job + 1)
                for t in range(2):
                    last = nc.scalar.copy(v[:, b * nkt + t0 + t, :].rearrange("p (h d) -> p h d", h=H)[:, :, 0:DN],
                                          ring.bank(job)[:, t * D:(t + 1) * D].rearrange("p (h d) -> p h d", h=H))
                last.then_inc(ring.freed_by(job), 1)
            def evacuate(g):
                unit, j = divmod(g, 4)
                if j == 2 and unit >= 1:
                    high_v(unit - 1)
                for c in range(tj):
                    if by_act(g - 1, c):
                        job = job_of["T", g - 1, c]
                        act.wait_ge(ring.full, job + 1)
                        nc.scalar.copy(probsT[:, (g - 1) % 6, c * 512:(c + 1) * 512],
                                       ring.bank(job)[:, :]).then_inc(ring.freed_by(job), 1)

            def high_v(unit):
                job = job_of["V", unit, 0]
                b, quad = divmod(unit, quads)
                act.wait_ge(ring.full, job + 1)
                nc.scalar.activation(attended[0][:, quad, b * Q:(b + 1) * Q], ring.bank(job)[:, 0:Q], ACT.Identity,
                                     bias=bias[:, 4 + quad:5 + quad]).then_inc(ring.hi_done, 1)

            for g in range(HEADS + 1):
                if g < HEADS:
                    for qt in range(2):
                        m = 2 * g + qt
                        act.wait_ge(max_done, m + 1)
                        if m >= 4:
                            act.wait_ge(ring.full, job_of["T", m // 2 - 2, tj - 1] + 1)
                        nc.scalar.activation(probs[:, m % 4, :], scores[m % 2][:, 0:nk], ACT.Exp,
                                             bias=neg_max[:, m % 4:m % 4 + 1],
                                             accum_out=row_sum[:, m % 4:m % 4 + 1]).then_inc(exp_done, 1)
                if g:
                    evacuate(g)
            high_v(units - 1)

        @block.vector
        def _(dve):
            link = Chain(dve, dve_done)
            dve.wait_ge(loaded[0], 16)
            nc.vector.tensor_scalar(stage[:, 0, :], stage[:, 0, :], cfg["scale"], None, ALU.mult).then_inc(q_scaled, 1)
            for i in range(5):
                dve.wait_ge(w_hi, i + 1)
                nc.vector.tensor_tensor(w[1][:, i, :], stage[:, i, :], raw(w[0][:, i, :]), ALU.subtract).then_inc(w_lo, 1)
            dve.wait_ge(small_loaded, 64)
            dve.wait_ge(cleared, 4)
            nc.vector.tensor_scalar(bias[:, 0:2], bias[:, 0:2], cfg["scale"], None, ALU.mult).then_inc(bias_ready, 1)
            nc.vector.tensor_scalar(mask_row[0:1, :, 0:S], mask_raw[0:1, :].rearrange("o (b s) -> o b s", b=B), 0.0, MASKED,
                                    ALU.is_equal, ALU.mult).then_inc(mask_ready, 1)
            dve.wait_ge(bias_ready, 1)

            def low(job, nth, out, col, n):
                dve.wait_ge(ring.hi_done, nth + 1)
                nc.vector.scalar_tensor_tensor(out[1], ring.bank(job)[:, 0:n], bias[:, col:col + 1], raw(out[0]),
                                               ALU.add, ALU.subtract).then_inc(ring.freed_by(job), 1)

            for job in range(len(q_jobs)):
                low(job, job, [t[:, job, :] for t in qT], job, 512)
            for i, (mt, b, c0, n) in enumerate(k_jobs):
                low(k0 + i, k0 + i, [t[:, mt, b * nk + c0:b * nk + c0 + n] for t in kT], 2 + mt, n)

            def low_v(unit):
                b, quad = divmod(unit, quads)
                low(job_of["V", unit, 0], v0 + unit, [t[:, quad, b * Q:(b + 1) * Q] for t in attended], 4 + quad, Q)

            for g in range(HEADS + 1):
                if g < HEADS:
                    for m in (2 * g, 2 * g + 1):
                        dve.wait_ge(scores_full, m + 1)
                        nc.vector.tensor_reduce(neg_max[:, m % 4:m % 4 + 1], scores[m % 2][:, 0:nk], AX.X, ALU.max,
                                                negate=True).then_inc(max_done, 1)
                if g % 4 == 2 and g > 4:
                    low_v(g // 4 - 1)
                if g:
                    for c in range(tj):
                        if not by_act(g - 1, c):
                            job = job_of["T", g - 1, c]
                            dve.wait_ge(ring.full, job + 1)
                            nc.vector.tensor_copy(probsT[:, (g - 1) % 6, c * 512:(c + 1) * 512],
                                                  ring.bank(job)[:, :]).then_inc(ring.freed_by(job), 1)
                if g < HEADS:
                    for m in (2 * g, 2 * g + 1):
                        dve.wait_ge(exp_done, m + 1)
                        if m >= 4:
                            dve.wait_ge(normed, m - 3)
                        nc.vector.reciprocal(inverse[:, m % 4:m % 4 + 1],
                                             row_sum[:, m % 4:m % 4 + 1]).then_inc(inverse_done, 1)
            low_v(units - 1)

            if cfg["gated"]:
                dve.wait_ge(gate_ready, 1)
            for t in range(RT):
                last = nc.vector.tensor_tensor(keep["x"][:, t, :] if cfg["in_place"] else keep["sum"][:, t, :],
                                               keep["x"][:, t, :], out_bias[:, :], ALU.add)
            link(last)
            for t in range(RT):
                job = o0 + t
                rows = (keep["x"] if cfg["in_place"] else keep["sum"])[:, t, :]
                dve.wait_ge(ring.full, job + 1)
                nc.vector.scalar_tensor_tensor(rows, ring.bank(job)[:, 0:D], gate[:, 0:1] if cfg["gated"] else 1.0, rows,
                                               ALU.mult, ALU.add).then_inc(ring.freed_by(job), 1)


def normalised_rows(nc, io, keep, name, lnp, out, eps, context=False):
    with Phase(nc, name) as ph:
        parts = NormParts(ph, lnp, CT if context else RT)
        rows = ph.sb("ctx_rows", [P, CT, D]) if context else keep["x"]
        rows_loaded = ph.sem("rows_loaded")
        ring = ph.ring(ph.psum(4))
        block = ph.block()

        @block.sync
        def _(sp):
            parts.load(sp, io)
            if context:
                sp.dma_start(rows[:, :, :], io["ctx_2048"].rearrange("b (t p) d -> p (b t) d", p=P)).then_inc(rows_loaded, 16)

        @block.gpsimd
        def _(pool):
            parts.root(nc, pool)

        @block.tensor
        def _(pe):
            parts.transpose(nc, pe, ring, keep)

        @block.scalar
        def _(act):
            parts.scale(nc, act, ring)

        @block.vector
        def _(dve):
            link = Chain(dve, parts.dve_done)
            if context:
                dve.wait_ge(rows_loaded, 16)
            parts.normalise(nc, dve, link, rows, eps, True)
            parts.split(nc, dve, link, ring, out)


class NormParts:

    def __init__(self, ph, lnp, tiles=RT):
        self.lnp, self.tiles = lnp, tiles
        self.normed = ph.sb("normed", [P, tiles, D])
        self.whole = ph.sb("whole", [P, KT, tiles * P])
        self.stats, self.moments = ph.sb("stats", [P, tiles, 6]), ph.sb("moments", [P, tiles, 2])
        self.shifted, self.power, self.rstd = ph.sb("shifted", [P, tiles]), ph.sb("power", [P, tiles]), ph.sb("rstd", [P, tiles])
        self.scale_shift = ph.sb("scale_shift", [P, 4])
        self.cols_loaded, self.power_set = ph.sem("cols_loaded"), ph.sem("power_set")
        self.shifted_ready, self.rstd_ready, self.normed_ready = ph.sem("shifted_ready"), ph.sem("rstd_ready"), ph.sem("normed_ready")
        self.dve_done = ph.sem("dve_done")
        self.jobs = [(kt, 4 * g) for kt in range(KT) for g in range(tiles // 4)]

    def load(self, sp, io):
        sp.dma_start(self.scale_shift[:, :], io[self.lnp]).then_inc(self.cols_loaded, 16)

    def root(self, nc, pool):
        nc.gpsimd.memset(self.power[:, :], -0.5).then_inc(self.power_set, 1)
        pool.wait_ge(self.power_set, 1)
        pool.wait_ge(self.shifted_ready, 1)
        nc.gpsimd.tensor_tensor(self.rstd[:, :], self.shifted[:, :], self.power[:, :], ALU.pow).then_inc(self.rstd_ready, 1)

    def normalise(self, nc, dve, link, rows, eps, centred):
        row_statistics(nc, link, rows, self.tiles, self.stats, self.moments, self.shifted, eps,
                       centred).then_inc(self.shifted_ready, 1)
        dve.wait_ge(self.rstd_ready, 1)
        for t in range(self.tiles):
            mean = self.moments[:, t, 0:1] if centred else 0.0
            last = nc.vector.tensor_scalar(self.normed[:, t, :], rows[:, t, :], mean, self.rstd[:, t:t + 1],
                                           ALU.subtract, ALU.mult)
        last.then_inc(self.normed_ready, 1)

    def transpose(self, nc, pe, ring, keep):
        pe.wait_ge(self.normed_ready, 1)
        for job, (kt, t0) in enumerate(self.jobs):
            for t in range(4):
                last = nc.tensor.transpose(ring.bank(job)[:, t * P:(t + 1) * P],
                                           self.normed[:, t0 + t, kt * P:(kt + 1) * P], keep["ident"][:, :])
            last.then_inc(ring.full, 1)

    def scale(self, nc, act, ring):
        act.wait_ge(self.cols_loaded, 16)
        for job, (kt, t0) in enumerate(self.jobs):
            act.wait_ge(ring.full, job + 1)
            nc.scalar.activation(self.whole[:, kt, t0 * P:t0 * P + 512], ring.bank(job)[:, :], ACT.Identity,
                                 bias=self.scale_shift[:, 2 + kt:3 + kt],
                                 scale=self.scale_shift[:, kt:kt + 1]).then_inc(ring.hi_done, 1)

    def split(self, nc, dve, link, ring, out):
        for job, (kt, t0) in enumerate(self.jobs):
            hi, lo, whole = (t[:, kt, t0 * P:t0 * P + 512] for t in (*out, self.whole))
            dve.wait_ge(ring.hi_done, job + 1)
            link(nc.vector.tensor_copy(hi, whole))
            nc.vector.tensor_tensor(lo, whole, raw(hi), ALU.subtract).then_inc(ring.freed_by(job), 1)


def mlp(nc, io, keep, cfg):
    with Phase(nc, cfg["name"]) as ph:
        parts = NormParts(ph, cfg["lnp"])
        stage = ph.sb("stage", [P, 8, 512])
        w = ph.hilo("w", [P, 8, 512])
        b1 = ph.sb("b1", [P, FT])
        b2 = ph.sb("b2", [P, D])
        hT = ph.hilo("hT", [P, KT, ROWS])
        activated = ph.sb("activated", [P, 2, ROWS])
        hidden = ph.hilo("hidden", [P, FT, ROWS])
        ring = ph.ring(ph.psum(4))
        loaded = [ph.sem(f"loaded{i}") for i in range(4)]
        small_loaded, w_hi, w_lo = ph.sem("small_loaded"), ph.sem("w_hi"), ph.sem("w_lo")
        stored = keep["stored"]
        block = ph.block()
        w1 = [t[:, 0:4, :].rearrange("p (k s) n -> p k (s n)", k=KT) for t in w]
        w2 = [t[:, 4:8, :].rearrange("p s (g n) -> p (s g) n", g=2) for t in w]
        rows = keep[cfg["rows"]]
        up0 = KT
        down0 = up0 + FT

        @block.sync
        def _(sp):
            parts.load(sp, io)
            for i in range(4):
                sp.dma_start(stage[:, 2 * i:2 * i + 2, :], io[cfg["w"]][:, 2 * i:2 * i + 2, :]).then_inc(loaded[i], 16)
            sp.dma_start(b1[:, :], io[cfg["b1"]]).then_inc(small_loaded, 16)
            sp.dma_start(b2[:, :], io[cfg["b2"]].partition_broadcast(P)).then_inc(small_loaded, 16)
            if cfg["out"] is not None:
                for t in range(RT):
                    ring.wait_evacuated(sp, down0 + t)
                    sp.dma_start(io["out"].rearrange("b (t p) d -> p (b t) d", p=P)[:, t, :], keep["x"][:, t, :]).then_inc(stored, 16)
                sp.wait_ge(stored, 16 * RT)

        @block.gpsimd
        def _(pool):
            parts.root(nc, pool)

        @block.tensor
        def _(pe):
            parts.transpose(nc, pe, ring, keep)
            for m in range(FT):
                job = up0 + m
                if m == 0:
                    ring.wait_evacuated(pe, 0)
                    ring.wait_evacuated(pe, 1)
                pe.wait_ge(w_lo, 4)
                ring.wait_bank(pe, job)
                for kt in range(KT):
                    last = product3(nc, ring.bank(job)[:, :], [t[:, kt, m * P:(m + 1) * P] for t in w1],
                                    [t[:, kt, :] for t in hT], kt == 0, kt == KT - 1)
                last.then_inc(ring.full, 1)
            pe.wait_ge(w_lo, 8)
            for t in range(RT):
                job = down0 + t
                ring.wait_bank(pe, job)
                for f in range(FT):
                    if t == 0:
                        ring.wait_evacuated(pe, up0 + f)
                    last = product3(nc, ring.bank(job)[:, 0:D], [x[:, f, t * P:(t + 1) * P] for x in hidden],
                                    [x[:, f, :] for x in w2], f == 0, f == FT - 1)
                last.then_inc(ring.full, 1)

        @block.scalar
        def _(act):
            for i in range(8):
                act.wait_ge(loaded[i // 2], 16)
                nc.scalar.copy(w[0][:, i, :], stage[:, i, :]).then_inc(w_hi, 1)
            parts.scale(nc, act, ring)
            act.wait_ge(small_loaded, 32)
            for m in range(FT):
                job = up0 + m
                act.wait_ge(ring.full, job + 1)
                if m >= 2:
                    ring.wait_evacuated(act, job - 2)
                nc.scalar.activation(activated[:, m % 2, :], ring.bank(job)[:, :], cfg["gelu"],
                                     bias=b1[:, m:m + 1]).then_inc(ring.hi_done, 1)

        @block.vector
        def _(dve):
            link = Chain(dve, parts.dve_done)
            parts.normalise(nc, dve, link, rows, cfg["eps"], cfg["centred"])
            for i in range(8):
                dve.wait_ge(w_hi, i + 1)
                nc.vector.tensor_tensor(w[1][:, i, :], stage[:, i, :], raw(w[0][:, i, :]), ALU.subtract).then_inc(w_lo, 1)
                if i == 3:
                    parts.split(nc, dve, link, ring, hT)
            dve.wait_ge(small_loaded, 32)
            for t in range(RT):
                last = nc.vector.tensor_tensor(keep["x"][:, t, :], keep["x"][:, t, :], b2[:, :], ALU.add)
            link(last)
            for m in range(FT):
                job = up0 + m
                dve.wait_ge(ring.hi_done, up0 + m + 1)
                link(nc.vector.tensor_copy(hidden[0][:, m, :], activated[:, m % 2, :]))
                nc.vector.tensor_tensor(hidden[1][:, m, :], activated[:, m % 2, :], raw(hidden[0][:, m, :]),
                                        ALU.subtract).then_inc(ring.freed_by(job), 1)
            for t in range(RT):
                job = down0 + t
                dve.wait_ge(ring.full, job + 1)
                nc.vector.tensor_tensor(keep["x"][:, t, :], ring.bank(job)[:, 0:D], keep["x"][:, t, :],
                                        ALU.add).then_inc(ring.freed_by(job), 1)


def wide_prologue(nc, io, keep, cfg):
    name, i = cfg["name"], cfg["index"]
    with Phase(nc, name + "_pre") as ph:
        parts = NormParts(ph, f"L1_ln{i}p")
        wq = ph.sb("wq", [P, KT, H * DW])
        bias_k = ph.sb("bias_k", [P, H * DW])
        product = ph.sb("product", [P, KT, H * DW])
        folded = ph.sb("folded", [P, KT, H])
        cols = ph.sb("cols", [P, 5, H])
        ones = ph.sb("ones", [P, P])
        spread = ph.sb("spread", [P, H, H])
        wo = ph.sb("wo", [P, H, D])
        ring = ph.ring(ph.psum(4))
        loaded, small_loaded, wo_loaded = ph.sem("loaded"), ph.sem("small_loaded"), ph.sem("wo_loaded")
        set_up, folded_ready, spread_ready = ph.sem("set_up"), ph.sem("folded_ready"), ph.sem("spread_ready")
        block = ph.block()

        @block.sync
        def _(sp):
            parts.load(sp, io)
            sp.dma_start(cols[:, 0:4, :], io[f"L1_cols{i}"]).then_inc(small_loaded, 16)
            sp.dma_start(bias_k[:, :], io[f"L1_bias_k{i}"].partition_broadcast(P)).then_inc(loaded, 16)
            sp.dma_start(wq[:, :, :], io[f"L1_wq{i}"].rearrange("(k p) n -> p k n", p=P)).then_inc(loaded, 16)
            sp.dma_start(wo[:, :, :], io[f"L1_wo{i}"].rearrange("(h p) n -> p h n", p=P)).then_inc(wo_loaded, 16)

        @block.gpsimd
        def _(pool):
            nc.gpsimd.memset(ones[:, :], 1.0).then_inc(set_up, 1)
            nc.gpsimd.memset(spread[:, :, :], 0.0).then_inc(set_up, 1)
            parts.root(nc, pool)

        @block.tensor
        def _(pe):
            pe.wait_ge(spread_ready, 1)
            pe.wait_ge(wo_loaded, 16)
            for h in range(H):
                last = nc.tensor.matmul(ring.bank(2)[0:H, 0:D], spread[:, h, :], wo[:, h, :], start=h == 0, stop=h == H - 1)
            parts.transpose(nc, pe, ring, keep)
            last = None
            pe.wait_ge(folded_ready, 1)
            ring.wait_evacuated(pe, 1)
            for t in range(RT):
                out = ring.bank(3)[:, t * H:(t + 1) * H]
                for kt in range(KT):
                    nc.tensor.matmul(out, parts.whole[:, kt, t * P:(t + 1) * P], folded[:, kt, :], start=kt == 0, stop=False)
                last = nc.tensor.matmul(out, ones[:, :], cols[:, 4, :], start=False, stop=True)
            last.then_inc(ring.full, 1)

        @block.scalar
        def _(act):
            parts.scale(nc, act, ring)
            act.wait_ge(ring.full, 3)
            nc.scalar.copy(keep["bias_values"][:, :], ring.bank(2)[0:H, 0:D]).then_inc(ring.freed_by(2), 1)
            nc.scalar.mul(keep["bias_scores"][:, :, :].rearrange("p t h -> p (t h)"), ring.bank(3)[:, 0:RT * H],
                          float(DW) ** -0.5).then_inc(ring.hi_done, 1)

        @block.vector
        def _(dve):
            link = Chain(dve, parts.dve_done)
            dve.wait_ge(small_loaded, 16)
            dve.wait_ge(set_up, 2)
            link(nc.vector.tensor_tensor(cols[:, 4, :], cols[:, 0, :], cols[:, 1, :], ALU.mult))
            nc.vector.tensor_tensor(spread[:, :, :].rearrange("p a b -> p (a b)")[:, 0:H * H:H + 1], cols[:, 3, :], cols[:, 2, :],
                                    ALU.subtract).then_inc(spread_ready, 1)
            parts.normalise(nc, dve, link, keep["x"], 1e-5, True)
            parts.split(nc, dve, link, ring, keep["hT"])
            dve.wait_ge(loaded, 32)
            for kt in range(KT):
                link(nc.vector.tensor_tensor(product[:, kt, :], wq[:, kt, :], bias_k[:, :], ALU.mult))
            for kt in range(KT):
                last = nc.vector.tensor_reduce(folded[:, kt, :], product[:, kt, :].rearrange("p (h d) -> p h d", h=H), AX.X, ALU.add)
            last.then_inc(folded_ready, 1)
            dve.wait_ge(ring.hi_done, 3)
            nc.vector.tensor_scalar(keep["neg_bias_scores"][:, :, :], keep["bias_scores"][:, :, :], -1.0, None, ALU.mult)


def wide_attention(nc, io, keep, cfg):
    name, i = cfg["name"], cfg["index"]
    UN = 2 * B
    SK = S // P
    scale = float(DW) ** -0.5
    PROJ = [("q", 0), ("q", 1), ("k", 0, 0), ("k", 0, 1), ("k", 1, 0), ("k", 1, 1)] + [("v", t) for t in range(0, CT, 2)]
    SHARES = [PROJ[0:3], PROJ[3:6], PROJ[6:8], PROJ[8:10]]
    NPROJ = len(PROJ)
    with Phase(nc, name) as ph:
        stage = [ph.sb(f"stage{j}", [P, 2048]) for j in range(2)]
        w = [ph.hilo(f"w{j}", [P, 1536]) for j in range(2)]
        wo = [ph.hilo(f"wo{j}", [P, 2, D]) for j in range(2)]
        q = [ph.hilo(f"q{j}", [P, 2, ROWS]) for j in range(2)]
        k = [ph.hilo(f"k{j}", [P, 2, B * S]) for j in range(2)]
        v = [ph.hilo(f"v{j}", [P, CT, 2 * DW]) for j in range(2)]
        cols = ph.sb("cols", [P, 4, H])
        bk = ph.sb("bk", [P, H])
        out_bias = ph.sb("out_bias", [P, D])
        probs = ph.sb("probs", [P, 2, 2, S])
        probsT = [ph.hilo(f"probsT{j}", [P, 2 * SK * P]) for j in range(2)]
        attended = [ph.hilo(f"attended{j}", [P, Q]) for j in range(2)]
        top, neg_max, bias_shifted = ph.sb("top", [P, 2]), ph.sb("neg_max", [P, 2, 2]), ph.sb("bias_shifted", [P, 2, 2])
        row_sum, bias_prob, inverse = ph.sb("row_sum", [P, 2, 2]), ph.sb("bias_prob", [P, 2, 2]), ph.sb("inverse", [P, 2])
        bias_probs = ph.sb("bias_probs", [P, RT, H])
        bias_probsT = ph.sb("bias_probsT", [H, ROWS])
        banks = ph.psum(4)
        scores = ph.ctx.enter_context(nc.psum_tensor(f"{name}_scores", [P, 2, S], F32))
        sums = ph.ctx.enter_context(nc.psum_tensor(f"{name}_sums", [P, RT, D], F32))
        ring = ph.ring(banks)
        loaded, small_loaded = [ph.sem(f"loaded{j}") for j in range(2)], ph.sem("small_loaded")
        pool_done, w_ready, wo_ready = ph.sem("pool_done"), ph.sem("w_ready"), ph.sem("wo_ready")
        cols_scaled, out_done, scores_full = ph.sem("cols_scaled"), ph.sem("out_done"), ph.sem("scores_full")
        max_done, exp_done, normed, dve_done = ph.sem("max_done"), ph.sem("exp_done"), ph.sem("normed"), ph.sem("dve_done")
        sums_full = ph.sem("sums_full")
        block = ph.block()
        LAST = PAIRS * UN - 1

        job_of, n = {}, 0
        for item in PROJ:
            job_of[0, item] = n
            n += 1
        for g in range(LAST + 2):
            p, u = divmod(g, UN)
            if g:
                for qt in range(2):
                    job_of["T", g - 1, qt] = n
                    n += 1
            if p + 1 < PAIRS:
                for item in SHARES[u]:
                    job_of[p + 1, item] = n
                    n += 1
            if g:
                job_of["V", g - 1] = n
                n += 1
        job_of["bias"] = n

        def unit(g):
            p, u = divmod(g, UN)
            return p % 2, u // B, u % B, 2 * p + u // B

        @block.sync
        def _(sp):
            for p in range(PAIRS):
                if p >= 2:
                    sp.wait_ge(wo_ready, p - 1)
                sp.dma_start(stage[p % 2][:, :], io[f"L1_w{i}"][p]).then_inc(loaded[p % 2], 16)
                if p == 0:
                    sp.dma_start(cols[:, :, :], io[f"L1_cols{i}"]).then_inc(small_loaded, 16)
                    sp.dma_start(bk[:, :], io[f"L1_bk{i}"]).then_inc(small_loaded, 16)
                    sp.dma_start(out_bias[:, :], io[f"L1_bo{i}"].partition_broadcast(P)).then_inc(small_loaded, 16)

        @block.gpsimd
        def _(pool):
            link = Chain(pool, pool_done)
            for p in range(PAIRS):
                j = p % 2
                pool.wait_ge(loaded[j], 16 * (p // 2 + 1))
                link(nc.gpsimd.tensor_scalar(stage[j][:, 0:512], stage[j][:, 0:512], scale, 1.0, ALU.mult, ALU.mult))
                if p >= 2:
                    pool.wait_ge(ring.full, job_of[p - 2, PROJ[-1]] + 1)
                link(nc.gpsimd.tensor_scalar(w[j][0][:, :], stage[j][:, 0:1536], 1.0, 1.0, ALU.mult, ALU.mult))
                nc.gpsimd.tensor_tensor(w[j][1][:, :], stage[j][:, 0:1536], raw(w[j][0][:, :]), ALU.subtract).then_inc(w_ready, 1)
                if p >= 2:
                    pool.wait_ge(out_done, UN * (p - 1))
                part = stage[j][:, 1536:2048]
                link(nc.gpsimd.tensor_scalar(wo[j][0][:, :, :].rearrange("p h n -> p (h n)"), part, 1.0, 1.0, ALU.mult, ALU.mult))
                nc.gpsimd.tensor_tensor(wo[j][1][:, :, :].rearrange("p h n -> p (h n)"), part,
                                        raw(wo[j][0][:, :, :]).rearrange("p h n -> p (h n)"), ALU.subtract).then_inc(wo_ready, 1)

        @block.tensor
        def _(pe):
            def project(p, item):
                j, job = p % 2, job_of[p, item]
                wq, wk, wv = ([t[:, c * 512:(c + 1) * 512].rearrange("p (k n) -> p k n", k=KT) for t in w[j]] for c in range(3))
                ring.wait_bank(pe, job)
                for t in range(2 if item[0] == "v" else 1):
                    for kt in range(KT):
                        if item[0] == "q":
                            out = ring.bank(job)[:, :]
                            lhs, rhs = both(wq, np.s_[:, kt, item[1] * DW:(item[1] + 1) * DW]), both(keep["hT"], np.s_[:, kt, :])
                        elif item[0] == "k":
                            out = ring.bank(job)[:, :]
                            lhs = both(wk, np.s_[:, kt, item[1] * DW:(item[1] + 1) * DW])
                            rhs = both(keep["ctxT"], np.s_[:, kt, item[2] * S:(item[2] + 1) * S])
                        else:
                            out = ring.bank(job)[:, t * 2 * DW:(t + 1) * 2 * DW]
                            lhs = both(keep["ctxT"], np.s_[:, kt, (item[1] + t) * P:(item[1] + t + 1) * P])
                            rhs = both(wv, np.s_[:, kt, :])
                        last = product3(nc, out, lhs, rhs, kt == 0, kt == KT - 1)
                last.then_inc(ring.full, 1)

            def score(g):
                j, hh, b, h = unit(g)
                if g:
                    pe.wait_ge(exp_done, 3 * g - 1)
                for qt in range(2):
                    at = b * Q + qt * P
                    last = product3(nc, scores[:, qt, :], both(q[j], np.s_[:, hh, at:at + P]),
                                    both(k[j], np.s_[:, hh, b * S:(b + 1) * S]), True, True)
                last.then_inc(scores_full, 1)

            def transposes(g):
                for qt in range(2):
                    job = job_of["T", g, qt]
                    pe.wait_ge(normed, 2 * g + qt + 1)
                    ring.wait_bank(pe, job)
                    for kt in range(SK):
                        last = nc.tensor.transpose(ring.bank(job)[:, kt * P:(kt + 1) * P],
                                                   probs[:, g % 2, qt, kt * P:(kt + 1) * P], keep["ident"][:, :])
                    last.then_inc(ring.full, 1)

            def product_v(g):
                j, hh, b, h = unit(g)
                job = job_of["V", g]
                ring.wait_evacuated(pe, job_of["T", g, 0])
                ring.wait_evacuated(pe, job_of["T", g, 1])
                ring.wait_bank(pe, job)
                for kt in range(SK):
                    weights = [t[:, :].rearrange("p (q k n) -> p q k n", q=2, k=SK)[:, :, kt, :] for t in probsT[g % 2]]
                    last = product3(nc, ring.bank(job)[:, 0:Q], both(v[j], np.s_[:, b * SK + kt, hh * DW:(hh + 1) * DW]),
                                    weights, kt == 0, kt == SK - 1)
                last.then_inc(ring.full, 1)

            def output(g):
                j, hh, b, h = unit(g)
                pe.wait_ge(wo_ready, g // UN + 1)
                ring.wait_evacuated(pe, job_of["V", g])
                for qt in range(2):
                    last = product3(nc, sums[:, b * 2 + qt, :], both(attended[g % 2], np.s_[:, qt * P:(qt + 1) * P]),
                                    both(wo[j], np.s_[:, hh, :]), h == 0 and qt == 0, False, loose=True)
                last.then_inc(out_done, 1)

            pe.wait_ge(w_ready, 1)
            for item in PROJ:
                project(0, item)
            for g in range(LAST + 2):
                p, u = divmod(g, UN)
                if g <= LAST:
                    if u == 0:
                        for back in range(ring.n):
                            ring.wait_evacuated(pe, job_of[p, PROJ[-1 - back]])
                        ring.wait_evacuated(pe, job_of[p, ("k", 1, 1)])
                        ring.wait_evacuated(pe, job_of[p, ("q", 1)])
                    score(g)
                if g:
                    transposes(g - 1)
                if p + 1 < PAIRS:
                    if u == 0:
                        pe.wait_ge(w_ready, p + 2)
                    for item in SHARES[u]:
                        project(p + 1, item)
                if g >= 2:
                    output(g - 2)
                if g:
                    product_v(g - 1)
            output(LAST)

            job = job_of["bias"]
            ring.wait_bank(pe, job)
            for t in range(RT):
                last = nc.tensor.transpose(ring.bank(job)[0:H, t * P:(t + 1) * P], bias_probs[:, t, :], keep["ident"][:, :])
            last.then_inc(ring.full, 1)
            ring.wait_evacuated(pe, job)
            for t in range(RT):
                last = nc.tensor.matmul(sums[:, t, :], bias_probsT[:, t * P:(t + 1) * P], keep["bias_values"][:, :],
                                        start=False, stop=True, skip_group_check=True)
            last.then_inc(sums_full, 1)

        def destination(p, item):
            j = p % 2
            if item[0] == "q":
                return both(q[j], np.s_[:, item[1], :])
            if item[0] == "k":
                return both(k[j], np.s_[:, item[1], item[2] * S:(item[2] + 1) * S])
            return [t[:, item[1]:item[1] + 2, :].rearrange("p t n -> p (t n)") for t in v[j]]

        def bias_of(p, item):
            if item[0] == "v":
                return None
            return (cols[:, 0, :] if item[0] == "q" else bk[:, :])[:, 2 * p + item[1]:2 * p + item[1] + 1]

        @block.scalar
        def _(act):
            def high(job, out, column, n=512):
                act.wait_ge(ring.full, job + 1)
                source = ring.bank(job)[:, 0:n]
                if column is None:
                    nc.scalar.copy(out, source).then_inc(ring.hi_done, 1)
                else:
                    nc.scalar.activation(out, source, ACT.Identity, bias=column).then_inc(ring.hi_done, 1)

            act.wait_ge(small_loaded, 48)
            act.wait_ge(cols_scaled, 1)
            for item in PROJ:
                high(job_of[0, item], destination(0, item)[0], bias_of(0, item))
            for g in range(LAST + 2):
                p, u = divmod(g, UN)
                if g:
                    for qt in range(2):
                        high(job_of["T", g - 1, qt], probsT[(g - 1) % 2][0][:, qt * 512:(qt + 1) * 512], None)
                if g <= LAST:
                    act.wait_ge(max_done, g + 1)
                    for qt in range(2):
                        nc.scalar.activation(probs[:, g % 2, qt, :], scores[:, qt, :], ACT.Exp, bias=neg_max[:, g % 2, qt:qt + 1],
                                             accum_out=row_sum[:, g % 2, qt:qt + 1]).then_inc(exp_done, 1)
                    nc.scalar.activation(bias_prob[:, g % 2, :], bias_shifted[:, g % 2, :], ACT.Exp).then_inc(exp_done, 1)
                if p + 1 < PAIRS:
                    for item in SHARES[u]:
                        high(job_of[p + 1, item], destination(p + 1, item)[0], bias_of(p + 1, item))
                if g:
                    j, hh, b, h = unit(g - 1)
                    high(job_of["V", g - 1], attended[(g - 1) % 2][0][:, :], cols[:, 2, h:h + 1], Q)
            job = job_of["bias"]
            act.wait_ge(ring.full, job + 1)
            nc.scalar.copy(bias_probsT[:, :], ring.bank(job)[0:H, :]).then_inc(ring.freed_by(job), 1)

        @block.vector
        def _(dve):
            link = Chain(dve, dve_done)
            highs = [0]

            def low(job, out, column, n=512):
                highs[0] += 1
                dve.wait_ge(ring.hi_done, highs[0])
                source = ring.bank(job)[:, 0:n]
                if column is None:
                    nc.vector.tensor_tensor(out[1], source, raw(out[0]), ALU.subtract).then_inc(ring.freed_by(job), 1)
                else:
                    nc.vector.scalar_tensor_tensor(out[1], source, column, raw(out[0]), ALU.add,
                                                   ALU.subtract).then_inc(ring.freed_by(job), 1)

            dve.wait_ge(small_loaded, 48)
            nc.vector.tensor_scalar(cols[:, 0, :], cols[:, 0, :], scale, None, ALU.mult).then_inc(cols_scaled, 1)
            for t in range(RT):
                last = nc.vector.tensor_tensor(keep["x"][:, t, :], keep["x"][:, t, :], out_bias[:, :], ALU.add)
            link(last)
            dve.wait_ge(cols_scaled, 1)
            for item in PROJ:
                low(job_of[0, item], destination(0, item), bias_of(0, item))
            for g in range(LAST + 2):
                p, u = divmod(g, UN)
                s = g % 2
                if g <= LAST:
                    j, hh, b, h = unit(g)
                    dve.wait_ge(scores_full, g + 1)
                    link(nc.vector.tensor_reduce(top[:, :], scores[:, :, :], AX.X, ALU.max))
                    link(nc.vector.scalar_tensor_tensor(neg_max[:, s, :], top[:, :], -1.0, keep["neg_bias_scores"][:, 2 * b:2 * b + 2, h],
                                                        ALU.mult, ALU.min))
                    nc.vector.tensor_tensor(bias_shifted[:, s, :], keep["bias_scores"][:, 2 * b:2 * b + 2, h], neg_max[:, s, :],
                                            ALU.add).then_inc(max_done, 1)
                if g:
                    for qt in range(2):
                        low(job_of["T", g - 1, qt], [t[:, qt * 512:(qt + 1) * 512] for t in probsT[(g - 1) % 2]], None)
                if g <= LAST:
                    dve.wait_ge(exp_done, 3 * (g + 1))
                    link(nc.vector.tensor_tensor(inverse[:, :], row_sum[:, s, :], bias_prob[:, s, :], ALU.add))
                    link(nc.vector.reciprocal(inverse[:, :], inverse[:, :]))
                    nc.vector.tensor_tensor(bias_probs[:, 2 * b:2 * b + 2, h], bias_prob[:, s, :], inverse[:, :], ALU.mult)
                    for qt in range(2):
                        nc.vector.tensor_scalar(probs[:, s, qt, :], probs[:, s, qt, :], inverse[:, qt:qt + 1], None,
                                                ALU.mult).then_inc(normed, 1)
                if p + 1 < PAIRS:
                    for item in SHARES[u]:
                        low(job_of[p + 1, item], destination(p + 1, item), bias_of(p + 1, item))
                if g:
                    j, hh, b, h = unit(g - 1)
                    low(job_of["V", g - 1], both(attended[(g - 1) % 2], np.s_[:, :]), cols[:, 2, h:h + 1], Q)
            dve.wait_ge(sums_full, 1)
            for t in range(RT):
                nc.vector.tensor_tensor(keep["x"][:, t, :], sums[:, t, :], keep["x"][:, t, :], ALU.add)


def program(nc, io):
    with ExitStack() as ctx:
        def sb(name, shape, dt=F32):
            return ctx.enter_context(nc.sbuf_tensor(name, shape, dt))

        keep = {"x": sb("x_rows", [P, RT, D]), "sum": sb("sum_rows", [P, RT, D]), "ident": sb("ident", [P, P]),
                "bias_scores": sb("bias_scores", [P, RT, H]), "neg_bias_scores": sb("neg_bias_scores", [P, RT, H]),
                "bias_values": sb("bias_values", [H, D])}
        for name, n in (("ctxT", B * S), ("latT", ROWS)):
            keep[name] = sb(name + "_hi", [P, KT, n], F32R), sb(name + "_lo", [P, KT, n], F32R)
        keep["stored"] = ctx.enter_context(nc.semaphore("stored"))
        keep["hT"] = keep["latT"]

        transpose_context(nc, io, keep)
        narrow_attention(nc, io, keep, dict(
            name="L0a", nk=S + Q, queries=keep["latT"], keys=[keep["ctxT"], keep["latT"]], mask="mask_ik0", mask_dtype=I32,
            w="L0_w", bias="L0_bias", out_bias="L0_bo", gate="L2_gate", gated=False, scale=1.0 / DN, in_place=False))
        mlp(nc, io, keep, dict(name="L0m", rows="sum", lnp="L0_lnp", eps=1e-6, centred=False, w="L0_wm", b1="L0_b1", b2="L0_b2",
                               gelu=ACT.Gelu_apprx_tanh, out=None))
        for i in (1, 2):
            cfg = dict(name=f"L1a{i}", index=i)
            wide_prologue(nc, io, keep, cfg)
            wide_attention(nc, io, keep, cfg)
        mlp(nc, io, keep, dict(name="L1m", rows="x", lnp="L1_lnmp", eps=1e-5, centred=True, w="L1_wm", b1="L1_b1", b2="L1_b2",
                               gelu=ACT.Gelu, out=None))
        plain_rows(nc, keep)
        with Phase(nc, "L2") as ph:
            audT = ph.hilo("audT", [P, KT, B * S])
            normalised_rows(nc, io, keep, "L2c", "L2_lnp", audT, 1e-5, context=True)
            narrow_attention(nc, io, keep, dict(
                name="L2a", nk=S, queries=keep["hT"], keys=[audT], mask="mask_bf1", mask_dtype=U8,
                w="L2_w", bias="L2_bias", out_bias="L2_bo", gate="L2_gate", gated=True, scale=DN ** -0.5, in_place=True))
        normalised_rows(nc, io, keep, "L3q", "L3_ln1p", keep["hT"], 1e-5)
        narrow_attention(nc, io, keep, dict(
            name="L3a", nk=S, queries=keep["hT"], keys=[keep["ctxT"]], mask="mask_bf1", mask_dtype=U8,
            w="L3_w", bias="L3_bias", out_bias="L3_bo", gate="L2_gate", gated=False, scale=DN ** -0.5, in_place=True))
        mlp(nc, io, keep, dict(name="L3m", rows="x", lnp="L3_ln2p", eps=1e-5, centred=True, w="L3_wm", b1="L3_b1", b2="L3_b2",
                               gelu=ACT.Gelu_apprx_tanh, out="out"))


def plain_rows(nc, keep):
    with Phase(nc, "L2q") as ph:
        ring = ph.ring(ph.psum(4))
        block = ph.block()

        @block.tensor
        def _(pe):
            for kt in range(KT):
                for t in range(RT):
                    last = nc.tensor.transpose(ring.bank(kt)[:, t * P:(t + 1) * P], keep["x"][:, t, kt * P:(kt + 1) * P],
                                               keep["ident"][:, :])
                last.then_inc(ring.full, 1)

        @block.scalar
        def _(act):
            for kt in range(KT):
                act.wait_ge(ring.full, kt + 1)
                nc.scalar.copy(keep["hT"][0][:, kt, :], ring.bank(kt)[:, :]).then_inc(ring.hi_done, 1)

        @block.vector
        def _(dve):
            for kt in range(KT):
                dve.wait_ge(ring.hi_done, kt + 1)
                nc.vector.tensor_tensor(keep["hT"][1][:, kt, :], ring.bank(kt)[:, :], raw(keep["hT"][0][:, kt, :]), ALU.subtract)


def kernel(**inputs):
    import concourse.bacc as bacc
    from concourse.bass_utils import run_bass_kernel_spmd as run

    a = {name: np.asarray(value) for name, value in inputs.items()}

    def tiles(w):
        return w.reshape(-1, P, w.shape[1]).transpose(1, 0, 2)

    def columns(vector):
        return vector.reshape(-1, P).T

    def padded_heads(w):
        out = np.zeros((H, 32, w.shape[1]), w.dtype)
        out[:, 0:DN] = w.reshape(H, DN, -1)
        return out.reshape(H * 32, -1)

    def narrow(q, k, v, o):
        return np.concatenate([tiles(w).reshape(P, -1, 512) for w in (q, k, v, padded_heads(o))], axis=1)

    def narrow_bias(q, k, v):
        return np.concatenate([columns(q), columns(k), columns(padded_heads(v[:, None])[:, 0])], axis=1)

    def mlp_weights(w1, w2):
        return np.concatenate([tiles(w).reshape(P, -1, 512) for w in (w1, w2)], axis=1)

    zeros = np.zeros(D, np.float32)
    t = {"x": a["x"], "ctx_2048": a["ctx_2048"], "mask_ik0": a["mask_BxS2_ik0"].reshape(1, -1),
         "mask_bf1": a["mask_BxS2_bf1"].view(np.uint8).reshape(1, -1)}
    kv, kvb = (a[f"L0_xattn_kv_{n}"].reshape(-1, H, DN, 2) for n in "wb")
    key_value = [(kv[..., i].reshape(D, D), kvb[..., i].reshape(D)) for i in range(2)]
    t["L0_w"] = narrow(a["L0_xattn_q_w"], key_value[0][0], key_value[1][0], a["L0_xattn_out_w"])
    t["L0_bias"] = narrow_bias(a["L0_xattn_q_b"], key_value[0][1], key_value[1][1])
    t["L0_bo"] = a["L0_xattn_out_b"]
    t["L0_lnp"] = np.concatenate([columns(a["L0_xattn_postnorm_w"]), columns(zeros)], axis=1)
    t["L2_w"] = narrow(*(a[f"L2_xattn_W{n}"].T for n in "qkvo"))
    t["L2_bias"], t["L2_bo"], t["L2_gate"] = narrow_bias(zeros, zeros, zeros), zeros, a["L2_xattn_gate"]
    t["L2_lnp"] = np.concatenate([columns(a["L2_xattn_ln_gamma"]), columns(a["L2_xattn_ln_beta"])], axis=1)
    t["L3_w"] = narrow(*(a[f"L3_xattn_{n}_w"] for n in ("q", "k", "v", "cproj")))
    t["L3_bias"] = narrow_bias(*(a[f"L3_xattn_{n}_b"] for n in "qkv"))
    t["L3_bo"] = a["L3_xattn_cproj_b"]
    for n in (1, 2):
        t[f"L3_ln{n}p"] = np.concatenate([columns(a[f"L3_xattn_ln{n}_w"]), columns(a[f"L3_xattn_ln{n}_b"])], axis=1)
    for out, names in (("L0", ("mlp_w1", "mlp_b1", "mlp_w2", "mlp_b2")), ("L1", ("w_fc1", "b_fc1", "w_fc2", "b_fc2")),
                       ("L3", ("fc_w", "fc_b", "proj_w", "proj_b"))):
        w1, b1, w2, b2 = (a[f"{out}_xattn_{n}"] for n in names)
        t[f"{out}_wm"], t[f"{out}_b1"], t[f"{out}_b2"] = mlp_weights(w1, w2), columns(b1), b2
    for n in ("1", "2", "_mlp"):
        t[f"L1_ln{n.replace('_mlp', 'm')}p"] = np.concatenate(
            [columns(a[f"L1_xattn_ln{n}_scale"]), columns(a[f"L1_xattn_ln{n}_offset"])], axis=1)
    for n in (1, 2):
        wq, wk, wv, wo = (a[f"L1_xattn_w{m}{n}"] for m in "qkvo")
        by_pair = [tiles(w).reshape(P, KT, PAIRS, 2 * DW).transpose(2, 0, 1, 3).reshape(PAIRS, P, -1) for w in (wq, wk, wv)]
        by_pair.append(wo.reshape(PAIRS, 2, P, D).transpose(0, 2, 1, 3).reshape(PAIRS, P, -1))
        t[f"L1_w{n}"] = np.concatenate(by_pair, axis=2)
        t[f"L1_wq{n}"], t[f"L1_wo{n}"], t[f"L1_bias_k{n}"] = wq, wo, a[f"L1_xattn_bias_k{n}"].reshape(-1)
        t[f"L1_cols{n}"] = np.stack([columns(a[f"L1_xattn_{m}{n}"].reshape(-1)) for m in ("bq", "bias_k", "bv", "bias_v")], axis=1)
        t[f"L1_bk{n}"], t[f"L1_bo{n}"] = columns(a[f"L1_xattn_bk{n}"]), a[f"L1_xattn_bo{n}"]

    nc = bacc.Bacc("TRN2", target_bir_lowering=False, num_devices=1)
    arrays, io = {}, {}
    for name, value in t.items():
        arrays[f"in_{name}"] = np.ascontiguousarray(value)
        io[name] = nc.dram_tensor(f"in_{name}", value.shape, mybir.dt.from_np(value.dtype), kind="ExternalInput").ap()
    io["out"] = nc.dram_tensor("out_x", (B, Q, D), F32, kind="ExternalOutput").ap()
    program(nc, io)
    result = run(nc, [arrays], core_ids=[0])
    return result.results[0]["out_x"]
```

```python
from contextlib import ExitStack

import numpy as np

import concourse.bass as bass
from concourse import mybir

F32 = mybir.dt.float32
F32R = mybir.dt.float32r
I32 = mybir.dt.int32
U8 = mybir.dt.uint8
ALU = mybir.AluOpType
ACT = mybir.ActivationFunctionType
AX = mybir.AxisListType

P = 128
B = 2
Q = 256
S = 512
D = 256
KT = D // P
ROWS = B * Q
RT = ROWS // P
CT = B * S // P
H = 16
DN = D // H
DW = 128
F = 1024
FT = F // P
PAIRS = H // 2
MASKED = -float(2 ** 100)
BANKS = 8


def raw(ap):
    return ap.bitcast(F32)


class Ring:

    def __init__(self, banks, sem, name, regular):
        self.banks = banks
        self.n = len(banks)
        self.full = sem(f"{name}_full")
        self.hi_done = sem(f"{name}_hi_done")
        self.free = [sem(f"{name}_free{i}") for i in range(self.n)]
        self.regular = regular

    def bank(self, job):
        return self.banks[job % self.n]

    def wait_bank(self, pe, job, late=0):
        if self.regular or job >= self.n:
            pe.wait_ge(self.free[job % self.n], job // self.n + late)

    def wait_evacuated(self, engine, job, late=0):
        engine.wait_ge(self.free[job % self.n], job // self.n + 1 + late)

    def freed_by(self, job):
        return self.free[job % self.n]


def product3(nc, out, lhs, rhs, start, stop, loose=False):
    (lh, ll), (rh, rl) = lhs, rhs
    nc.tensor.matmul(out, lh, rh, start=start, stop=False, skip_group_check=loose)
    nc.tensor.matmul(out, lh, rl, start=False, stop=False, skip_group_check=loose)
    return nc.tensor.matmul(out, ll, rh, start=False, stop=stop, skip_group_check=loose)


def both(pair, index):
    return tuple(t[index] for t in pair)


class Chain:

    def __init__(self, engine, done):
        self.engine, self.done, self.count = engine, done, 0

    def __call__(self, instruction):
        self.count += 1
        instruction.then_inc(self.done, 1)
        self.engine.wait_ge(self.done, self.count)


def row_statistics(nc, link, rows, tiles, stats, moments, shifted, eps, centred):
    for t in range(tiles):
        last = nc.vector.bn_stats(stats[:, t, :], rows[:, t, :])
        if t == tiles - 1:
            link(last)
    for t in range(tiles):
        last = nc.vector.bn_aggr(moments[:, t, :], stats[:, t, :])
        if t == tiles - 1:
            link(last)
    if not centred:
        link(nc.vector.tensor_tensor(shifted[:, 0:tiles], moments[:, 0:tiles, 0], moments[:, 0:tiles, 0], ALU.mult))
        link(nc.vector.tensor_tensor(shifted[:, 0:tiles], shifted[:, 0:tiles], moments[:, 0:tiles, 1], ALU.add))
        return nc.vector.tensor_scalar(shifted[:, 0:tiles], shifted[:, 0:tiles], eps, None, ALU.add)
    return nc.vector.tensor_scalar(shifted[:, 0:tiles], moments[:, 0:tiles, 1], eps, None, ALU.add)


class Phase:

    def __init__(self, nc, name):
        self.nc, self.name, self.ctx, self.sems = nc, name, ExitStack(), []

    def __enter__(self):
        self.ctx.__enter__()
        return self

    def __exit__(self, *error):
        self.ctx.__exit__(*error)
        if self.sems and not error[0]:
            self.nc.clear_and_free_semaphores(self.sems)
            self.nc.all_engine_barrier()

    def sb(self, name, shape, dt=F32):
        return self.ctx.enter_context(self.nc.sbuf_tensor(f"{self.name}_{name}", shape, dt))

    def hilo(self, name, shape):
        return self.sb(name + "_hi", shape, F32R), self.sb(name + "_lo", shape, F32R)

    def psum(self, n):
        return [self.ctx.enter_context(self.nc.psum_tensor(f"{self.name}_bank{i}", [P, 512], F32)) for i in range(n)]

    def sem(self, name):
        self.sems.append(self.nc.alloc_semaphore(f"{self.name}_{name}"))
        return self.sems[-1]

    def ring(self, banks, regular=False):
        return Ring(banks, self.sem, "ring", regular)

    def block(self):
        return self.ctx.enter_context(self.nc.Block())


def transpose_context(nc, io, keep):
    with Phase(nc, "prep") as ph:
        ctx_rows = ph.sb("ctx_rows", [P, CT, D])
        ring = ph.ring(ph.psum(4))
        loaded, cleared, ident_ready = ph.sem("loaded"), ph.sem("cleared"), ph.sem("ident_ready")
        block = ph.block()
        jobs = [(keep["ctxT"], ctx_rows, kt, 4 * g) for kt in range(KT) for g in range(CT // 4)]
        jobs += [(keep["latT"], keep["x"], kt, 0) for kt in range(KT)]

        @block.sync
        def _(sp):
            sp.dma_start(ctx_rows[:, :, :], io["ctx_2048"].rearrange("b (t p) d -> p (b t) d", p=P)).then_inc(loaded, 16)
            sp.dma_start(keep["x"][:, :, :], io["x"].rearrange("b (t p) d -> p (b t) d", p=P)).then_inc(loaded, 16)

        @block.gpsimd
        def _(pool):
            nc.gpsimd.memset(keep["ident"][:, :], 0.0).then_inc(cleared, 1)
            pool.wait_ge(cleared, 1)
            nc.gpsimd.affine_select(out=keep["ident"][:, :], in_=keep["ident"][:, :], compare_op=ALU.not_equal, fill=1.0,
                                    base=0, pattern=[[-1, P]], channel_multiplier=1).then_inc(ident_ready, 1)

        @block.tensor
        def _(pe):
            pe.wait_ge(loaded, 32)
            pe.wait_ge(ident_ready, 1)
            for job, (_, rows, kt, t0) in enumerate(jobs):
                ring.wait_bank(pe, job)
                for t in range(4):
                    last = nc.tensor.transpose(ring.bank(job)[:, t * P:(t + 1) * P],
                                               rows[:, t0 + t, kt * P:(kt + 1) * P], keep["ident"][:, :])
                last.then_inc(ring.full, 1)

        @block.scalar
        def _(act):
            for job, (to, _, kt, t0) in enumerate(jobs):
                act.wait_ge(ring.full, job + 1)
                nc.scalar.copy(to[0][:, kt, t0 * P:t0 * P + 512], ring.bank(job)[:, :]).then_inc(ring.hi_done, 1)

        @block.vector
        def _(dve):
            for job, (to, _, kt, t0) in enumerate(jobs):
                dve.wait_ge(ring.hi_done, job + 1)
                nc.vector.tensor_tensor(to[1][:, kt, t0 * P:t0 * P + 512], ring.bank(job)[:, :],
                                        raw(to[0][:, kt, t0 * P:t0 * P + 512]), ALU.subtract).then_inc(ring.freed_by(job), 1)


def narrow_attention(nc, io, keep, cfg):
    name, nk, queries, sources = cfg["name"], cfg["nk"], cfg["queries"], cfg["keys"]
    nkt = nk // P
    extra = nk - S
    quads = H // 4
    units = B * quads
    OCTETS = B * KT
    with Phase(nc, name) as ph:
        w_qkv = ph.sb("w_qkv", [P, 2, 3, 512], F32R)
        w_out = ph.sb("w_out", [P, 2, 2, 512], F32R)
        bias = ph.sb("bias", [P, 8])
        out_bias = ph.sb("out_bias", [P, D])
        gate = ph.sb("gate", [P, 1])
        mask_row = ph.sb("mask_row", [1, B, nk], F32R)
        q_parts = ph.sb("q_parts", [P, 2, KT, ROWS], F32R)
        qT = [q_parts[:, part, :, :] for part in range(2)]
        kT = ph.hilo("kT", [P, KT, B * nk])
        v = ph.sb("v", [P, B * nkt, H * 32])
        k_stack = [ph.sb("k_stack", [P, 4, nk], F32R),
                   w_qkv[:, :, :, :].rearrange("p s i n -> p (s i n)")[:, 0:4 * nk].rearrange("p (t n) -> p t n", t=4)]
        q_stack = [ph.sb(f"q_stack{i}", [P, 8, Q], F32R) for i in range(2)]
        score_slots, probs_slots, small_slots = (4, 8, 8) if nk == S else (2, 6, 8)
        probs = ph.sb("probs", [P, probs_slots, nk])
        TSLOTS = 5
        probsT = ph.sb("probsT", [P, TSLOTS, 2 * nkt * P])
        flat = probsT[:, :, :].rearrange("p s n -> p (s n)")
        stage = flat[:, 0:5 * 512].rearrange("p (i n) -> p i n", i=5)
        mask_raw = flat[0:1, 5 * 512:5 * 512 + B * S].bitcast(cfg["mask_dtype"])[:, 0:B * S]
        neg_max, row_sum, inverse = (ph.sb(n, [P, small_slots]) for n in ("neg_max", "row_sum", "inverse"))
        attended = [ph.sb("attended_hi", [P, quads, ROWS], F32R), q_parts[:, :, :, :].rearrange("p s k n -> p (s k) n")]
        slot_width = -(-nk // 512) * 512
        score_banks = score_slots * slot_width // 512
        banks = ph.psum(8 - score_banks)
        scores = ph.ctx.enter_context(nc.psum_tensor(f"{name}_scores", [P, score_slots, slot_width], F32))
        ring = ph.ring(banks)
        q_dram = nc.dram_tensor(f"{name}_q_dram", [2, D, ROWS], F32).ap()
        k_dram = nc.dram_tensor(f"{name}_k_dram", [2, D, B * nk], F32).ap()
        mask_dram = nc.dram_tensor(f"{name}_mask_dram", [1, B, nk], F32).ap()
        written = [ph.sem(f"written{i}") for i in range(KT)]
        loaded, small_loaded = [ph.sem(f"loaded{i}") for i in range(5)], ph.sem("small_loaded")
        q_scaled, w_hi, w_lo = ph.sem("q_scaled"), ph.sem("w_hi"), ph.sem("w_lo")
        zeroed, padded, cleared, mask_ready, gate_ready, resid_ready = ph.sem("zeroed"), ph.sem("padded"), [ph.sem(f"cleared{i}") for i in range(2)], ph.sem("mask_ready"), ph.sem("gate_ready"), ph.sem("resid_ready")
        stack_loaded = [ph.sem(f"stack_loaded{i}") for i in range(2)]
        scores_full, max_done, exp_done = ph.sem("scores_full"), ph.sem("max_done"), ph.sem("exp_done")
        inverse_done, normed, dve_done, bias_ready = ph.sem("inverse_done"), ph.sem("normed"), ph.sem("dve_done"), ph.sem("bias_ready")
        block = ph.block()

        w = [[w_qkv[:, part, i, :] if i < 3 else w_out[:, part, i - 3, :] for i in range(5)] for part in range(2)]
        wq, wk, wv = ([w[part][i].rearrange("p (k n) -> p k n", k=KT) for part in range(2)] for i in range(3))
        wo = [w_out[:, part, :, :].rearrange("p s (g n) -> p (s g) n", g=2) for part in range(2)]

        q_jobs = [(mt,) for mt in range(KT)]
        k_jobs = [(mt, b, c0, n) for mt in range(KT) for b in range(B) for c0, n in ([(0, S)] + ([(S, extra)] if extra else []))]
        v_jobs = [(b, 2 * i) for b in range(B) for i in range(nkt // 2)]
        k0 = len(q_jobs)
        v0 = k0 + len(k_jobs)
        u0 = v0 + len(v_jobs)
        tj = 2 * nkt // 4
        HEADS = units * 4

        def key_source(part, kt, b, c0, n):
            src, per = (sources[0], S) if c0 < S else (sources[1], extra)
            at = b * per + (c0 if c0 < S else c0 - S)
            return src[part][:, kt, at:at + n]

        LAG = 2

        def product_before(t):
            return t // 4 - 1 if t % 4 == 1 and t >= 4 else None

        order = []
        for t in range(HEADS):
            if product_before(t) is not None:
                order.append(("V", product_before(t), 0))
            order += [("T", t, c) for c in range(tj)]
        order.append(("V", units - 1, 0))

        def slot_scores(m):
            return scores[:, m % score_slots, 0:nk]

        job_of = {what: u0 + i for i, what in enumerate(order)}
        o0 = u0 + len(order)
        by_act = lambda g, c: (c + (g if tj % 2 else 0)) % 2 == 0
        unit_copies = lambda unit: [job_of["T", 4 * unit + j, c] for j in range(4) for c in range(tj)]

        @block.sync
        def _(sp):
            for i in range(5):
                sp.dma_start(stage[:, i, :], io[cfg["w"]][:, i, :]).then_inc(loaded[i], 16)
                if i == 0:
                    sp.dma_start(bias[:, :], io[cfg["bias"]]).then_inc(small_loaded, 16)
                    sp.dma_start(mask_raw[:, :], io[cfg["mask"]]).then_inc(small_loaded, 16)
                    sp.dma_start(gate[:, :], io[cfg["gate"]].partition_broadcast(P)).then_inc(small_loaded, 16)
                    sp.dma_start(out_bias[:, :], io[cfg["out_bias"]].partition_broadcast(P)).then_inc(small_loaded, 16)
            for kt in range(KT):
                ring.wait_evacuated(sp, kt)
                k_last = k0 + (kt + 1) * len(k_jobs) // KT - 1
                ring.wait_evacuated(sp, k_last)
                for part in range(2):
                    rows = slice(kt * P, (kt + 1) * P)
                    sp.dma_start(q_dram[part, rows, :], raw(qT[part][:, kt, :])).then_inc(written[kt], 16)
                    sp.dma_start(k_dram[part, rows, :], raw(kT[part][:, kt, :])).then_inc(written[kt], 16)
                if kt == 0:
                    sp.wait_ge(mask_ready, 1)
                    sp.dma_start(mask_dram, raw(mask_row[:, :, :])).then_inc(written[kt], 16)
            for o in range(OCTETS):
                b, kt, r = o // KT, o % KT, o % 2
                if b == 0:
                    sp.wait_ge(written[kt], 64 if kt else 80)
                sp.wait_ge(cleared[r], 3)
                if o >= 2:
                    sp.wait_ge(scores_full, 16 * (o - 1))
                for a in range(2):
                    for c, (kp, qp) in enumerate(((0, 0), (0, 1), (1, 0))):
                        row = 64 * a + 16 * c
                        for to, of, at, n in ((k_stack[r][row:row + 16, :, :], k_dram[kp], b * nk, nk),
                                              (q_stack[r][row:row + 16, a:8:2, :], q_dram[qp], b * Q, Q)):
                            heads = of[kt * P:(kt + 1) * P, at:at + n].rearrange("(t a r) n -> a r t n", a=2, r=DN)[a]
                            sp.dma_start(raw(to), heads).then_inc(stack_loaded[r], 16)
                    row = 64 * a + 48
                    sp.dma_start(raw(k_stack[r][row:row + 1, :, :]),
                                 mask_dram[0:1, b:b + 1, :].broadcast_to([1, 4, nk])).then_inc(stack_loaded[r], 16)
        stack_dmas = 14

        @block.gpsimd
        def _(pool):
            nc.gpsimd.memset(raw(mask_row[:, :, :]), 0.0)
            nc.gpsimd.memset(v[:, :, :], 0.0).then_inc(padded, 1)
            for r in range(2):
                nc.gpsimd.memset(raw(q_stack[r][:, :, :]), 0.0).then_inc(zeroed, 1)
                pool.wait_ge(zeroed, r + 1)
                for a in range(2):
                    nc.gpsimd.memset(raw(q_stack[r][64 * a + 32:64 * a + 64, a:8:2, :]), 1.0).then_inc(cleared[r], 1)
                pool.wait_ge(cleared[r], 2)
                if r:
                    pool.wait_ge(ring.full, u0)
                nc.gpsimd.memset(raw(k_stack[r][:, :, :]), 0.0).then_inc(cleared[r], 1)
            for m in range(2 * HEADS):
                pool.wait_ge(inverse_done, m + 1)
                slot, small = m % probs_slots, m % small_slots
                nc.gpsimd.tensor_scalar(probs[:, slot, :], probs[:, slot, :], inverse[:, small:small + 1], 1.0,
                                        ALU.mult, ALU.mult).then_inc(normed, 1)

        @block.tensor
        def _(pe):
            for job, (mt,) in enumerate(q_jobs):
                pe.wait_ge(w_lo, 1)
                ring.wait_bank(pe, job)
                for kt in range(KT):
                    last = product3(nc, ring.bank(job)[:, :], [t[:, kt, mt * P:(mt + 1) * P] for t in wq],
                                    [t[:, kt, :] for t in queries], kt == 0, kt == KT - 1)
                last.then_inc(ring.full, 1)
            for i, (mt, b, c0, n) in enumerate(k_jobs):
                job = k0 + i
                pe.wait_ge(w_lo, 2)
                ring.wait_bank(pe, job)
                for kt in range(KT):
                    last = product3(nc, ring.bank(job)[:, 0:n], [t[:, kt, mt * P:(mt + 1) * P] for t in wk],
                                    [key_source(part, kt, b, c0, n) for part in range(2)], kt == 0, kt == KT - 1)
                last.then_inc(ring.full, 1)
            for i, (b, t0) in enumerate(v_jobs):
                job = v0 + i
                pe.wait_ge(w_lo, 3)
                ring.wait_bank(pe, job)
                for t in range(2):
                    for kt in range(KT):
                        last = product3(nc, ring.bank(job)[:, t * D:(t + 1) * D],
                                        [key_source(part, kt, b, (t0 + t) * P, P) for part in range(2)],
                                        [t_[:, kt, :] for t_ in wv], kt == 0, kt == KT - 1)
                last.then_inc(ring.full, 1)

            def transpose_head(g):
                pe.wait_ge(normed, 2 * g + 2)
                for c in range(tj):
                    job = job_of["T", g, c]
                    ring.wait_bank(pe, job)
                    for i in range(4):
                        qt, kt = divmod(4 * c + i, nkt)
                        last = nc.tensor.transpose(ring.bank(job)[:, i * P:(i + 1) * P],
                                                   probs[:, (2 * g + qt) % probs_slots, kt * P:(kt + 1) * P], keep["ident"][:, :])
                    last.then_inc(ring.full, 1)

            def product_v(unit):
                job = job_of["V", unit, 0]
                ring.wait_bank(pe, job)
                b, quad = divmod(unit, quads)
                for back in range(ring.n):
                    ring.wait_evacuated(pe, unit_copies(unit)[-1 - back])
                for kt in range(nkt):
                    for j in range(4):
                        g = 4 * unit + j
                        moving = probsT[:, g % TSLOTS, :].rearrange("p (t k n) -> p t k n", t=2, k=nkt)[:, :, kt, :]
                        last = nc.tensor.matmul(ring.bank(job)[32 * j:32 * j + 32, 0:Q],
                                                v[:, b * nkt + kt, 32 * (4 * quad + j):32 * (4 * quad + j) + 32],
                                                moving, start=kt == 0, stop=kt == nkt - 1)
                last.then_inc(ring.full, 1)

            for g in range(HEADS + LAG):
                t = g - LAG
                if g < HEADS:
                    octet, e = divmod(g, 8)
                    r = octet % 2
                    if e == 0:
                        pe.wait_ge(stack_loaded[r], 16 * stack_dmas * (octet // 2 + 1))
                    for qt in range(2):
                        m = 2 * g + qt
                        if m >= score_slots:
                            pe.wait_ge(exp_done, m - score_slots + 1)
                        for c0, n in [(0, S)] + ([(S, extra)] if extra else []):
                            last = nc.tensor.matmul(slot_scores(m)[:, c0:c0 + n], q_stack[r][:, e, qt * P:(qt + 1) * P],
                                                    k_stack[r][:, e // 2, c0:c0 + n], start=True, stop=True)
                        last.then_inc(scores_full, 1)
                if t >= 0:
                    if product_before(t) is not None:
                        product_v(product_before(t))
                    transpose_head(t)
            product_v(units - 1)

            ring.wait_evacuated(pe, job_of["V", units - 1, 0])
            pe.wait_ge(w_lo, 5)
            for t in range(RT):
                job = o0 + t
                ring.wait_bank(pe, job)
                for quad in range(quads):
                    last = product3(nc, ring.bank(job)[:, 0:D], [x[:, quad, t * P:(t + 1) * P] for x in attended],
                                    [x[:, quad, :] for x in wo], quad == 0, quad == quads - 1)
                last.then_inc(ring.full, 1)

        @block.scalar
        def _(act):
            act.wait_ge(q_scaled, 1)
            for i in range(5):
                act.wait_ge(loaded[i], 16)
                nc.scalar.copy(w[0][i], stage[:, i, :]).then_inc(w_hi, 1)
            act.wait_ge(small_loaded, 64)
            if cfg["gated"]:
                nc.scalar.activation(gate[:, :], gate[:, :], ACT.Tanh).then_inc(gate_ready, 1)
            act.wait_ge(bias_ready, 1)
            for job in range(len(q_jobs)):
                act.wait_ge(ring.full, job + 1)
                nc.scalar.activation(qT[0][:, job, :], ring.bank(job)[:, :], ACT.Identity,
                                     bias=bias[:, job:job + 1]).then_inc(ring.hi_done, 1)
            for i, (mt, b, c0, n) in enumerate(k_jobs):
                job = k0 + i
                act.wait_ge(ring.full, job + 1)
                nc.scalar.activation(kT[0][:, mt, b * nk + c0:b * nk + c0 + n], ring.bank(job)[:, 0:n], ACT.Identity,
                                     bias=bias[:, 2 + mt:3 + mt]).then_inc(ring.hi_done, 1)
            act.wait_ge(padded, 1)
            for i, (b, t0) in enumerate(v_jobs):
                job = v0 + i
                act.wait_ge(ring.full, job + 1)
                for t in range(2):
                    last = nc.scalar.copy(v[:, b * nkt + t0 + t, :].rearrange("p (h d) -> p h d", h=H)[:, :, 0:DN],
                                          ring.bank(job)[:, t * D:(t + 1) * D].rearrange("p (h d) -> p h d", h=H))
                last.then_inc(ring.freed_by(job), 1)

            def evacuate(t):
                if product_before(t) is not None:
                    high_v(product_before(t))
                for c in range(tj):
                    if by_act(t, c):
                        job = job_of["T", t, c]
                        act.wait_ge(ring.full, job + 1)
                        nc.scalar.copy(probsT[:, t % TSLOTS, c * 512:(c + 1) * 512],
                                       ring.bank(job)[:, :]).then_inc(ring.freed_by(job), 1)

            def high_v(unit):
                job = job_of["V", unit, 0]
                b, quad = divmod(unit, quads)
                act.wait_ge(ring.full, job + 1)
                nc.scalar.activation(attended[0][:, quad, b * Q:(b + 1) * Q], ring.bank(job)[:, 0:Q], ACT.Identity,
                                     bias=bias[:, 4 + quad:5 + quad]).then_inc(ring.hi_done, 1)

            for g in range(HEADS + LAG):
                if g < HEADS:
                    for m in (2 * g, 2 * g + 1):
                        small = m % small_slots
                        act.wait_ge(max_done, m + 1)
                        if m >= probs_slots:
                            act.wait_ge(ring.full, job_of["T", (m - probs_slots) // 2, tj - 1] + 1)
                        nc.scalar.activation(probs[:, m % probs_slots, :], slot_scores(m), ACT.Exp,
                                             bias=neg_max[:, small:small + 1],
                                             accum_out=row_sum[:, small:small + 1]).then_inc(exp_done, 1)
                if g >= LAG:
                    evacuate(g - LAG)
            high_v(units - 1)

        @block.vector
        def _(dve):
            link = Chain(dve, dve_done)
            dve.wait_ge(loaded[0], 16)
            nc.vector.tensor_scalar(stage[:, 0, :], stage[:, 0, :], cfg["scale"], None, ALU.mult).then_inc(q_scaled, 1)
            for i in range(5):
                dve.wait_ge(w_hi, i + 1)
                nc.vector.tensor_tensor(w[1][i], stage[:, i, :], raw(w[0][i]), ALU.subtract).then_inc(w_lo, 1)
            dve.wait_ge(small_loaded, 64)
            dve.wait_ge(padded, 1)
            nc.vector.tensor_scalar(bias[:, 0:2], bias[:, 0:2], cfg["scale"], None, ALU.mult).then_inc(bias_ready, 1)
            nc.vector.tensor_scalar(mask_row[0:1, :, 0:S], mask_raw[0:1, :].rearrange("o (b s) -> o b s", b=B), 0.0, MASKED,
                                    ALU.is_equal, ALU.mult).then_inc(mask_ready, 1)
            dve.wait_ge(bias_ready, 1)

            def low(job, nth, out, col, n):
                dve.wait_ge(ring.hi_done, nth + 1)
                nc.vector.scalar_tensor_tensor(out[1], ring.bank(job)[:, 0:n], bias[:, col:col + 1], raw(out[0]),
                                               ALU.add, ALU.subtract).then_inc(ring.freed_by(job), 1)

            for job in range(len(q_jobs)):
                low(job, job, [t[:, job, :] for t in qT], job, 512)
            for i, (mt, b, c0, n) in enumerate(k_jobs):
                low(k0 + i, k0 + i, [t[:, mt, b * nk + c0:b * nk + c0 + n] for t in kT], 2 + mt, n)

            def low_v(unit):
                b, quad = divmod(unit, quads)
                low(job_of["V", unit, 0], v0 + unit, [t[:, quad, b * Q:(b + 1) * Q] for t in attended], 4 + quad, Q)

            dve.wait_ge(written[0], 80)
            dve.wait_ge(written[1], 64)
            for g in range(HEADS + LAG):
                t = g - LAG
                if g < HEADS:
                    for m in (2 * g, 2 * g + 1):
                        small = m % small_slots
                        dve.wait_ge(scores_full, m + 1)
                        nc.vector.tensor_reduce(neg_max[:, small:small + 1], slot_scores(m), AX.X, ALU.max,
                                                negate=True).then_inc(max_done, 1)
                if 1 <= g <= HEADS:
                    for m in (2 * g - 2, 2 * g - 1):
                        small = m % small_slots
                        dve.wait_ge(exp_done, m + 1)
                        if m >= small_slots:
                            dve.wait_ge(normed, m - small_slots + 1)
                        nc.vector.reciprocal(inverse[:, small:small + 1],
                                             row_sum[:, small:small + 1]).then_inc(inverse_done, 1)
                if t >= 0:
                    if product_before(t) is not None:
                        low_v(product_before(t))
                    for c in range(tj):
                        if not by_act(t, c):
                            job = job_of["T", t, c]
                            dve.wait_ge(ring.full, job + 1)
                            nc.vector.tensor_copy(probsT[:, t % TSLOTS, c * 512:(c + 1) * 512],
                                                  ring.bank(job)[:, :]).then_inc(ring.freed_by(job), 1)
            low_v(units - 1)

            if cfg["gated"]:
                dve.wait_ge(gate_ready, 1)
            for t in range(RT):
                last = nc.vector.tensor_tensor(keep["x"][:, t, :] if cfg["in_place"] else keep["sum"][:, t, :],
                                               keep["x"][:, t, :], out_bias[:, :], ALU.add)
            link(last)
            for t in range(RT):
                job = o0 + t
                rows = (keep["x"] if cfg["in_place"] else keep["sum"])[:, t, :]
                dve.wait_ge(ring.full, job + 1)
                nc.vector.scalar_tensor_tensor(rows, ring.bank(job)[:, 0:D], gate[:, 0:1] if cfg["gated"] else 1.0, rows,
                                               ALU.mult, ALU.add).then_inc(ring.freed_by(job), 1)


def normalised_rows(nc, io, keep, name, lnp, out, eps, context=False):
    with Phase(nc, name) as ph:
        parts = NormParts(ph, lnp, CT if context else RT)
        rows = ph.sb("ctx_rows", [P, CT, D]) if context else keep["x"]
        rows_loaded = ph.sem("rows_loaded")
        ring = ph.ring(ph.psum(4))
        block = ph.block()

        @block.sync
        def _(sp):
            parts.load(sp, io)
            if context:
                sp.dma_start(rows[:, :, :], io["ctx_2048"].rearrange("b (t p) d -> p (b t) d", p=P)).then_inc(rows_loaded, 16)

        @block.gpsimd
        def _(pool):
            parts.root(nc, pool)

        @block.tensor
        def _(pe):
            parts.transpose(nc, pe, ring, keep)

        @block.scalar
        def _(act):
            parts.scale(nc, act, ring)

        @block.vector
        def _(dve):
            link = Chain(dve, parts.dve_done)
            if context:
                dve.wait_ge(rows_loaded, 16)
            parts.normalise(nc, dve, link, rows, eps, True)
            parts.split(nc, dve, link, ring, out)


class NormParts:

    def __init__(self, ph, lnp, tiles=RT):
        self.lnp, self.tiles = lnp, tiles
        self.normed = ph.sb("normed", [P, tiles, D])
        self.whole = ph.sb("whole", [P, KT, tiles * P])
        self.stats, self.moments = ph.sb("stats", [P, tiles, 6]), ph.sb("moments", [P, tiles, 2])
        self.shifted, self.power, self.rstd = ph.sb("shifted", [P, tiles]), ph.sb("power", [P, tiles]), ph.sb("rstd", [P, tiles])
        self.scale_shift = ph.sb("scale_shift", [P, 4])
        self.cols_loaded, self.power_set = ph.sem("cols_loaded"), ph.sem("power_set")
        self.shifted_ready, self.rstd_ready, self.normed_ready = ph.sem("shifted_ready"), ph.sem("rstd_ready"), ph.sem("normed_ready")
        self.dve_done = ph.sem("dve_done")
        self.jobs = [(kt, 4 * g) for kt in range(KT) for g in range(tiles // 4)]

    def load(self, sp, io):
        sp.dma_start(self.scale_shift[:, :], io[self.lnp]).then_inc(self.cols_loaded, 16)

    def root(self, nc, pool):
        nc.gpsimd.memset(self.power[:, :], -0.5).then_inc(self.power_set, 1)
        pool.wait_ge(self.power_set, 1)
        pool.wait_ge(self.shifted_ready, 1)
        nc.gpsimd.tensor_tensor(self.rstd[:, :], self.shifted[:, :], self.power[:, :], ALU.pow).then_inc(self.rstd_ready, 1)

    def normalise(self, nc, dve, link, rows, eps, centred):
        row_statistics(nc, link, rows, self.tiles, self.stats, self.moments, self.shifted, eps,
                       centred).then_inc(self.shifted_ready, 1)
        dve.wait_ge(self.rstd_ready, 1)
        for t in range(self.tiles):
            mean = self.moments[:, t, 0:1] if centred else 0.0
            last = nc.vector.tensor_scalar(self.normed[:, t, :], rows[:, t, :], mean, self.rstd[:, t:t + 1],
                                           ALU.subtract, ALU.mult)
        last.then_inc(self.normed_ready, 1)

    def transpose(self, nc, pe, ring, keep):
        pe.wait_ge(self.normed_ready, 1)
        for job, (kt, t0) in enumerate(self.jobs):
            for t in range(4):
                last = nc.tensor.transpose(ring.bank(job)[:, t * P:(t + 1) * P],
                                           self.normed[:, t0 + t, kt * P:(kt + 1) * P], keep["ident"][:, :])
            last.then_inc(ring.full, 1)

    def scale(self, nc, act, ring):
        act.wait_ge(self.cols_loaded, 16)
        for job, (kt, t0) in enumerate(self.jobs):
            act.wait_ge(ring.full, job + 1)
            nc.scalar.activation(self.whole[:, kt, t0 * P:t0 * P + 512], ring.bank(job)[:, :], ACT.Identity,
                                 bias=self.scale_shift[:, 2 + kt:3 + kt],
                                 scale=self.scale_shift[:, kt:kt + 1]).then_inc(ring.hi_done, 1)

    def split(self, nc, dve, link, ring, out):
        for job, (kt, t0) in enumerate(self.jobs):
            hi, lo, whole = (t[:, kt, t0 * P:t0 * P + 512] for t in (*out, self.whole))
            dve.wait_ge(ring.hi_done, job + 1)
            link(nc.vector.tensor_copy(hi, whole))
            nc.vector.tensor_tensor(lo, whole, raw(hi), ALU.subtract).then_inc(ring.freed_by(job), 1)


def mlp(nc, io, keep, cfg):
    with Phase(nc, cfg["name"]) as ph:
        parts = NormParts(ph, cfg["lnp"])
        stage = ph.sb("stage", [P, 8, 512])
        w = ph.hilo("w", [P, 8, 512])
        b1 = ph.sb("b1", [P, FT])
        b2 = ph.sb("b2", [P, D])
        hT = ph.hilo("hT", [P, KT, ROWS])
        activated = ph.sb("activated", [P, 2, ROWS])
        hidden = ph.hilo("hidden", [P, FT, ROWS])
        ring = ph.ring(ph.psum(4))
        loaded = [ph.sem(f"loaded{i}") for i in range(4)]
        small_loaded, w_hi, w_lo = ph.sem("small_loaded"), ph.sem("w_hi"), ph.sem("w_lo")
        stored = keep["stored"]
        block = ph.block()
        w1 = [t[:, 0:4, :].rearrange("p (k s) n -> p k (s n)", k=KT) for t in w]
        w2 = [t[:, 4:8, :].rearrange("p s (g n) -> p (s g) n", g=2) for t in w]
        rows = keep[cfg["rows"]]
        up0 = KT
        down0 = up0 + FT

        @block.sync
        def _(sp):
            parts.load(sp, io)
            for i in range(4):
                sp.dma_start(stage[:, 2 * i:2 * i + 2, :], io[cfg["w"]][:, 2 * i:2 * i + 2, :]).then_inc(loaded[i], 16)
            sp.dma_start(b1[:, :], io[cfg["b1"]]).then_inc(small_loaded, 16)
            sp.dma_start(b2[:, :], io[cfg["b2"]].partition_broadcast(P)).then_inc(small_loaded, 16)
            if cfg["out"] is not None:
                for t in range(RT):
                    ring.wait_evacuated(sp, down0 + t)
                    sp.dma_start(io["out"].rearrange("b (t p) d -> p (b t) d", p=P)[:, t, :], keep["x"][:, t, :]).then_inc(stored, 16)
                sp.wait_ge(stored, 16 * RT)

        @block.gpsimd
        def _(pool):
            parts.root(nc, pool)

        @block.tensor
        def _(pe):
            parts.transpose(nc, pe, ring, keep)
            for m in range(FT):
                job = up0 + m
                if m == 0:
                    ring.wait_evacuated(pe, 0)
                    ring.wait_evacuated(pe, 1)
                pe.wait_ge(w_lo, 4)
                ring.wait_bank(pe, job)
                for kt in range(KT):
                    last = product3(nc, ring.bank(job)[:, :], [t[:, kt, m * P:(m + 1) * P] for t in w1],
                                    [t[:, kt, :] for t in hT], kt == 0, kt == KT - 1)
                last.then_inc(ring.full, 1)
            pe.wait_ge(w_lo, 8)
            for t in range(RT):
                job = down0 + t
                ring.wait_bank(pe, job)
                for f in range(FT):
                    if t == 0:
                        ring.wait_evacuated(pe, up0 + f)
                    last = product3(nc, ring.bank(job)[:, 0:D], [x[:, f, t * P:(t + 1) * P] for x in hidden],
                                    [x[:, f, :] for x in w2], f == 0, f == FT - 1)
                last.then_inc(ring.full, 1)

        @block.scalar
        def _(act):
            for i in range(8):
                act.wait_ge(loaded[i // 2], 16)
                nc.scalar.copy(w[0][:, i, :], stage[:, i, :]).then_inc(w_hi, 1)
            parts.scale(nc, act, ring)
            act.wait_ge(small_loaded, 32)
            for m in range(FT):
                job = up0 + m
                act.wait_ge(ring.full, job + 1)
                if m >= 2:
                    ring.wait_evacuated(act, job - 2)
                nc.scalar.activation(activated[:, m % 2, :], ring.bank(job)[:, :], cfg["gelu"],
                                     bias=b1[:, m:m + 1]).then_inc(ring.hi_done, 1)

        @block.vector
        def _(dve):
            link = Chain(dve, parts.dve_done)
            parts.normalise(nc, dve, link, rows, cfg["eps"], cfg["centred"])
            for i in range(8):
                dve.wait_ge(w_hi, i + 1)
                nc.vector.tensor_tensor(w[1][:, i, :], stage[:, i, :], raw(w[0][:, i, :]), ALU.subtract).then_inc(w_lo, 1)
                if i == 3:
                    parts.split(nc, dve, link, ring, hT)
            dve.wait_ge(small_loaded, 32)
            for t in range(RT):
                last = nc.vector.tensor_tensor(keep["x"][:, t, :], keep["x"][:, t, :], b2[:, :], ALU.add)
            link(last)
            for m in range(FT):
                job = up0 + m
                dve.wait_ge(ring.hi_done, up0 + m + 1)
                link(nc.vector.tensor_copy(hidden[0][:, m, :], activated[:, m % 2, :]))
                nc.vector.tensor_tensor(hidden[1][:, m, :], activated[:, m % 2, :], raw(hidden[0][:, m, :]),
                                        ALU.subtract).then_inc(ring.freed_by(job), 1)
            for t in range(RT):
                job = down0 + t
                dve.wait_ge(ring.full, job + 1)
                nc.vector.tensor_tensor(keep["x"][:, t, :], ring.bank(job)[:, 0:D], keep["x"][:, t, :],
                                        ALU.add).then_inc(ring.freed_by(job), 1)


def wide_prologue(nc, io, keep, cfg):
    name, i = cfg["name"], cfg["index"]
    with Phase(nc, name + "_pre") as ph:
        parts = NormParts(ph, f"L1_ln{i}p")
        wq = ph.sb("wq", [P, KT, H * DW])
        bias_k = ph.sb("bias_k", [P, H * DW])
        product = ph.sb("product", [P, KT, H * DW])
        folded = ph.sb("folded", [P, KT, H])
        cols = ph.sb("cols", [P, 5, H])
        ones = ph.sb("ones", [P, P])
        spread = ph.sb("spread", [P, H, H])
        wo = ph.sb("wo", [P, H, D])
        ring = ph.ring(ph.psum(4))
        loaded, small_loaded, wo_loaded = ph.sem("loaded"), ph.sem("small_loaded"), ph.sem("wo_loaded")
        set_up, folded_ready, spread_ready = ph.sem("set_up"), ph.sem("folded_ready"), ph.sem("spread_ready")
        block = ph.block()

        @block.sync
        def _(sp):
            parts.load(sp, io)
            sp.dma_start(cols[:, 0:4, :], io[f"L1_cols{i}"]).then_inc(small_loaded, 16)
            sp.dma_start(bias_k[:, :], io[f"L1_bias_k{i}"].partition_broadcast(P)).then_inc(loaded, 16)
            sp.dma_start(wq[:, :, :], io[f"L1_wq{i}"].rearrange("(k p) n -> p k n", p=P)).then_inc(loaded, 16)
            sp.dma_start(wo[:, :, :], io[f"L1_wo{i}"].rearrange("(h p) n -> p h n", p=P)).then_inc(wo_loaded, 16)

        @block.gpsimd
        def _(pool):
            nc.gpsimd.memset(ones[:, :], 1.0).then_inc(set_up, 1)
            nc.gpsimd.memset(spread[:, :, :], 0.0).then_inc(set_up, 1)
            parts.root(nc, pool)

        @block.tensor
        def _(pe):
            pe.wait_ge(spread_ready, 1)
            pe.wait_ge(wo_loaded, 16)
            for h in range(H):
                last = nc.tensor.matmul(ring.bank(2)[0:H, 0:D], spread[:, h, :], wo[:, h, :], start=h == 0, stop=h == H - 1)
            parts.transpose(nc, pe, ring, keep)
            last = None
            pe.wait_ge(folded_ready, 1)
            ring.wait_evacuated(pe, 1)
            for t in range(RT):
                out = ring.bank(3)[:, t * H:(t + 1) * H]
                for kt in range(KT):
                    nc.tensor.matmul(out, parts.whole[:, kt, t * P:(t + 1) * P], folded[:, kt, :], start=kt == 0, stop=False)
                last = nc.tensor.matmul(out, ones[:, :], cols[:, 4, :], start=False, stop=True)
            last.then_inc(ring.full, 1)

        @block.scalar
        def _(act):
            parts.scale(nc, act, ring)
            act.wait_ge(ring.full, 3)
            nc.scalar.copy(keep["bias_values"][:, :], ring.bank(2)[0:H, 0:D]).then_inc(ring.freed_by(2), 1)
            nc.scalar.mul(keep["bias_scores"][:, :, :].rearrange("p t h -> p (t h)"), ring.bank(3)[:, 0:RT * H],
                          float(DW) ** -0.5).then_inc(ring.hi_done, 1)

        @block.vector
        def _(dve):
            link = Chain(dve, parts.dve_done)
            dve.wait_ge(small_loaded, 16)
            dve.wait_ge(set_up, 2)
            link(nc.vector.tensor_tensor(cols[:, 4, :], cols[:, 0, :], cols[:, 1, :], ALU.mult))
            nc.vector.tensor_tensor(spread[:, :, :].rearrange("p a b -> p (a b)")[:, 0:H * H:H + 1], cols[:, 3, :], cols[:, 2, :],
                                    ALU.subtract).then_inc(spread_ready, 1)
            parts.normalise(nc, dve, link, keep["x"], 1e-5, True)
            parts.split(nc, dve, link, ring, keep["hT"])
            dve.wait_ge(loaded, 32)
            for kt in range(KT):
                link(nc.vector.tensor_tensor(product[:, kt, :], wq[:, kt, :], bias_k[:, :], ALU.mult))
            for kt in range(KT):
                last = nc.vector.tensor_reduce(folded[:, kt, :], product[:, kt, :].rearrange("p (h d) -> p h d", h=H), AX.X, ALU.add)
            last.then_inc(folded_ready, 1)
            dve.wait_ge(ring.hi_done, 3)
            nc.vector.tensor_scalar(keep["neg_bias_scores"][:, :, :], keep["bias_scores"][:, :, :], -1.0, None, ALU.mult)


def wide_attention(nc, io, keep, cfg):
    name, i = cfg["name"], cfg["index"]
    UN = 2 * B
    SK = S // P
    scale = float(DW) ** -0.5
    PROJ = [("q", 0), ("q", 1), ("k", 0, 0), ("k", 0, 1), ("k", 1, 0), ("k", 1, 1)] + [("v", t) for t in range(0, CT, 2)]
    SHARES = [PROJ[0:3], PROJ[3:6], PROJ[6:8], PROJ[8:10]]
    NPROJ = len(PROJ)
    with Phase(nc, name) as ph:
        stage = [ph.sb(f"stage{j}", [P, 2048]) for j in range(2)]
        w = [ph.hilo(f"w{j}", [P, 1536]) for j in range(2)]
        wo = [ph.hilo(f"wo{j}", [P, 2, D]) for j in range(2)]
        q = [ph.hilo(f"q{j}", [P, 2, ROWS]) for j in range(2)]
        k = [ph.hilo(f"k{j}", [P, 2, B * S]) for j in range(2)]
        v = [ph.hilo(f"v{j}", [P, CT, 2 * DW]) for j in range(2)]
        cols = ph.sb("cols", [P, 4, H])
        bk = ph.sb("bk", [P, H])
        out_bias = ph.sb("out_bias", [P, D])
        probs = ph.sb("probs", [P, 2, 2, S])
        probsT = [ph.hilo(f"probsT{j}", [P, 2 * SK * P]) for j in range(2)]
        attended = [ph.hilo(f"attended{j}", [P, Q]) for j in range(2)]
        top, neg_max, bias_shifted = ph.sb("top", [P, 2]), ph.sb("neg_max", [P, 2, 2]), ph.sb("bias_shifted", [P, 2, 2])
        row_sum, bias_prob, inverse = ph.sb("row_sum", [P, 2, 2]), ph.sb("bias_prob", [P, 2, 2]), ph.sb("inverse", [P, 2])
        bias_probs = ph.sb("bias_probs", [P, RT, H])
        bias_probsT = ph.sb("bias_probsT", [H, ROWS])
        banks = ph.psum(4)
        scores = ph.ctx.enter_context(nc.psum_tensor(f"{name}_scores", [P, 2, S], F32))
        sums = ph.ctx.enter_context(nc.psum_tensor(f"{name}_sums", [P, RT, D], F32))
        ring = ph.ring(banks)
        loaded, small_loaded = [ph.sem(f"loaded{j}") for j in range(2)], ph.sem("small_loaded")
        pool_done, w_ready, wo_ready = ph.sem("pool_done"), ph.sem("w_ready"), ph.sem("wo_ready")
        cols_scaled, out_done, scores_full = ph.sem("cols_scaled"), ph.sem("out_done"), ph.sem("scores_full")
        max_done, exp_done, normed, dve_done = ph.sem("max_done"), ph.sem("exp_done"), ph.sem("normed"), ph.sem("dve_done")
        sums_full = ph.sem("sums_full")
        block = ph.block()
        LAST = PAIRS * UN - 1

        job_of, n = {}, 0
        for item in PROJ:
            job_of[0, item] = n
            n += 1
        for g in range(LAST + 2):
            p, u = divmod(g, UN)
            if g:
                for qt in range(2):
                    job_of["T", g - 1, qt] = n
                    n += 1
            if p + 1 < PAIRS:
                for item in SHARES[u]:
                    job_of[p + 1, item] = n
                    n += 1
            if g:
                job_of["V", g - 1] = n
                n += 1
        job_of["bias"] = n

        def unit(g):
            p, u = divmod(g, UN)
            return p % 2, u // B, u % B, 2 * p + u // B

        @block.sync
        def _(sp):
            for p in range(PAIRS):
                if p >= 2:
                    sp.wait_ge(wo_ready, p - 1)
                sp.dma_start(stage[p % 2][:, :], io[f"L1_w{i}"][p]).then_inc(loaded[p % 2], 16)
                if p == 0:
                    sp.dma_start(cols[:, :, :], io[f"L1_cols{i}"]).then_inc(small_loaded, 16)
                    sp.dma_start(bk[:, :], io[f"L1_bk{i}"]).then_inc(small_loaded, 16)
                    sp.dma_start(out_bias[:, :], io[f"L1_bo{i}"].partition_broadcast(P)).then_inc(small_loaded, 16)

        @block.gpsimd
        def _(pool):
            link = Chain(pool, pool_done)
            for p in range(PAIRS):
                j = p % 2
                pool.wait_ge(loaded[j], 16 * (p // 2 + 1))
                link(nc.gpsimd.tensor_scalar(stage[j][:, 0:512], stage[j][:, 0:512], scale, 1.0, ALU.mult, ALU.mult))
                if p >= 2:
                    pool.wait_ge(ring.full, job_of[p - 2, PROJ[-1]] + 1)
                link(nc.gpsimd.tensor_scalar(w[j][0][:, :], stage[j][:, 0:1536], 1.0, 1.0, ALU.mult, ALU.mult))
                nc.gpsimd.tensor_tensor(w[j][1][:, :], stage[j][:, 0:1536], raw(w[j][0][:, :]), ALU.subtract).then_inc(w_ready, 1)
                if p >= 2:
                    pool.wait_ge(out_done, UN * (p - 1))
                part = stage[j][:, 1536:2048]
                link(nc.gpsimd.tensor_scalar(wo[j][0][:, :, :].rearrange("p h n -> p (h n)"), part, 1.0, 1.0, ALU.mult, ALU.mult))
                nc.gpsimd.tensor_tensor(wo[j][1][:, :, :].rearrange("p h n -> p (h n)"), part,
                                        raw(wo[j][0][:, :, :]).rearrange("p h n -> p (h n)"), ALU.subtract).then_inc(wo_ready, 1)

        @block.tensor
        def _(pe):
            def project(p, item):
                j, job = p % 2, job_of[p, item]
                wq, wk, wv = ([t[:, c * 512:(c + 1) * 512].rearrange("p (k n) -> p k n", k=KT) for t in w[j]] for c in range(3))
                ring.wait_bank(pe, job)
                for t in range(2 if item[0] == "v" else 1):
                    for kt in range(KT):
                        if item[0] == "q":
                            out = ring.bank(job)[:, :]
                            lhs, rhs = both(wq, np.s_[:, kt, item[1] * DW:(item[1] + 1) * DW]), both(keep["hT"], np.s_[:, kt, :])
                        elif item[0] == "k":
                            out = ring.bank(job)[:, :]
                            lhs = both(wk, np.s_[:, kt, item[1] * DW:(item[1] + 1) * DW])
                            rhs = both(keep["ctxT"], np.s_[:, kt, item[2] * S:(item[2] + 1) * S])
                        else:
                            out = ring.bank(job)[:, t * 2 * DW:(t + 1) * 2 * DW]
                            lhs = both(keep["ctxT"], np.s_[:, kt, (item[1] + t) * P:(item[1] + t + 1) * P])
                            rhs = both(wv, np.s_[:, kt, :])
                        last = product3(nc, out, lhs, rhs, kt == 0, kt == KT - 1)
                last.then_inc(ring.full, 1)

            def score(g):
                j, hh, b, h = unit(g)
                if g:
                    pe.wait_ge(exp_done, 3 * g - 1)
                for qt in range(2):
                    at = b * Q + qt * P
                    last = product3(nc, scores[:, qt, :], both(q[j], np.s_[:, hh, at:at + P]),
                                    both(k[j], np.s_[:, hh, b * S:(b + 1) * S]), True, True)
                last.then_inc(scores_full, 1)

            def transposes(g):
                for qt in range(2):
                    job = job_of["T", g, qt]
                    pe.wait_ge(normed, 2 * g + qt + 1)
                    ring.wait_bank(pe, job)
                    for kt in range(SK):
                        last = nc.tensor.transpose(ring.bank(job)[:, kt * P:(kt + 1) * P],
                                                   probs[:, g % 2, qt, kt * P:(kt + 1) * P], keep["ident"][:, :])
                    last.then_inc(ring.full, 1)

            def product_v(g):
                j, hh, b, h = unit(g)
                job = job_of["V", g]
                ring.wait_evacuated(pe, job_of["T", g, 0])
                ring.wait_evacuated(pe, job_of["T", g, 1])
                ring.wait_bank(pe, job)
                for kt in range(SK):
                    weights = [t[:, :].rearrange("p (q k n) -> p q k n", q=2, k=SK)[:, :, kt, :] for t in probsT[g % 2]]
                    last = product3(nc, ring.bank(job)[:, 0:Q], both(v[j], np.s_[:, b * SK + kt, hh * DW:(hh + 1) * DW]),
                                    weights, kt == 0, kt == SK - 1)
                last.then_inc(ring.full, 1)

            def output(g):
                j, hh, b, h = unit(g)
                pe.wait_ge(wo_ready, g // UN + 1)
                ring.wait_evacuated(pe, job_of["V", g])
                for qt in range(2):
                    last = product3(nc, sums[:, b * 2 + qt, :], both(attended[g % 2], np.s_[:, qt * P:(qt + 1) * P]),
                                    both(wo[j], np.s_[:, hh, :]), h == 0 and qt == 0, False, loose=True)
                last.then_inc(out_done, 1)

            pe.wait_ge(w_ready, 1)
            for item in PROJ:
                project(0, item)
            for g in range(LAST + 2):
                p, u = divmod(g, UN)
                if g <= LAST:
                    if u == 0:
                        for back in range(ring.n):
                            ring.wait_evacuated(pe, job_of[p, PROJ[-1 - back]])
                        ring.wait_evacuated(pe, job_of[p, ("k", 1, 1)])
                        ring.wait_evacuated(pe, job_of[p, ("q", 1)])
                    score(g)
                if g:
                    transposes(g - 1)
                if p + 1 < PAIRS:
                    if u == 0:
                        pe.wait_ge(w_ready, p + 2)
                    for item in SHARES[u]:
                        project(p + 1, item)
                if g >= 2:
                    output(g - 2)
                if g:
                    product_v(g - 1)
            output(LAST)

            job = job_of["bias"]
            ring.wait_bank(pe, job)
            for t in range(RT):
                last = nc.tensor.transpose(ring.bank(job)[0:H, t * P:(t + 1) * P], bias_probs[:, t, :], keep["ident"][:, :])
            last.then_inc(ring.full, 1)
            ring.wait_evacuated(pe, job)
            for t in range(RT):
                last = nc.tensor.matmul(sums[:, t, :], bias_probsT[:, t * P:(t + 1) * P], keep["bias_values"][:, :],
                                        start=False, stop=True, skip_group_check=True)
            last.then_inc(sums_full, 1)

        def destination(p, item):
            j = p % 2
            if item[0] == "q":
                return both(q[j], np.s_[:, item[1], :])
            if item[0] == "k":
                return both(k[j], np.s_[:, item[1], item[2] * S:(item[2] + 1) * S])
            return [t[:, item[1]:item[1] + 2, :].rearrange("p t n -> p (t n)") for t in v[j]]

        def bias_of(p, item):
            if item[0] == "v":
                return None
            return (cols[:, 0, :] if item[0] == "q" else bk[:, :])[:, 2 * p + item[1]:2 * p + item[1] + 1]

        @block.scalar
        def _(act):
            def high(job, out, column, n=512):
                act.wait_ge(ring.full, job + 1)
                source = ring.bank(job)[:, 0:n]
                if column is None:
                    nc.scalar.copy(out, source).then_inc(ring.hi_done, 1)
                else:
                    nc.scalar.activation(out, source, ACT.Identity, bias=column).then_inc(ring.hi_done, 1)

            act.wait_ge(small_loaded, 48)
            act.wait_ge(cols_scaled, 1)
            for item in PROJ:
                high(job_of[0, item], destination(0, item)[0], bias_of(0, item))
            for g in range(LAST + 2):
                p, u = divmod(g, UN)
                if g:
                    for qt in range(2):
                        high(job_of["T", g - 1, qt], probsT[(g - 1) % 2][0][:, qt * 512:(qt + 1) * 512], None)
                if g <= LAST:
                    act.wait_ge(max_done, g + 1)
                    for qt in range(2):
                        nc.scalar.activation(probs[:, g % 2, qt, :], scores[:, qt, :], ACT.Exp, bias=neg_max[:, g % 2, qt:qt + 1],
                                             accum_out=row_sum[:, g % 2, qt:qt + 1]).then_inc(exp_done, 1)
                    nc.scalar.activation(bias_prob[:, g % 2, :], bias_shifted[:, g % 2, :], ACT.Exp).then_inc(exp_done, 1)
                if p + 1 < PAIRS:
                    for item in SHARES[u]:
                        high(job_of[p + 1, item], destination(p + 1, item)[0], bias_of(p + 1, item))
                if g:
                    j, hh, b, h = unit(g - 1)
                    high(job_of["V", g - 1], attended[(g - 1) % 2][0][:, :], cols[:, 2, h:h + 1], Q)
            job = job_of["bias"]
            act.wait_ge(ring.full, job + 1)
            nc.scalar.copy(bias_probsT[:, :], ring.bank(job)[0:H, :]).then_inc(ring.freed_by(job), 1)

        @block.vector
        def _(dve):
            link = Chain(dve, dve_done)
            highs = [0]

            def low(job, out, column, n=512):
                highs[0] += 1
                dve.wait_ge(ring.hi_done, highs[0])
                source = ring.bank(job)[:, 0:n]
                if column is None:
                    nc.vector.tensor_tensor(out[1], source, raw(out[0]), ALU.subtract).then_inc(ring.freed_by(job), 1)
                else:
                    nc.vector.scalar_tensor_tensor(out[1], source, column, raw(out[0]), ALU.add,
                                                   ALU.subtract).then_inc(ring.freed_by(job), 1)

            dve.wait_ge(small_loaded, 48)
            nc.vector.tensor_scalar(cols[:, 0, :], cols[:, 0, :], scale, None, ALU.mult).then_inc(cols_scaled, 1)
            for t in range(RT):
                last = nc.vector.tensor_tensor(keep["x"][:, t, :], keep["x"][:, t, :], out_bias[:, :], ALU.add)
            link(last)
            dve.wait_ge(cols_scaled, 1)
            for item in PROJ:
                low(job_of[0, item], destination(0, item), bias_of(0, item))
            for g in range(LAST + 2):
                p, u = divmod(g, UN)
                s = g % 2
                if g <= LAST:
                    j, hh, b, h = unit(g)
                    dve.wait_ge(scores_full, g + 1)
                    link(nc.vector.tensor_reduce(top[:, :], scores[:, :, :], AX.X, ALU.max))
                    link(nc.vector.scalar_tensor_tensor(neg_max[:, s, :], top[:, :], -1.0, keep["neg_bias_scores"][:, 2 * b:2 * b + 2, h],
                                                        ALU.mult, ALU.min))
                    nc.vector.tensor_tensor(bias_shifted[:, s, :], keep["bias_scores"][:, 2 * b:2 * b + 2, h], neg_max[:, s, :],
                                            ALU.add).then_inc(max_done, 1)
                if g:
                    for qt in range(2):
                        low(job_of["T", g - 1, qt], [t[:, qt * 512:(qt + 1) * 512] for t in probsT[(g - 1) % 2]], None)
                if g <= LAST:
                    dve.wait_ge(exp_done, 3 * (g + 1))
                    link(nc.vector.tensor_tensor(inverse[:, :], row_sum[:, s, :], bias_prob[:, s, :], ALU.add))
                    link(nc.vector.reciprocal(inverse[:, :], inverse[:, :]))
                    nc.vector.tensor_tensor(bias_probs[:, 2 * b:2 * b + 2, h], bias_prob[:, s, :], inverse[:, :], ALU.mult)
                    for qt in range(2):
                        nc.vector.tensor_scalar(probs[:, s, qt, :], probs[:, s, qt, :], inverse[:, qt:qt + 1], None,
                                                ALU.mult).then_inc(normed, 1)
                if p + 1 < PAIRS:
                    for item in SHARES[u]:
                        low(job_of[p + 1, item], destination(p + 1, item), bias_of(p + 1, item))
                if g:
                    j, hh, b, h = unit(g - 1)
                    low(job_of["V", g - 1], both(attended[(g - 1) % 2], np.s_[:, :]), cols[:, 2, h:h + 1], Q)
            dve.wait_ge(sums_full, 1)
            for t in range(RT):
                nc.vector.tensor_tensor(keep["x"][:, t, :], sums[:, t, :], keep["x"][:, t, :], ALU.add)


def program(nc, io):
    with ExitStack() as ctx:
        def sb(name, shape, dt=F32):
            return ctx.enter_context(nc.sbuf_tensor(name, shape, dt))

        keep = {"x": sb("x_rows", [P, RT, D]), "sum": sb("sum_rows", [P, RT, D]), "ident": sb("ident", [P, P]),
                "bias_scores": sb("bias_scores", [P, RT, H]), "neg_bias_scores": sb("neg_bias_scores", [P, RT, H]),
                "bias_values": sb("bias_values", [H, D])}
        for name, n in (("ctxT", B * S), ("latT", ROWS)):
            keep[name] = sb(name + "_hi", [P, KT, n], F32R), sb(name + "_lo", [P, KT, n], F32R)
        keep["stored"] = ctx.enter_context(nc.semaphore("stored"))
        keep["hT"] = keep["latT"]

        transpose_context(nc, io, keep)
        narrow_attention(nc, io, keep, dict(
            name="L0a", nk=S + Q, queries=keep["latT"], keys=[keep["ctxT"], keep["latT"]], mask="mask_ik0", mask_dtype=I32,
            w="L0_w", bias="L0_bias", out_bias="L0_bo", gate="L2_gate", gated=False, scale=1.0 / DN, in_place=False))
        mlp(nc, io, keep, dict(name="L0m", rows="sum", lnp="L0_lnp", eps=1e-6, centred=False, w="L0_wm", b1="L0_b1", b2="L0_b2",
                               gelu=ACT.Gelu_apprx_tanh, out=None))
        for i in (1, 2):
            cfg = dict(name=f"L1a{i}", index=i)
            wide_prologue(nc, io, keep, cfg)
            wide_attention(nc, io, keep, cfg)
        mlp(nc, io, keep, dict(name="L1m", rows="x", lnp="L1_lnmp", eps=1e-5, centred=True, w="L1_wm", b1="L1_b1", b2="L1_b2",
                               gelu=ACT.Gelu, out=None))
        plain_rows(nc, keep)
        with Phase(nc, "L2") as ph:
            audT = ph.hilo("audT", [P, KT, B * S])
            normalised_rows(nc, io, keep, "L2c", "L2_lnp", audT, 1e-5, context=True)
            narrow_attention(nc, io, keep, dict(
                name="L2a", nk=S, queries=keep["hT"], keys=[audT], mask="mask_bf1", mask_dtype=U8,
                w="L2_w", bias="L2_bias", out_bias="L2_bo", gate="L2_gate", gated=True, scale=DN ** -0.5, in_place=True))
        normalised_rows(nc, io, keep, "L3q", "L3_ln1p", keep["hT"], 1e-5)
        narrow_attention(nc, io, keep, dict(
            name="L3a", nk=S, queries=keep["hT"], keys=[keep["ctxT"]], mask="mask_bf1", mask_dtype=U8,
            w="L3_w", bias="L3_bias", out_bias="L3_bo", gate="L2_gate", gated=False, scale=DN ** -0.5, in_place=True))
        mlp(nc, io, keep, dict(name="L3m", rows="x", lnp="L3_ln2p", eps=1e-5, centred=True, w="L3_wm", b1="L3_b1", b2="L3_b2",
                               gelu=ACT.Gelu_apprx_tanh, out="out"))


def plain_rows(nc, keep):
    with Phase(nc, "L2q") as ph:
        ring = ph.ring(ph.psum(4))
        block = ph.block()

        @block.tensor
        def _(pe):
            for kt in range(KT):
                for t in range(RT):
                    last = nc.tensor.transpose(ring.bank(kt)[:, t * P:(t + 1) * P], keep["x"][:, t, kt * P:(kt + 1) * P],
                                               keep["ident"][:, :])
                last.then_inc(ring.full, 1)

        @block.scalar
        def _(act):
            for kt in range(KT):
                act.wait_ge(ring.full, kt + 1)
                nc.scalar.copy(keep["hT"][0][:, kt, :], ring.bank(kt)[:, :]).then_inc(ring.hi_done, 1)

        @block.vector
        def _(dve):
            for kt in range(KT):
                dve.wait_ge(ring.hi_done, kt + 1)
                nc.vector.tensor_tensor(keep["hT"][1][:, kt, :], ring.bank(kt)[:, :], raw(keep["hT"][0][:, kt, :]), ALU.subtract)


def kernel(**inputs):
    import concourse.bacc as bacc
    from concourse.bass_utils import run_bass_kernel_spmd as run

    a = {name: np.asarray(value) for name, value in inputs.items()}

    def tiles(w):
        return w.reshape(-1, P, w.shape[1]).transpose(1, 0, 2)

    def columns(vector):
        return vector.reshape(-1, P).T

    def padded_heads(w):
        out = np.zeros((H, 32, w.shape[1]), w.dtype)
        out[:, 0:DN] = w.reshape(H, DN, -1)
        return out.reshape(H * 32, -1)

    def narrow(q, k, v, o):
        return np.concatenate([tiles(w).reshape(P, -1, 512) for w in (q, k, v, padded_heads(o))], axis=1)

    def narrow_bias(q, k, v):
        return np.concatenate([columns(q), columns(k), columns(padded_heads(v[:, None])[:, 0])], axis=1)

    def mlp_weights(w1, w2):
        return np.concatenate([tiles(w).reshape(P, -1, 512) for w in (w1, w2)], axis=1)

    zeros = np.zeros(D, np.float32)
    t = {"x": a["x"], "ctx_2048": a["ctx_2048"], "mask_ik0": a["mask_BxS2_ik0"].reshape(1, -1),
         "mask_bf1": a["mask_BxS2_bf1"].view(np.uint8).reshape(1, -1)}
    kv, kvb = (a[f"L0_xattn_kv_{n}"].reshape(-1, H, DN, 2) for n in "wb")
    key_value = [(kv[..., i].reshape(D, D), kvb[..., i].reshape(D)) for i in range(2)]
    t["L0_w"] = narrow(a["L0_xattn_q_w"], key_value[0][0], key_value[1][0], a["L0_xattn_out_w"])
    t["L0_bias"] = narrow_bias(a["L0_xattn_q_b"], key_value[0][1], key_value[1][1])
    t["L0_bo"] = a["L0_xattn_out_b"]
    t["L0_lnp"] = np.concatenate([columns(a["L0_xattn_postnorm_w"]), columns(zeros)], axis=1)
    t["L2_w"] = narrow(*(a[f"L2_xattn_W{n}"].T for n in "qkvo"))
    t["L2_bias"], t["L2_bo"], t["L2_gate"] = narrow_bias(zeros, zeros, zeros), zeros, a["L2_xattn_gate"]
    t["L2_lnp"] = np.concatenate([columns(a["L2_xattn_ln_gamma"]), columns(a["L2_xattn_ln_beta"])], axis=1)
    t["L3_w"] = narrow(*(a[f"L3_xattn_{n}_w"] for n in ("q", "k", "v", "cproj")))
    t["L3_bias"] = narrow_bias(*(a[f"L3_xattn_{n}_b"] for n in "qkv"))
    t["L3_bo"] = a["L3_xattn_cproj_b"]
    for n in (1, 2):
        t[f"L3_ln{n}p"] = np.concatenate([columns(a[f"L3_xattn_ln{n}_w"]), columns(a[f"L3_xattn_ln{n}_b"])], axis=1)
    for out, names in (("L0", ("mlp_w1", "mlp_b1", "mlp_w2", "mlp_b2")), ("L1", ("w_fc1", "b_fc1", "w_fc2", "b_fc2")),
                       ("L3", ("fc_w", "fc_b", "proj_w", "proj_b"))):
        w1, b1, w2, b2 = (a[f"{out}_xattn_{n}"] for n in names)
        t[f"{out}_wm"], t[f"{out}_b1"], t[f"{out}_b2"] = mlp_weights(w1, w2), columns(b1), b2
    for n in ("1", "2", "_mlp"):
        t[f"L1_ln{n.replace('_mlp', 'm')}p"] = np.concatenate(
            [columns(a[f"L1_xattn_ln{n}_scale"]), columns(a[f"L1_xattn_ln{n}_offset"])], axis=1)
    for n in (1, 2):
        wq, wk, wv, wo = (a[f"L1_xattn_w{m}{n}"] for m in "qkvo")
        by_pair = [tiles(w).reshape(P, KT, PAIRS, 2 * DW).transpose(2, 0, 1, 3).reshape(PAIRS, P, -1) for w in (wq, wk, wv)]
        by_pair.append(wo.reshape(PAIRS, 2, P, D).transpose(0, 2, 1, 3).reshape(PAIRS, P, -1))
        t[f"L1_w{n}"] = np.concatenate(by_pair, axis=2)
        t[f"L1_wq{n}"], t[f"L1_wo{n}"], t[f"L1_bias_k{n}"] = wq, wo, a[f"L1_xattn_bias_k{n}"].reshape(-1)
        t[f"L1_cols{n}"] = np.stack([columns(a[f"L1_xattn_{m}{n}"].reshape(-1)) for m in ("bq", "bias_k", "bv", "bias_v")], axis=1)
        t[f"L1_bk{n}"], t[f"L1_bo{n}"] = columns(a[f"L1_xattn_bk{n}"]), a[f"L1_xattn_bo{n}"]

    nc = bacc.Bacc("TRN2", target_bir_lowering=False, num_devices=1)
    arrays, io = {}, {}
    for name, value in t.items():
        arrays[f"in_{name}"] = np.ascontiguousarray(value)
        io[name] = nc.dram_tensor(f"in_{name}", value.shape, mybir.dt.from_np(value.dtype), kind="ExternalInput").ap()
    io["out"] = nc.dram_tensor("out_x", (B, Q, D), F32, kind="ExternalOutput").ap()
    program(nc, io)
    result = run(nc, [arrays], core_ids=[0])
    return result.results[0]["out_x"]
```

```python
from contextlib import ExitStack

import numpy as np

from concourse import mybir

F32 = mybir.dt.float32
F32R = mybir.dt.float32r
I32 = mybir.dt.int32
U8 = mybir.dt.uint8
ALU = mybir.AluOpType
ACT = mybir.ActivationFunctionType
AX = mybir.AxisListType

P = 128
B = 2
Q = 256
S = 512
D = 256
KT = D // P
ROWS = B * Q
RT = ROWS // P
CT = B * S // P
H = 16
DN = D // H
DW = 128
F = 1024
FT = F // P
PAIRS = H // 2
MASKED = -float(2 ** 100)


def padded(h):
    return 32 * (h // 4) + h % 4


def raw(ap):
    return ap.bitcast(F32)


class Ring:

    def __init__(self, banks, sem, name):
        self.banks = banks
        self.n = len(banks)
        self.full = sem(f"{name}_full")
        self.hi_done = sem(f"{name}_hi_done")
        self.free = [sem(f"{name}_free{i}") for i in range(self.n)]

    def bank(self, job):
        return self.banks[job % self.n]

    def wait_bank(self, pe, job):
        if job >= self.n:
            pe.wait_ge(self.free[job % self.n], job // self.n)

    def wait_evacuated(self, engine, job):
        engine.wait_ge(self.free[job % self.n], job // self.n + 1)

    def freed_by(self, job):
        return self.free[job % self.n]


def product3(nc, out, lhs, rhs, start, stop, loose=False):
    (lh, ll), (rh, rl) = lhs, rhs
    nc.tensor.matmul(out, lh, rh, start=start, stop=False, skip_group_check=loose)
    nc.tensor.matmul(out, lh, rl, start=False, stop=False, skip_group_check=loose)
    return nc.tensor.matmul(out, ll, rh, start=False, stop=stop, skip_group_check=loose)


def both(pair, index):
    return tuple(t[index] for t in pair)


def load_table(nc, keep, function):
    nc.scalar.activation(keep["nowhere"][:, :], keep["ident"][:, 0:1], function)


class Chain:

    def __init__(self, engine, done):
        self.engine, self.done, self.count = engine, done, 0

    def __call__(self, instruction):
        self.count += 1
        instruction.then_inc(self.done, 1)
        self.engine.wait_ge(self.done, self.count)


def row_statistics(nc, link, rows, tiles, stats, moments, shifted, eps, centred):
    for t in range(tiles):
        last = nc.vector.bn_stats(stats[:, t, :], rows[:, t, :])
        if t == tiles - 1:
            link(last)
    for t in range(tiles):
        last = nc.vector.bn_aggr(moments[:, t, :], stats[:, t, :])
        if t == tiles - 1:
            link(last)
    if not centred:
        link(nc.vector.tensor_tensor(shifted[:, 0:tiles], moments[:, 0:tiles, 0], moments[:, 0:tiles, 0], ALU.mult))
        link(nc.vector.tensor_tensor(shifted[:, 0:tiles], shifted[:, 0:tiles], moments[:, 0:tiles, 1], ALU.add))
        return nc.vector.tensor_scalar(shifted[:, 0:tiles], shifted[:, 0:tiles], eps, None, ALU.add)
    return nc.vector.tensor_scalar(shifted[:, 0:tiles], moments[:, 0:tiles, 1], eps, None, ALU.add)


class Phase:

    def __init__(self, nc, name):
        self.nc, self.name, self.ctx, self.sems = nc, name, ExitStack(), []

    def __enter__(self):
        self.ctx.__enter__()
        return self

    def __exit__(self, *error):
        self.ctx.__exit__(*error)
        if self.sems and not error[0]:
            self.nc.clear_and_free_semaphores(self.sems)
            self.nc.all_engine_barrier()

    def sb(self, name, shape, dt=F32):
        return self.ctx.enter_context(self.nc.sbuf_tensor(f"{self.name}_{name}", shape, dt))

    def hilo(self, name, shape):
        return self.sb(name + "_hi", shape, F32R), self.sb(name + "_lo", shape, F32R)

    def psum(self, n):
        return [self.ctx.enter_context(self.nc.psum_tensor(f"{self.name}_bank{i}", [P, 512], F32)) for i in range(n)]

    def sem(self, name):
        self.sems.append(self.nc.alloc_semaphore(f"{self.name}_{name}"))
        return self.sems[-1]

    def ring(self, banks):
        return Ring(banks, self.sem, "ring")

    def block(self):
        return self.ctx.enter_context(self.nc.Block())


def transpose_context(nc, io, keep):
    with Phase(nc, "prep") as ph:
        ctx_rows = ph.sb("ctx_rows", [P, CT, D])
        ring = ph.ring(ph.psum(4))
        loaded, cleared, ident_ready = ph.sem("loaded"), ph.sem("cleared"), ph.sem("ident_ready")
        block = ph.block()
        jobs = [(keep["ctxT"], ctx_rows, kt, 4 * g) for kt in range(KT) for g in range(CT // 4)]
        jobs += [(keep["latT"], keep["x"], kt, 0) for kt in range(KT)]

        @block.sync
        def _(sp):
            sp.dma_start(ctx_rows[:, :, :], io["ctx_2048"].rearrange("b (t p) d -> p (b t) d", p=P)).then_inc(loaded, 16)
            sp.dma_start(keep["x"][:, :, :], io["x"].rearrange("b (t p) d -> p (b t) d", p=P)).then_inc(loaded, 16)

        @block.gpsimd
        def _(pool):
            nc.gpsimd.memset(keep["ident"][:, :], 0.0).then_inc(cleared, 1)
            pool.wait_ge(cleared, 1)
            nc.gpsimd.affine_select(out=keep["ident"][:, :], in_=keep["ident"][:, :], compare_op=ALU.not_equal, fill=1.0,
                                    base=0, pattern=[[-1, P]], channel_multiplier=1).then_inc(ident_ready, 1)

        @block.tensor
        def _(pe):
            pe.wait_ge(loaded, 32)
            pe.wait_ge(ident_ready, 1)
            for job, (_, rows, kt, t0) in enumerate(jobs):
                ring.wait_bank(pe, job)
                for t in range(4):
                    last = nc.tensor.transpose(ring.bank(job)[:, t * P:(t + 1) * P],
                                               rows[:, t0 + t, kt * P:(kt + 1) * P], keep["ident"][:, :])
                last.then_inc(ring.full, 1)

        @block.scalar
        def _(act):
            for job, (to, _, kt, t0) in enumerate(jobs):
                act.wait_ge(ring.full, job + 1)
                nc.scalar.copy(to[0][:, kt, t0 * P:t0 * P + 512], ring.bank(job)[:, :]).then_inc(ring.hi_done, 1)

        @block.vector
        def _(dve):
            for job, (to, _, kt, t0) in enumerate(jobs):
                dve.wait_ge(ring.hi_done, job + 1)
                nc.vector.tensor_tensor(to[1][:, kt, t0 * P:t0 * P + 512], ring.bank(job)[:, :],
                                        raw(to[0][:, kt, t0 * P:t0 * P + 512]), ALU.subtract).then_inc(ring.freed_by(job), 1)


def narrow_attention(nc, io, keep, cfg):
    name, nk, queries, sources = cfg["name"], cfg["nk"], cfg["queries"], cfg["keys"]
    nkt = nk // P
    extra = nk - S
    quads = H // 4
    units = B * quads
    OCTETS = B * KT
    with Phase(nc, name) as ph:
        w_qkv = ph.sb("w_qkv", [P, 2, 3, 512], F32R)
        w_out = ph.sb("w_out", [P, 2, 2, 512], F32R)
        bias = ph.sb("bias", [P, 8])
        out_bias = ph.sb("out_bias", [P, D])
        gate = ph.sb("gate", [P, 1])
        q_parts = ph.sb("q_parts", [P, 2, KT, ROWS], F32R)
        qT = [q_parts[:, part, :, :] for part in range(2)]
        kT = ph.hilo("kT", [P, KT, B * nk])
        v = ph.sb("v", [P, B * nkt, H * 32])
        k_stack = [ph.sb("k_stack", [P, 4, nk], F32R),
                   w_qkv[:, :, :, :].rearrange("p s i n -> p (s i n)")[:, 0:4 * nk].rearrange("p (t n) -> p t n", t=4)]
        q_stack = [ph.sb(f"q_stack{i}", [P, 8, Q], F32R) for i in range(2)]
        score_slots, probs_slots, small_slots = (4, 8, 8) if nk == S else (2, 6, 8)
        probs = ph.sb("probs", [P, probs_slots, nk])
        spoiled = ph.sb("spoiled", [P, 2])
        TSLOTS = 5
        probsT = ph.sb("probsT", [P, TSLOTS, 2 * nkt * P])
        flat = probsT[:, :, :].rearrange("p s n -> p (s n)")
        stage = flat[:, 0:5 * 512].rearrange("p (i n) -> p i n", i=5)
        if cfg["bias_values"]:
            wide_wo = [t[:, at:at + H * D].rearrange("p (h n) -> p h n", h=H)
                       for t, at in ((probs[:, :, :].rearrange("p s n -> p (s n)"), 0), (flat, 5 * 512 + B * S))]
            wide_cols = ph.sb("wide_cols", [P, 2, 4, H])
            spread = ph.sb("spread", [P, 2, H, 32])
            wide_loaded, spread_clear, spread_ready = ph.sem("wide_loaded"), ph.sem("spread_clear"), ph.sem("spread_ready")
        mask_raw = flat[0:1, 5 * 512:5 * 512 + B * S].bitcast(cfg["mask_dtype"])[:, 0:B * S]
        neg_max, row_sum, inverse = (ph.sb(n, [P, small_slots]) for n in ("neg_max", "row_sum", "inverse"))
        attended = [ph.sb("attended_hi", [P, quads, ROWS], F32R), q_parts[:, :, :, :].rearrange("p s k n -> p (s k) n")]
        mask_row = attended[0][0:1, :, :].rearrange("o k n -> o (k n)")[:, 0:B * nk].rearrange("o (b n) -> o b n", b=B)
        slot_width = -(-nk // 512) * 512
        score_banks = score_slots * slot_width // 512
        banks = ph.psum(8 - score_banks)
        scores = ph.ctx.enter_context(nc.psum_tensor(f"{name}_scores", [P, score_slots, slot_width], F32))
        ring = ph.ring(banks)
        q_dram = nc.dram_tensor(f"{name}_q_dram", [2, D, ROWS], F32).ap()
        k_dram = nc.dram_tensor(f"{name}_k_dram", [2, D, B * nk], F32).ap()
        mask_dram = nc.dram_tensor(f"{name}_mask_dram", [1, B, nk], F32).ap()
        written = [ph.sem(f"written{o}") for o in range(OCTETS)]
        loaded, small_loaded = [ph.sem(f"loaded{i}") for i in range(5)], ph.sem("small_loaded")
        w_hi, w_lo = ph.sem("w_hi"), ph.sem("w_lo")
        zeroed, padding_set, mask_ready, gate_ready = ph.sem("zeroed"), ph.sem("padding_set"), ph.sem("mask_ready"), ph.sem("gate_ready")
        cleared = [ph.sem(f"cleared{i}") for i in range(2)]
        stack_loaded = [ph.sem(f"stack_loaded{i}") for i in range(2)]
        scores_full, max_done, exp_done = ph.sem("scores_full"), ph.sem("max_done"), ph.sem("exp_done")
        inverse_done, normed, dve_done, bias_ready = ph.sem("inverse_done"), ph.sem("normed"), ph.sem("dve_done"), ph.sem("bias_ready")
        block = ph.block()

        WEIGHTS = (1, 0, 2, 3, 4)
        w = [[w_qkv[:, part, i, :] if i < 3 else w_out[:, part, i - 3, :] for i in range(5)] for part in range(2)]
        wq, wk, wv = ([w[part][i].rearrange("p (k n) -> p k n", k=KT) for part in range(2)] for i in range(3))
        wo = [w_out[:, part, :, :].rearrange("p s (g n) -> p (s g) n", g=2) for part in range(2)]

        key_jobs = {(mt, b): [("k", mt, b, c0, n) for c0, n in ([(0, S)] + ([(S, extra)] if extra else []))]
                    for mt in range(KT) for b in range(B)}
        front = ["rows"] * (KT if cfg["rows"] else 0) + key_jobs[0, 0] + [("q", 0)] + key_jobs[1, 0] + [("q", 1)] + \
                key_jobs[0, 1] + key_jobs[1, 1]
        parts = NormParts(ph, cfg["lnp"]) if cfg["rows"] else None
        v_jobs = [(b, 2 * i) for b in range(B) for i in range(nkt // 2)]
        v0 = len(front)
        m0 = v0 + len(v_jobs)
        u0 = m0 + (1 if cfg["bias_values"] else 0)
        tj = 2 * nkt // 4
        HEADS = units * 4

        def key_source(part, kt, b, c0, n):
            src, per = (sources[0], S) if c0 < S else (sources[1], extra)
            at = b * per + (c0 if c0 < S else c0 - S)
            return src[part][:, kt, at:at + n]

        LAG = 3 if nk == S else 2

        def product_before(t):
            return t // 4 - 1 if t % 4 == 1 and t >= 4 else None

        order = []
        for t in range(HEADS):
            if product_before(t) is not None:
                order.append(("V", product_before(t), 0))
            order += [("T", t, c) for c in range(tj)]
        order.append(("V", units - 1, 0))

        def slot_scores(m):
            return scores[:, m % score_slots, 0:nk]

        job_of = {what: u0 + i for i, what in enumerate(order)}
        o0 = u0 + len(order)
        by_act = lambda g, c: c % 2 == 0
        unit_copies = lambda unit: [job_of["T", 4 * unit + j, c] for j in range(4) for c in range(tj)]

        @block.sync
        def _(sp):
            for i in WEIGHTS:
                sp.dma_start(stage[:, i, :], io[cfg["w"]][:, i, :]).then_inc(loaded[i], 16)
                if i == WEIGHTS[0]:
                    if parts:
                        parts.load(sp, io)
                    sp.dma_start(bias[:, :], io[cfg["bias"]]).then_inc(small_loaded, 16)
                    sp.dma_start(mask_raw[:, :], io[cfg["mask"]]).then_inc(small_loaded, 16)
                    sp.dma_start(gate[:, :], io[cfg["gate"]].partition_broadcast(P)).then_inc(small_loaded, 16)
                    sp.dma_start(out_bias[:, :], io[cfg["out_bias"]].partition_broadcast(P)).then_inc(small_loaded, 16)
            if cfg["bias_values"]:
                for i in range(2):
                    sp.dma_start(wide_cols[:, i, :, :], io[f"L1_cols{i + 1}"]).then_inc(wide_loaded, 16)
                    sp.dma_start(wide_wo[i], io[f"L1_wo{i + 1}"].rearrange("(h p) n -> p h n", p=P)).then_inc(wide_loaded, 16)
            def write(o):
                b, kt = divmod(o, KT)
                ring.wait_evacuated(sp, max(front.index(("q", kt)), front.index(key_jobs[kt, b][-1])))
                rows = slice(kt * P, (kt + 1) * P)
                for part in range(2):
                    for of, at, n, to in ((qT[part][:, kt, :], b * Q, Q, q_dram), (kT[part][:, kt, :], b * nk, nk, k_dram)):
                        sp.dma_start(to[part, rows, at:at + n], raw(of[:, at:at + n])).then_inc(written[o], 16)
                if o == 0:
                    sp.wait_ge(mask_ready, 1)
                    sp.dma_start(mask_dram, raw(mask_row[:, :, :])).then_inc(written[o], 16)

            for o in range(OCTETS):
                b, kt, r = o // KT, o % KT, o % 2
                if o == 0:
                    write(o)
                if o == 1:
                    for other in range(1, OCTETS):
                        write(other)
                sp.wait_ge(written[o], 64 if o else 80)
                sp.wait_ge(cleared[r], 3)
                if o >= 2:
                    sp.wait_ge(scores_full, 16 * (o - 1))
                for a in range(2):
                    for c, (kp, qp) in enumerate(((0, 0), (0, 1), (1, 0))):
                        row = 64 * a + 16 * c
                        for to, of, at, n in ((k_stack[r][row:row + 16, :, :], k_dram[kp], b * nk, nk),
                                              (q_stack[r][row:row + 16, a:8:2, :], q_dram[qp], b * Q, Q)):
                            heads = of[kt * P:(kt + 1) * P, at:at + n].rearrange("(t a r) n -> a r t n", a=2, r=DN)[a]
                            sp.dma_start(raw(to), heads).then_inc(stack_loaded[r], 16)
                    row = 64 * a + 48
                    sp.dma_start(raw(k_stack[r][row:row + 1, :, :]),
                                 mask_dram[0:1, b:b + 1, :].broadcast_to([1, 4, nk])).then_inc(stack_loaded[r], 16)
        stack_dmas = 14

        @block.gpsimd
        def _(pool):
            if parts and not parts.plain:
                parts.root(nc, pool)
                pool.wait_ge(parts.rstd_ready, 1)
            nc.gpsimd.memset(raw(mask_row[:, :, :]), 0.0).then_inc(padding_set, 1)
            for r in range(2):
                if r:
                    nc.gpsimd.memset(v[:, :, :], 0.0).then_inc(padding_set, 1)
                    if cfg["bias_values"]:
                        nc.gpsimd.memset(spread[:, :, :, :], 0.0).then_inc(spread_clear, 1)
                nc.gpsimd.memset(raw(q_stack[r][:, :, :]), 0.0).then_inc(zeroed, 1)
                pool.wait_ge(zeroed, r + 1)
                for a in range(2):
                    nc.gpsimd.memset(raw(q_stack[r][64 * a + 32:64 * a + 64, a:8:2, :]), 1.0).then_inc(cleared[r], 1)
                pool.wait_ge(cleared[r], 2)
                if r:
                    pool.wait_ge(ring.full, u0)
                nc.gpsimd.memset(raw(k_stack[r][:, :, :]), 0.0).then_inc(cleared[r], 1)
            for m in range(2 * HEADS):
                slot, small = m % probs_slots, m % small_slots
                pool.wait_ge(inverse_done, m // 2 + 1)
                nc.gpsimd.tensor_scalar(probs[:, slot, :], probs[:, slot, :], inverse[:, small:small + 1], 1.0,
                                        ALU.mult, ALU.mult).then_inc(normed, 1)

        @block.tensor
        def _(pe):
            for job, item in enumerate(front):
                if item == "rows":
                    if job == parts.first:
                        parts.transpose(nc, pe, ring, keep)
                    continue
                ring.wait_bank(pe, job)
                kind, mt = item[0:2]
                pe.wait_ge(w_lo, 2 if kind == "q" else 1)
                if kind == "q" and parts:
                    for back in range(KT):
                        ring.wait_evacuated(pe, parts.first + back)
                for kt in range(KT):
                    if kind == "q":
                        out, moving, weight = ring.bank(job)[:, :], [t[:, kt, :] for t in queries], wq
                    else:
                        b, c0, n = item[2:]
                        out, moving, weight = ring.bank(job)[:, 0:n], [key_source(part, kt, b, c0, n) for part in range(2)], wk
                    last = product3(nc, out, [t[:, kt, mt * P:(mt + 1) * P] for t in weight], moving, kt == 0, kt == KT - 1)
                last.then_inc(ring.full, 1)
            for i, (b, t0) in enumerate(v_jobs):
                job = v0 + i
                pe.wait_ge(w_lo, 3)
                ring.wait_bank(pe, job)
                for t in range(2):
                    for kt in range(KT):
                        last = product3(nc, ring.bank(job)[:, t * D:(t + 1) * D],
                                        [key_source(part, kt, b, (t0 + t) * P, P) for part in range(2)],
                                        [t_[:, kt, :] for t_ in wv], kt == 0, kt == KT - 1)
                last.then_inc(ring.full, 1)

            if cfg["bias_values"]:
                pe.wait_ge(spread_ready, 1)
                ring.wait_bank(pe, m0)
                for i in range(2):
                    for c in range(4):
                        for j in range(4):
                            h = 4 * j + c
                            last = nc.tensor.matmul(ring.bank(m0)[32 * j:32 * j + 32, i * D:(i + 1) * D], spread[:, i, h, :],
                                                    wide_wo[i][:, h, :], start=c == 0, stop=c == 3)
                last.then_inc(ring.full, 1)

            def transpose_head(g):
                pe.wait_ge(normed, 2 * g + 2)
                for c in range(tj):
                    job = job_of["T", g, c]
                    ring.wait_bank(pe, job)
                    for i in range(4):
                        qt, kt = divmod(4 * c + i, nkt)
                        last = nc.tensor.transpose(ring.bank(job)[:, i * P:(i + 1) * P],
                                                   probs[:, (2 * g + qt) % probs_slots, kt * P:(kt + 1) * P], keep["ident"][:, :])
                    last.then_inc(ring.full, 1)

            def product_v(unit):
                job = job_of["V", unit, 0]
                ring.wait_bank(pe, job)
                b, quad = divmod(unit, quads)
                for back in range(ring.n):
                    ring.wait_evacuated(pe, unit_copies(unit)[-1 - back])
                for kt in range(nkt):
                    for j in range(4):
                        g = 4 * unit + j
                        moving = probsT[:, g % TSLOTS, :].rearrange("p (t k n) -> p t k n", t=2, k=nkt)[:, :, kt, :]
                        last = nc.tensor.matmul(ring.bank(job)[32 * j:32 * j + 32, 0:Q],
                                                v[:, b * nkt + kt, 32 * (4 * quad + j):32 * (4 * quad + j) + 32],
                                                moving, start=kt == 0, stop=kt == nkt - 1)
                last.then_inc(ring.full, 1)

            for g in range(HEADS + LAG):
                t = g - LAG
                if g < HEADS:
                    octet, e = divmod(g, 8)
                    r = octet % 2
                    if e == 0:
                        pe.wait_ge(stack_loaded[r], 16 * stack_dmas * (octet // 2 + 1))
                    for qt in range(2):
                        m = 2 * g + qt
                        if m >= score_slots:
                            pe.wait_ge(exp_done, m - score_slots + 1)
                        for c0, n in [(0, S)] + ([(S, extra)] if extra else []):
                            last = nc.tensor.matmul(slot_scores(m)[:, c0:c0 + n], q_stack[r][:, e, qt * P:(qt + 1) * P],
                                                    k_stack[r][:, e // 2, c0:c0 + n], start=True, stop=True)
                        last.then_inc(scores_full, 1)
                if t >= 0:
                    if product_before(t) is not None:
                        product_v(product_before(t))
                    transpose_head(t)
            product_v(units - 1)

            ring.wait_evacuated(pe, job_of["V", units - 1, 0])
            pe.wait_ge(w_lo, 5)
            for t in range(RT):
                job = o0 + t
                ring.wait_bank(pe, job)
                for quad in range(quads):
                    last = product3(nc, ring.bank(job)[:, 0:D], [x[:, quad, t * P:(t + 1) * P] for x in attended],
                                    [x[:, quad, :] for x in wo], quad == 0, quad == quads - 1)
                last.then_inc(ring.full, 1)

        def projected(item):
            if item[0] == "q":
                return [t[:, item[1], :] for t in qT], ROWS, item[1]
            kind, mt, b, c0, n = item
            return [t[:, mt, b * nk + c0:b * nk + c0 + n] for t in kT], n, 2 + mt

        @block.scalar
        def _(act):
            load_table(nc, keep, ACT.Exp)
            if parts and parts.plain:
                parts.scale(nc, act, ring)
            for n, i in enumerate(WEIGHTS):
                if parts and not parts.plain and n == 2:
                    parts.scale(nc, act, ring)
                act.wait_ge(loaded[i], 16)
                nc.scalar.mul(w[0][i], stage[:, i, :], 1.0 if i else cfg["scale"]).then_inc(w_hi, 1)
            act.wait_ge(small_loaded, 64)
            if cfg["gated"]:
                nc.scalar.activation(gate[:, :], gate[:, :], ACT.Tanh).then_inc(gate_ready, 1)
            act.wait_ge(bias_ready, 1)
            for job, item in enumerate(front):
                if item == "rows":
                    continue
                out, n, column = projected(item)
                act.wait_ge(ring.full, job + 1)
                nc.scalar.activation(out[0], ring.bank(job)[:, 0:n], ACT.Identity,
                                     bias=bias[:, column:column + 1]).then_inc(ring.hi_done, 1)
            act.wait_ge(padding_set, 2)
            for i, (b, t0) in enumerate(v_jobs):
                job = v0 + i
                act.wait_ge(ring.full, job + 1)
                for t in range(2):
                    last = nc.scalar.copy(v[:, b * nkt + t0 + t, :].rearrange("p (h d) -> p h d", h=H)[:, :, 0:DN],
                                          ring.bank(job)[:, t * D:(t + 1) * D].rearrange("p (h d) -> p h d", h=H))
                last.then_inc(ring.freed_by(job), 1)
            if cfg["bias_values"]:
                act.wait_ge(ring.full, m0 + 1)
                nc.scalar.copy(keep["bias_values"][:, :, :].rearrange("h i n -> h (i n)"),
                               ring.bank(m0)[:, :]).then_inc(ring.freed_by(m0), 1)

            def evacuate(t):
                if product_before(t) is not None:
                    high_v(product_before(t))
                for c in range(tj):
                    if by_act(t, c):
                        job = job_of["T", t, c]
                        act.wait_ge(ring.full, job + 1)
                        nc.scalar.copy(probsT[:, t % TSLOTS, c * 512:(c + 1) * 512],
                                       ring.bank(job)[:, :]).then_inc(ring.freed_by(job), 1)

            def high_v(unit):
                if unit == 0:
                    act.wait_ge(written[0], 80)
                job = job_of["V", unit, 0]
                b, quad = divmod(unit, quads)
                act.wait_ge(ring.full, job + 1)
                nc.scalar.activation(attended[0][:, quad, b * Q:(b + 1) * Q], ring.bank(job)[:, 0:Q], ACT.Identity,
                                     bias=bias[:, 4 + quad:5 + quad]).then_inc(ring.hi_done, 1)

            for g in range(HEADS + LAG):
                if g < HEADS:
                    for m in (2 * g, 2 * g + 1):
                        small = m % small_slots
                        act.wait_ge(max_done, m + 1)
                        if m >= probs_slots:
                            act.wait_ge(ring.full, job_of["T", (m - probs_slots) // 2, tj - 1] + 1)
                        nc.scalar.activation(probs[:, m % probs_slots, :], slot_scores(m), ACT.Exp,
                                             bias=neg_max[:, small:small + 1],
                                             accum_out=row_sum[:, small:small + 1]).then_inc(exp_done, 1)
                if g >= LAG:
                    evacuate(g - LAG)
            high_v(units - 1)

        @block.vector
        def _(dve):
            link = Chain(dve, dve_done)
            if parts:
                norm_link = Chain(dve, parts.dve_done)
                parts.normalise(nc, dve, norm_link, keep["x"], 1e-5, True)
                if parts.plain:
                    parts.split(nc, dve, norm_link, ring, queries)
            for n, i in enumerate(WEIGHTS):
                dve.wait_ge(w_hi, n + 1)
                nc.vector.scalar_tensor_tensor(w[1][i], stage[:, i, :], 1.0 if i else cfg["scale"], raw(w[0][i]),
                                               ALU.mult, ALU.subtract).then_inc(w_lo, 1)
                if n == 1 and parts and not parts.plain:
                    parts.split(nc, dve, norm_link, ring, queries)
            dve.wait_ge(small_loaded, 64)
            dve.wait_ge(padding_set, 1)
            nc.vector.tensor_scalar(bias[:, 0:2], bias[:, 0:2], cfg["scale"], None, ALU.mult).then_inc(bias_ready, 1)
            nc.vector.tensor_scalar(mask_row[0:1, :, 0:S], mask_raw[0:1, :].rearrange("o (b s) -> o b s", b=B), 0.0, MASKED,
                                    ALU.is_equal, ALU.mult).then_inc(mask_ready, 1)
            dve.wait_ge(bias_ready, 1)

            def low(job, nth, out, col, n):
                dve.wait_ge(ring.hi_done, nth + 1)
                nc.vector.scalar_tensor_tensor(out[1], ring.bank(job)[:, 0:n], bias[:, col:col + 1], raw(out[0]),
                                               ALU.add, ALU.subtract).then_inc(ring.freed_by(job), 1)

            for job, item in enumerate(front):
                if item == "rows":
                    continue
                out, n, column = projected(item)
                low(job, job, out, column, n)
            if cfg["bias_values"]:
                dve.wait_ge(wide_loaded, 64)
                dve.wait_ge(spread_clear, 1)
                for i in range(2):
                    for c in range(4):
                        last = nc.vector.tensor_tensor(spread[:, i, c:H:4, c], wide_cols[:, i, 3, c:H:4],
                                                       wide_cols[:, i, 2, c:H:4], ALU.subtract)
                last.then_inc(spread_ready, 1)

            def low_v(unit):
                if unit == 0:
                    for o in range(OCTETS):
                        dve.wait_ge(written[o], 64 if o else 80)
                b, quad = divmod(unit, quads)
                low(job_of["V", unit, 0], v0 + unit, [t[:, quad, b * Q:(b + 1) * Q] for t in attended], 4 + quad, Q)

            for g in range(HEADS + LAG):
                t = g - LAG
                if g < HEADS:
                    for m in (2 * g, 2 * g + 1):
                        small = m % small_slots
                        dve.wait_ge(scores_full, m + 1)
                        nc.vector.tensor_reduce(neg_max[:, small:small + 1], slot_scores(m), AX.X, ALU.max,
                                                negate=True).then_inc(max_done, 1)
                if 1 <= g <= HEADS:
                    dve.wait_ge(exp_done, 2 * g)
                    small = (2 * g - 2) % small_slots
                    if 2 * g - 2 >= small_slots:
                        dve.wait_ge(normed, 2 * g - small_slots)
                    sums = row_sum[:, small:small + 2]
                    if cfg["nan_if_masked"] and (g - 1) % H == 0:
                        link(nc.vector.tensor_scalar(spoiled[:, :], neg_max[:, small:small + 2], -MASKED, 0.0, ALU.mult, ALU.mult))
                        link(nc.vector.tensor_tensor(spoiled[:, :], spoiled[:, :], sums, ALU.add))
                        sums = spoiled[:, :]
                    nc.vector.reciprocal(inverse[:, small:small + 2], sums).then_inc(inverse_done, 1)
                if t >= 0:
                    if product_before(t) is not None:
                        low_v(product_before(t))
                    for c in range(tj):
                        if not by_act(t, c):
                            job = job_of["T", t, c]
                            dve.wait_ge(ring.full, job + 1)
                            nc.vector.tensor_copy(probsT[:, t % TSLOTS, c * 512:(c + 1) * 512],
                                                  ring.bank(job)[:, :]).then_inc(ring.freed_by(job), 1)
            low_v(units - 1)

            if cfg["gated"]:
                dve.wait_ge(gate_ready, 1)
            for t in range(RT):
                last = nc.vector.tensor_tensor(keep["x"][:, t, :] if cfg["in_place"] else keep["sum"][:, t, :],
                                               keep["x"][:, t, :], out_bias[:, :], ALU.add)
            link(last)
            for t in range(RT):
                job = o0 + t
                rows = (keep["x"] if cfg["in_place"] else keep["sum"])[:, t, :]
                dve.wait_ge(ring.full, job + 1)
                nc.vector.scalar_tensor_tensor(rows, ring.bank(job)[:, 0:D], gate[:, 0:1] if cfg["gated"] else 1.0, rows,
                                               ALU.mult, ALU.add).then_inc(ring.freed_by(job), 1)


class NormParts:

    def __init__(self, ph, lnp, tiles=RT, first=0, tag=""):
        self.lnp, self.tiles, self.first = lnp, tiles, first
        self.jobs = [(kt, 4 * g) for kt in range(KT) for g in range(tiles // 4)]
        self.plain = lnp is None
        if self.plain:
            self.whole = ph.sb(tag + "whole", [P, KT, tiles * P])
            self.dve_done = ph.sem(tag + "norm_step")
            return
        self.normed = ph.sb(tag + "normed", [P, tiles, D])
        self.whole = ph.sb(tag + "whole", [P, KT, tiles * P])
        self.stats, self.moments = ph.sb(tag + "stats", [P, tiles, 6]), ph.sb(tag + "moments", [P, tiles, 2])
        self.shifted, self.power, self.rstd = ph.sb(tag + "shifted", [P, tiles]), ph.sb(tag + "power", [P, tiles]), ph.sb(tag + "rstd", [P, tiles])
        self.scale_shift = ph.sb(tag + "scale_shift", [P, 4])
        self.cols_loaded, self.power_set = ph.sem(tag + "cols_loaded"), ph.sem(tag + "power_set")
        self.shifted_ready, self.rstd_ready, self.normed_ready = ph.sem(tag + "shifted_ready"), ph.sem(tag + "rstd_ready"), ph.sem(tag + "normed_ready")
        self.dve_done = ph.sem(tag + "norm_step")

    def load(self, sp, io):
        if self.plain:
            return
        sp.dma_start(self.scale_shift[:, :], io[self.lnp]).then_inc(self.cols_loaded, 16)

    def root(self, nc, pool):
        if self.plain:
            return
        nc.gpsimd.memset(self.power[:, :], -0.5).then_inc(self.power_set, 1)
        pool.wait_ge(self.power_set, 1)
        pool.wait_ge(self.shifted_ready, 1)
        nc.gpsimd.tensor_tensor(self.rstd[:, :], self.shifted[:, :], self.power[:, :], ALU.pow).then_inc(self.rstd_ready, 1)

    def statistics(self, nc, link, rows, eps, centred):
        if self.plain:
            return
        row_statistics(nc, link, rows, self.tiles, self.stats, self.moments, self.shifted, eps,
                       centred).then_inc(self.shifted_ready, 1)

    def apply(self, nc, dve, rows, centred):
        if self.plain:
            return
        dve.wait_ge(self.rstd_ready, 1)
        for t in range(self.tiles):
            mean = self.moments[:, t, 0:1] if centred else 0.0
            last = nc.vector.tensor_scalar(self.normed[:, t, :], rows[:, t, :], mean, self.rstd[:, t:t + 1],
                                           ALU.subtract, ALU.mult)
        last.then_inc(self.normed_ready, 1)

    def normalise(self, nc, dve, link, rows, eps, centred):
        self.statistics(nc, link, rows, eps, centred)
        self.apply(nc, dve, rows, centred)

    def transpose(self, nc, pe, ring, keep):
        if not self.plain:
            pe.wait_ge(self.normed_ready, 1)
        rows = keep["x"] if self.plain else self.normed
        for job, (kt, t0) in enumerate(self.jobs, self.first):
            ring.wait_bank(pe, job)
            for t in range(4):
                last = nc.tensor.transpose(ring.bank(job)[:, t * P:(t + 1) * P],
                                           rows[:, t0 + t, kt * P:(kt + 1) * P], keep["ident"][:, :])
            last.then_inc(ring.full, 1)

    def scale(self, nc, act, ring):
        if not self.plain:
            act.wait_ge(self.cols_loaded, 16)
        for job, (kt, t0) in enumerate(self.jobs, self.first):
            act.wait_ge(ring.full, job + 1)
            if self.plain:
                nc.scalar.copy(self.whole[:, kt, t0 * P:t0 * P + 512], ring.bank(job)[:, :]).then_inc(ring.hi_done, 1)
                continue
            nc.scalar.activation(self.whole[:, kt, t0 * P:t0 * P + 512], ring.bank(job)[:, :], ACT.Identity,
                                 bias=self.scale_shift[:, 2 + kt:3 + kt],
                                 scale=self.scale_shift[:, kt:kt + 1]).then_inc(ring.hi_done, 1)

    def split(self, nc, dve, link, ring, out):
        for job, (kt, t0) in enumerate(self.jobs, self.first):
            hi, lo, whole = (t[:, kt, t0 * P:t0 * P + 512] for t in (*out, self.whole))
            dve.wait_ge(ring.hi_done, job + 1)
            link(nc.vector.tensor_copy(hi, whole))
            nc.vector.tensor_tensor(lo, whole, raw(hi), ALU.subtract).then_inc(ring.freed_by(job), 1)


def mlp(nc, io, keep, cfg):
    with Phase(nc, cfg["name"]) as ph:
        parts = NormParts(ph, cfg["lnp"])
        stage = ph.sb("stage", [P, 8, 512])
        w = ph.hilo("w", [P, 8, 512])
        b1 = ph.sb("b1", [P, FT])
        b2 = ph.sb("b2", [P, D])
        hT = ph.hilo("hT", [P, KT, ROWS])
        activated = ph.sb("activated", [P, 4, ROWS])
        hidden = ph.hilo("hidden", [P, FT, ROWS])
        fold = BiasKeyFold(ph) if cfg["fold"] else None
        if cfg["context"]:
            context = NormParts(ph, cfg["context_lnp"], CT, first=KT + FT, tag="context_")
            context_rows, context_loaded = ph.sb("context_rows", [P, CT, D]), ph.sem("context_loaded")
        ring = ph.ring(ph.psum(4))
        loaded = [ph.sem(f"loaded{i}") for i in range(4)]
        small_loaded, w_hi, w_lo = ph.sem("small_loaded"), ph.sem("w_hi"), ph.sem("w_lo")
        stored = keep["stored"]
        block = ph.block()
        w1 = [t[:, 0:4, :].rearrange("p (k s) n -> p k (s n)", k=KT) for t in w]
        w2 = [t[:, 4:8, :].rearrange("p s (g n) -> p (s g) n", g=2) for t in w]
        rows = keep[cfg["rows"]]
        up0 = KT
        down0 = up0 + FT + (len(context.jobs) if cfg["context"] else 0)

        @block.sync
        def _(sp):
            parts.load(sp, io)
            for i in range(4):
                sp.dma_start(stage[:, 2 * i:2 * i + 2, :], io[cfg["w"]][:, 2 * i:2 * i + 2, :]).then_inc(loaded[i], 16)
            sp.dma_start(b1[:, :], io[cfg["b1"]]).then_inc(small_loaded, 16)
            sp.dma_start(b2[:, :], io[cfg["b2"]].partition_broadcast(P)).then_inc(small_loaded, 16)
            if fold:
                fold.load(sp, io)
            if cfg["context"]:
                context.load(sp, io)
                sp.dma_start(context_rows[:, :, :], io["ctx_2048"].rearrange("b (t p) d -> p (b t) d", p=P)).then_inc(context_loaded, 16)
            if cfg["out"] is not None:
                for t in range(RT):
                    ring.wait_evacuated(sp, down0 + t)
                    sp.dma_start(io["out"].rearrange("b (t p) d -> p (b t) d", p=P)[:, t, :], keep["x"][:, t, :]).then_inc(stored, 16)
                sp.wait_ge(stored, 16 * RT)

        @block.gpsimd
        def _(pool):
            parts.root(nc, pool)
            if fold:
                fold.multiply(nc, pool, nc.gpsimd, fold.pieces[:3])
            if cfg["context"]:
                context.root(nc, pool)

        @block.tensor
        def _(pe):
            parts.transpose(nc, pe, ring, keep)
            for m in range(FT):
                job = up0 + m
                if m == 0:
                    ring.wait_evacuated(pe, 0)
                    ring.wait_evacuated(pe, 1)
                pe.wait_ge(w_lo, 4)
                ring.wait_bank(pe, job)
                for kt in range(KT):
                    last = product3(nc, ring.bank(job)[:, :], [t[:, kt, m * P:(m + 1) * P] for t in w1],
                                    [t[:, kt, :] for t in hT], kt == 0, kt == KT - 1)
                last.then_inc(ring.full, 1)
            if cfg["context"]:
                context.transpose(nc, pe, ring, keep)
            pe.wait_ge(w_lo, 8)
            for t in range(RT):
                job = down0 + t
                ring.wait_bank(pe, job)
                for f in range(FT):
                    if t == 0:
                        ring.wait_evacuated(pe, up0 + f)
                    last = product3(nc, ring.bank(job)[:, 0:D], [x[:, f, t * P:(t + 1) * P] for x in hidden],
                                    [x[:, f, :] for x in w2], f == 0, f == FT - 1)
                last.then_inc(ring.full, 1)

        @block.scalar
        def _(act):
            load_table(nc, keep, cfg["gelu"])
            for i in range(8):
                act.wait_ge(loaded[i // 2], 16)
                nc.scalar.copy(w[0][:, i, :], stage[:, i, :]).then_inc(w_hi, 1)
                if i == 3:
                    parts.scale(nc, act, ring)
            act.wait_ge(small_loaded, 32)
            for m in range(FT):
                job = up0 + m
                act.wait_ge(ring.full, job + 1)
                if m >= 4:
                    ring.wait_evacuated(act, job - 4)
                nc.scalar.activation(activated[:, m % 4, :], ring.bank(job)[:, :], cfg["gelu"],
                                     bias=b1[:, m:m + 1]).then_inc(ring.hi_done, 1)
            if cfg["context"]:
                context.scale(nc, act, ring)

        @block.vector
        def _(dve):
            link = Chain(dve, parts.dve_done)
            parts.normalise(nc, dve, link, rows, cfg["eps"], cfg["centred"])
            for i in range(8):
                dve.wait_ge(w_hi, i + 1)
                nc.vector.tensor_tensor(w[1][:, i, :], stage[:, i, :], raw(w[0][:, i, :]), ALU.subtract).then_inc(w_lo, 1)
                if i == 3:
                    parts.split(nc, dve, link, ring, hT)
            dve.wait_ge(small_loaded, 32)
            for t in range(RT):
                last = nc.vector.tensor_tensor(keep["x"][:, t, :], keep["x"][:, t, :], b2[:, :], ALU.add)
            link(last)
            for m in range(FT):
                job = up0 + m
                dve.wait_ge(ring.hi_done, up0 + m + 1)
                link(nc.vector.tensor_copy(hidden[0][:, m, :], activated[:, m % 4, :]))
                nc.vector.tensor_tensor(hidden[1][:, m, :], activated[:, m % 4, :], raw(hidden[0][:, m, :]),
                                        ALU.subtract).then_inc(ring.freed_by(job), 1)
                if cfg["context"] and m == 0:
                    context_link = Chain(dve, context.dve_done)
                    dve.wait_ge(context_loaded, 16)
                    context.statistics(nc, context_link, context_rows, 1e-5, True)
                if fold and m >= FT - 2:
                    fold.reduce(nc, dve, keep, *fold.pieces[m - FT + 2])
                if cfg["context"] and m == 3:
                    context.apply(nc, dve, context_rows, True)
            if cfg["context"]:
                context.split(nc, dve, context_link, ring, cfg["context"])
            if fold:
                fold.multiply(nc, dve, nc.vector, fold.pieces[3:])
            for t in range(RT):
                if fold and t < 2:
                    fold.reduce(nc, dve, keep, *fold.pieces[3 - t])
                job = down0 + t
                dve.wait_ge(ring.full, job + 1)
                nc.vector.tensor_tensor(keep["x"][:, t, :], ring.bank(job)[:, 0:D], keep["x"][:, t, :],
                                        ALU.add).then_inc(ring.freed_by(job), 1)


class BiasKeyFold:

    def __init__(self, ph):
        self.wq = [ph.sb(f"fold_wq{i}", [P, KT, H * DW]) for i in range(2)]
        self.bias_k = [ph.sb(f"fold_bias_k{i}", [P, H * DW]) for i in range(2)]
        self.loaded = [ph.sem(f"fold_loaded{i}") for i in range(2)]
        self.multiplied = [[ph.sem(f"fold_multiplied{i}{kt}") for kt in range(KT)] for i in range(2)]
        self.pieces = [(i, kt) for i in range(2) for kt in range(KT)]

    def load(self, sp, io):
        for i in range(2):
            sp.dma_start(self.bias_k[i][:, :], io[f"L1_bias_k{i + 1}"].partition_broadcast(P)).then_inc(self.loaded[i], 16)
            sp.dma_start(self.wq[i][:, :, :], io[f"L1_wq{i + 1}"].rearrange("(k p) n -> p k n", p=P)).then_inc(self.loaded[i], 16)

    def multiply(self, nc, engine, on, pieces):
        for i, kt in pieces:
            engine.wait_ge(self.loaded[i], 32)
            on.tensor_tensor(self.wq[i][:, kt, :], self.wq[i][:, kt, :], self.bias_k[i][:, :],
                             ALU.mult).then_inc(self.multiplied[i][kt], 1)

    def reduce(self, nc, dve, keep, i, kt):
        dve.wait_ge(self.multiplied[i][kt], 1)
        nc.vector.tensor_reduce(keep["folded"][:, i, kt, :], self.wq[i][:, kt, :].rearrange("p (h d) -> p h d", h=H),
                                AX.X, ALU.add)


def wide_attention(nc, io, keep, cfg):
    name, i = cfg["name"], cfg["index"]
    UN = 2 * B
    SK = S // P
    scale = float(DW) ** -0.5
    PROJ = [("q", 0), ("q", 1), ("k", 0, 0), ("k", 0, 1), ("k", 1, 0), ("k", 1, 1)] + [("v", t) for t in range(0, CT, 2)]
    SHARES = [PROJ[0:3], PROJ[3:6], PROJ[6:8], PROJ[8:10]]
    FIRST = PROJ[2:]
    with Phase(nc, name) as ph:
        stage = [ph.sb(f"stage{j}", [P, 2048]) for j in range(2)]
        w = [ph.hilo(f"w{j}", [P, 1536]) for j in range(2)]
        wo = [ph.hilo(f"wo{j}", [P, 2, D]) for j in range(2)]
        q = [ph.hilo(f"q{j}", [P, 2, ROWS]) for j in range(2)]
        k = [ph.hilo(f"k{j}", [P, 2, B * S]) for j in range(2)]
        v = [ph.hilo(f"v{j}", [P, CT, 2 * DW]) for j in range(2)]
        cols = ph.sb("cols", [P, 4, H])
        bk = ph.sb("bk", [P, H])
        out_bias = ph.sb("out_bias", [P, D])
        probs = ph.sb("probs", [P, 2, 2, S])
        probsT = [ph.hilo(f"probsT{j}", [P, 2 * SK * P]) for j in range(2)]
        attended = [ph.hilo(f"attended{j}", [P, Q]) for j in range(2)]
        top, neg_max, bias_shifted = ph.sb("top", [P, 2]), ph.sb("neg_max", [P, 2, 2]), ph.sb("bias_shifted", [P, 2, 2])
        row_sum, bias_prob, inverse = ph.sb("row_sum", [P, 2, 2]), ph.sb("bias_prob", [P, 2, 2]), ph.sb("inverse", [P, 2])
        bias_probs = ph.sb("bias_probs", [P, RT, P])
        bias_probsT = ph.sb("bias_probsT", [P, ROWS])
        parts = NormParts(ph, f"L1_ln{i}p", first=4)
        ones, bias_product = ph.sb("ones", [P, P]), ph.sb("bias_product", [P, H])
        banks = ph.psum(4)
        scores = ph.ctx.enter_context(nc.psum_tensor(f"{name}_scores", [P, 2, S], F32))
        sums = ph.ctx.enter_context(nc.psum_tensor(f"{name}_sums", [P, RT, D], F32))
        ring = ph.ring(banks)
        loaded, small_loaded = [ph.sem(f"loaded{j}") for j in range(2)], ph.sem("small_loaded")
        pool_done, w_ready, wo_ready = ph.sem("pool_done"), ph.sem("w_ready"), ph.sem("wo_ready")
        cols_scaled, out_done, scores_full = ph.sem("cols_scaled"), ph.sem("out_done"), ph.sem("scores_full")
        max_done, exp_done, normed, dve_done = ph.sem("max_done"), ph.sem("exp_done"), ph.sem("normed"), ph.sem("dve_done")
        sums_full = ph.sem("sums_full")
        first_loaded = [ph.sem(f"first_loaded{c}") for c in range(4)]
        first_hi, first_lo, ones_set, bias_ready = ph.sem("first_hi"), ph.sem("first_lo"), ph.sem("ones_set"), ph.sem("bias_ready")
        block = ph.block()
        LAST = PAIRS * UN - 1
        FIRST_ORDER = (1, 2, 0, 3)

        job_of, n = {}, 0
        for item in FIRST[:4] + ["norm0", "norm1"] + FIRST[4:] + PROJ[0:2] + ["bias_scores"]:
            job_of[(0, item) if item in PROJ else item] = n
            n += 1
        last_projection = lambda p: job_of[p, PROJ[-1] if p else PROJ[1]]
        for g in range(LAST + 2):
            p, u = divmod(g, UN)
            if g:
                for qt in range(2):
                    job_of["T", g - 1, qt] = n
                    n += 1
            if p + 1 < PAIRS:
                for item in SHARES[u]:
                    job_of[p + 1, item] = n
                    n += 1
            if g:
                job_of["V", g - 1] = n
                n += 1
        job_of["bias"] = n

        def unit(g):
            p, u = divmod(g, UN)
            return p % 2, u // B, u % B, 2 * p + u // B

        @block.sync
        def _(sp):
            for c in FIRST_ORDER:
                sp.dma_start(stage[0][:, c * 512:(c + 1) * 512],
                             io[f"L1_w{i}"][0][:, c * 512:(c + 1) * 512]).then_inc(first_loaded[c], 16)
                if c == 1:
                    parts.load(sp, io)
                    sp.dma_start(cols[:, :, :], io[f"L1_cols{i}"]).then_inc(small_loaded, 16)
                    sp.dma_start(bk[:, :], io[f"L1_bk{i}"]).then_inc(small_loaded, 16)
                    sp.dma_start(out_bias[:, :], io[f"L1_bo{i}"].partition_broadcast(P)).then_inc(small_loaded, 16)
            for p in range(1, PAIRS):
                if p == 2:
                    sp.wait_ge(first_lo, 3)
                if p >= 2:
                    sp.wait_ge(wo_ready, p - 1)
                sp.dma_start(stage[p % 2][:, :], io[f"L1_w{i}"][p]).then_inc(loaded[p % 2], 16)

        @block.gpsimd
        def _(pool):
            link = Chain(pool, pool_done)
            nc.gpsimd.memset(ones[:, :], 1.0).then_inc(ones_set, 1)
            nc.gpsimd.memset(bias_probs[:, :, :], 0.0).then_inc(ones_set, 1)
            parts.root(nc, pool)
            for p in range(PAIRS):
                j = p % 2
                if p:
                    pool.wait_ge(loaded[j], 16 * (p // 2 + p % 2))
                    link(nc.gpsimd.tensor_scalar(stage[j][:, 0:512], stage[j][:, 0:512], scale, 1.0, ALU.mult, ALU.mult))
                    if p >= 2:
                        pool.wait_ge(ring.full, last_projection(p - 2) + 1)
                    link(nc.gpsimd.tensor_scalar(w[j][0][:, :], stage[j][:, 0:1536], 1.0, 1.0, ALU.mult, ALU.mult))
                    nc.gpsimd.tensor_tensor(w[j][1][:, :], stage[j][:, 0:1536], raw(w[j][0][:, :]),
                                            ALU.subtract).then_inc(w_ready, 1)
                else:
                    pool.wait_ge(first_loaded[3], 16)
                if p >= 2:
                    pool.wait_ge(out_done, UN * (p - 1))
                part = stage[j][:, 1536:2048]
                link(nc.gpsimd.tensor_scalar(wo[j][0][:, :, :].rearrange("p h n -> p (h n)"), part, 1.0, 1.0, ALU.mult, ALU.mult))
                nc.gpsimd.tensor_tensor(wo[j][1][:, :, :].rearrange("p h n -> p (h n)"), part,
                                        raw(wo[j][0][:, :, :]).rearrange("p h n -> p (h n)"), ALU.subtract).then_inc(wo_ready, 1)

        @block.tensor
        def _(pe):
            def project(p, item):
                j, job = p % 2, job_of[p, item]
                wq, wk, wv = ([t[:, c * 512:(c + 1) * 512].rearrange("p (k n) -> p k n", k=KT) for t in w[j]] for c in range(3))
                ring.wait_bank(pe, job)
                for t in range(2 if item[0] == "v" else 1):
                    for kt in range(KT):
                        if item[0] == "q":
                            out = ring.bank(job)[:, :]
                            lhs, rhs = both(wq, np.s_[:, kt, item[1] * DW:(item[1] + 1) * DW]), both(keep["hT"], np.s_[:, kt, :])
                        elif item[0] == "k":
                            out = ring.bank(job)[:, :]
                            lhs = both(wk, np.s_[:, kt, item[1] * DW:(item[1] + 1) * DW])
                            rhs = both(keep["ctxT"], np.s_[:, kt, item[2] * S:(item[2] + 1) * S])
                        else:
                            out = ring.bank(job)[:, t * 2 * DW:(t + 1) * 2 * DW]
                            lhs = both(keep["ctxT"], np.s_[:, kt, (item[1] + t) * P:(item[1] + t + 1) * P])
                            rhs = both(wv, np.s_[:, kt, :])
                        last = product3(nc, out, lhs, rhs, kt == 0, kt == KT - 1)
                last.then_inc(ring.full, 1)

            def score(g):
                j, hh, b, h = unit(g)
                if g:
                    pe.wait_ge(exp_done, 3 * g - 1)
                for qt in range(2):
                    at = b * Q + qt * P
                    last = product3(nc, scores[:, qt, :], both(q[j], np.s_[:, hh, at:at + P]),
                                    both(k[j], np.s_[:, hh, b * S:(b + 1) * S]), True, True)
                last.then_inc(scores_full, 1)

            def transposes(g):
                for qt in range(2):
                    job = job_of["T", g, qt]
                    pe.wait_ge(normed, 2 * g + qt + 1)
                    ring.wait_bank(pe, job)
                    for kt in range(SK):
                        last = nc.tensor.transpose(ring.bank(job)[:, kt * P:(kt + 1) * P],
                                                   probs[:, g % 2, qt, kt * P:(kt + 1) * P], keep["ident"][:, :])
                    last.then_inc(ring.full, 1)

            def product_v(g):
                j, hh, b, h = unit(g)
                job = job_of["V", g]
                ring.wait_evacuated(pe, job_of["T", g, 0])
                ring.wait_evacuated(pe, job_of["T", g, 1])
                ring.wait_bank(pe, job)
                for kt in range(SK):
                    weights = [t[:, :].rearrange("p (q k n) -> p q k n", q=2, k=SK)[:, :, kt, :] for t in probsT[g % 2]]
                    last = product3(nc, ring.bank(job)[:, 0:Q], both(v[j], np.s_[:, b * SK + kt, hh * DW:(hh + 1) * DW]),
                                    weights, kt == 0, kt == SK - 1)
                last.then_inc(ring.full, 1)

            def output(g):
                j, hh, b, h = unit(g)
                pe.wait_ge(wo_ready, g // UN + 1)
                ring.wait_evacuated(pe, job_of["V", g])
                for qt in range(2):
                    last = product3(nc, sums[:, b * 2 + qt, :], both(attended[g % 2], np.s_[:, qt * P:(qt + 1) * P]),
                                    both(wo[j], np.s_[:, hh, :]), h == 0 and qt == 0, False, loose=True)
                last.then_inc(out_done, 1)

            for n, item in enumerate(FIRST):
                if n in (0, 4):
                    pe.wait_ge(first_lo, 1 if n == 0 else 2)
                project(0, item)
                if n == 3:
                    parts.transpose(nc, pe, ring, keep)
            ring.wait_evacuated(pe, job_of["norm0"])
            ring.wait_evacuated(pe, job_of["norm1"])
            pe.wait_ge(first_lo, 3)
            for item in PROJ[0:2]:
                project(0, item)
            job = job_of["bias_scores"]
            ring.wait_bank(pe, job)
            pe.wait_ge(bias_ready, 1)
            for t in range(RT):
                out = ring.bank(job)[:, t * H:(t + 1) * H]
                for kt in range(KT):
                    nc.tensor.matmul(out, parts.whole[:, kt, t * P:(t + 1) * P], keep["folded"][:, i - 1, kt, :],
                                     start=kt == 0, stop=False)
                last = nc.tensor.matmul(out, ones[:, :], bias_product[:, :], start=False, stop=True)
            last.then_inc(ring.full, 1)
            for g in range(LAST + 2):
                p, u = divmod(g, UN)
                if g <= LAST:
                    if u == 0:
                        for back in range(ring.n):
                            ring.wait_evacuated(pe, job_of[p, PROJ[-1 - back]] if p else job_of["bias_scores"] - back)
                        if p:
                            ring.wait_evacuated(pe, job_of[p, ("k", 1, 1)])
                            ring.wait_evacuated(pe, job_of[p, ("q", 1)])
                    score(g)
                if g:
                    transposes(g - 1)
                if p + 1 < PAIRS:
                    if u == 0:
                        pe.wait_ge(w_ready, p + 1)
                    for item in SHARES[u]:
                        project(p + 1, item)
                if g >= 2:
                    output(g - 2)
                if g:
                    product_v(g - 1)
            output(LAST)

            job = job_of["bias"]
            ring.wait_bank(pe, job)
            for t in range(RT):
                last = nc.tensor.transpose(ring.bank(job)[:, t * P:(t + 1) * P], bias_probs[:, t, :], keep["ident"][:, :])
            last.then_inc(ring.full, 1)
            ring.wait_evacuated(pe, job)
            for t in range(RT):
                last = nc.tensor.matmul(sums[:, t, :], bias_probsT[:, t * P:(t + 1) * P], keep["bias_values"][:, i - 1, :],
                                        start=False, stop=True, skip_group_check=True)
            last.then_inc(sums_full, 1)

        def destination(p, item):
            j = p % 2
            if item[0] == "q":
                return both(q[j], np.s_[:, item[1], :])
            if item[0] == "k":
                return both(k[j], np.s_[:, item[1], item[2] * S:(item[2] + 1) * S])
            return [t[:, item[1]:item[1] + 2, :].rearrange("p t n -> p (t n)") for t in v[j]]

        def bias_of(p, item):
            if item[0] == "v":
                return None
            return (cols[:, 0, :] if item[0] == "q" else bk[:, :])[:, 2 * p + item[1]:2 * p + item[1] + 1]

        @block.scalar
        def _(act):
            load_table(nc, keep, ACT.Exp)

            def high(job, out, column, n=512):
                act.wait_ge(ring.full, job + 1)
                source = ring.bank(job)[:, 0:n]
                if column is None:
                    nc.scalar.copy(out, source).then_inc(ring.hi_done, 1)
                else:
                    nc.scalar.activation(out, source, ACT.Identity, bias=column).then_inc(ring.hi_done, 1)

            for c in FIRST_ORDER[:3]:
                act.wait_ge(first_loaded[c], 16)
                nc.scalar.mul(w[0][0][:, c * 512:(c + 1) * 512], stage[0][:, c * 512:(c + 1) * 512],
                              1.0 if c else scale).then_inc(first_hi, 1)
            act.wait_ge(small_loaded, 48)
            act.wait_ge(cols_scaled, 1)
            for n, item in enumerate(FIRST + PROJ[0:2]):
                high(job_of[0, item], destination(0, item)[0], bias_of(0, item))
                if n == 3:
                    parts.scale(nc, act, ring)
            job = job_of["bias_scores"]
            act.wait_ge(ring.full, job + 1)
            nc.scalar.mul(keep["bias_scores"][:, :, :].rearrange("p t h -> p (t h)"), ring.bank(job)[:, 0:RT * H],
                          scale).then_inc(ring.hi_done, 1)
            for g in range(LAST + 2):
                p, u = divmod(g, UN)
                if g:
                    for qt in range(2):
                        high(job_of["T", g - 1, qt], probsT[(g - 1) % 2][0][:, qt * 512:(qt + 1) * 512], None)
                if g <= LAST:
                    act.wait_ge(max_done, g + 1)
                    for qt in range(2):
                        nc.scalar.activation(probs[:, g % 2, qt, :], scores[:, qt, :], ACT.Exp, bias=neg_max[:, g % 2, qt:qt + 1],
                                             accum_out=row_sum[:, g % 2, qt:qt + 1]).then_inc(exp_done, 1)
                    nc.scalar.activation(bias_prob[:, g % 2, :], bias_shifted[:, g % 2, :], ACT.Exp).then_inc(exp_done, 1)
                if p + 1 < PAIRS:
                    for item in SHARES[u]:
                        high(job_of[p + 1, item], destination(p + 1, item)[0], bias_of(p + 1, item))
                if g:
                    j, hh, b, h = unit(g - 1)
                    high(job_of["V", g - 1], attended[(g - 1) % 2][0][:, :], cols[:, 2, h:h + 1], Q)
            job = job_of["bias"]
            act.wait_ge(ring.full, job + 1)
            nc.scalar.copy(bias_probsT[:, :], ring.bank(job)[:, :]).then_inc(ring.freed_by(job), 1)

        @block.vector
        def _(dve):
            link = Chain(dve, dve_done)
            highs = [0]

            def low(job, out, column, n=512):
                highs[0] += 1
                dve.wait_ge(ring.hi_done, highs[0])
                source = ring.bank(job)[:, 0:n]
                if column is None:
                    nc.vector.tensor_tensor(out[1], source, raw(out[0]), ALU.subtract).then_inc(ring.freed_by(job), 1)
                else:
                    nc.vector.scalar_tensor_tensor(out[1], source, column, raw(out[0]), ALU.add,
                                                   ALU.subtract).then_inc(ring.freed_by(job), 1)

            def low_weights(n, c):
                dve.wait_ge(first_hi, n)
                part = np.s_[:, c * 512:(c + 1) * 512]
                nc.vector.scalar_tensor_tensor(w[0][1][part], stage[0][part], 1.0 if c else scale, raw(w[0][0][part]),
                                               ALU.mult, ALU.subtract).then_inc(first_lo, 1)

            norm_link = Chain(dve, parts.dve_done)
            parts.normalise(nc, dve, norm_link, keep["x"], 1e-5, True)
            for n, c in enumerate(FIRST_ORDER[:3]):
                low_weights(n + 1, c)
            dve.wait_ge(small_loaded, 48)
            link(nc.vector.tensor_tensor(bias_product[:, :], cols[:, 0, :], cols[:, 1, :], ALU.mult))
            nc.vector.tensor_scalar(cols[:, 0, :], cols[:, 0, :], scale, None, ALU.mult).then_inc(cols_scaled, 1)
            dve.wait_ge(cols_scaled, 1)
            dve.wait_ge(ones_set, 2)
            dve.wait_ge(parts.normed_ready, 1)
            for t in range(RT):
                last = nc.vector.tensor_tensor(keep["x"][:, t, :], keep["x"][:, t, :], out_bias[:, :], ALU.add)
            last.then_inc(bias_ready, 1)
            for n, item in enumerate(FIRST + PROJ[0:2]):
                low(job_of[0, item], destination(0, item), bias_of(0, item))
                if n == 3:
                    highs[0] += 2
                    parts.split(nc, dve, norm_link, ring, keep["hT"])
            job = job_of["bias_scores"]
            highs[0] += 1
            dve.wait_ge(ring.hi_done, highs[0])
            last = nc.vector.tensor_scalar(keep["neg_bias_scores"][:, :, :], keep["bias_scores"][:, :, :], -1.0, None, ALU.mult)
            last.then_inc(ring.freed_by(job), 1)
            ring.wait_evacuated(dve, job)
            for g in range(LAST + 2):
                p, u = divmod(g, UN)
                s = g % 2
                if g <= LAST:
                    j, hh, b, h = unit(g)
                    dve.wait_ge(scores_full, g + 1)
                    link(nc.vector.tensor_reduce(top[:, :], scores[:, :, :], AX.X, ALU.max))
                    link(nc.vector.scalar_tensor_tensor(neg_max[:, s, :], top[:, :], -1.0, keep["neg_bias_scores"][:, 2 * b:2 * b + 2, h],
                                                        ALU.mult, ALU.min))
                    nc.vector.tensor_tensor(bias_shifted[:, s, :], keep["bias_scores"][:, 2 * b:2 * b + 2, h], neg_max[:, s, :],
                                            ALU.add).then_inc(max_done, 1)
                if g:
                    for qt in range(2):
                        low(job_of["T", g - 1, qt], [t[:, qt * 512:(qt + 1) * 512] for t in probsT[(g - 1) % 2]], None)
                if g <= LAST:
                    dve.wait_ge(exp_done, 3 * (g + 1))
                    link(nc.vector.tensor_tensor(inverse[:, :], row_sum[:, s, :], bias_prob[:, s, :], ALU.add))
                    link(nc.vector.reciprocal(inverse[:, :], inverse[:, :]))
                    nc.vector.tensor_tensor(bias_probs[:, 2 * b:2 * b + 2, padded(h)], bias_prob[:, s, :], inverse[:, :], ALU.mult)
                    for qt in range(2):
                        nc.vector.tensor_scalar(probs[:, s, qt, :], probs[:, s, qt, :], inverse[:, qt:qt + 1], None,
                                                ALU.mult).then_inc(normed, 1)
                if p + 1 < PAIRS:
                    for item in SHARES[u]:
                        low(job_of[p + 1, item], destination(p + 1, item), bias_of(p + 1, item))
                if g:
                    j, hh, b, h = unit(g - 1)
                    low(job_of["V", g - 1], both(attended[(g - 1) % 2], np.s_[:, :]), cols[:, 2, h:h + 1], Q)
            dve.wait_ge(sums_full, 1)
            for t in range(RT):
                nc.vector.tensor_tensor(keep["x"][:, t, :], sums[:, t, :], keep["x"][:, t, :], ALU.add)


def program(nc, io):
    with ExitStack() as ctx:
        def sb(name, shape, dt=F32):
            return ctx.enter_context(nc.sbuf_tensor(name, shape, dt))

        keep = {"x": sb("x_rows", [P, RT, D]), "sum": sb("sum_rows", [P, RT, D]), "ident": sb("ident", [P, P]), "nowhere": sb("nowhere", [P, 1]),
                "bias_scores": sb("bias_scores", [P, RT, H]), "neg_bias_scores": sb("neg_bias_scores", [P, RT, H]),
                "bias_values": sb("bias_values", [P, 2, D]), "folded": sb("folded", [P, 2, KT, H])}
        for name, n in (("ctxT", B * S), ("latT", ROWS)):
            keep[name] = sb(name + "_hi", [P, KT, n], F32R), sb(name + "_lo", [P, KT, n], F32R)
        keep["stored"] = ctx.enter_context(nc.semaphore("stored"))
        keep["hT"] = keep["latT"]

        transpose_context(nc, io, keep)
        narrow_attention(nc, io, keep, dict(
            name="L0a", nk=S + Q, nan_if_masked=False, queries=keep["latT"], keys=[keep["ctxT"], keep["latT"]], mask="mask_ik0", mask_dtype=I32,
            w="L0_w", bias="L0_bias", out_bias="L0_bo", gate="L2_gate", gated=False, scale=1.0 / DN, in_place=False, bias_values=True, rows=False, lnp=None))
        mlp(nc, io, keep, dict(name="L0m", rows="sum", lnp="L0_lnp", eps=1e-6, centred=False, w="L0_wm", b1="L0_b1", b2="L0_b2",
                               gelu=ACT.Gelu_apprx_tanh, out=None, fold=True, context=None))
        for i in (1, 2):
            cfg = dict(name=f"L1a{i}", index=i)
            wide_attention(nc, io, keep, cfg)
        with Phase(nc, "L2") as ph:
            audT = ph.hilo("audT", [P, KT, B * S])
            mlp(nc, io, keep, dict(name="L1m", rows="x", lnp="L1_lnmp", eps=1e-5, centred=True, w="L1_wm", b1="L1_b1", b2="L1_b2",
                                   gelu=ACT.Gelu, out=None, fold=False, context=audT, context_lnp="L2_lnp"))
            narrow_attention(nc, io, keep, dict(
                name="L2a", nk=S, nan_if_masked=True, rows=True, lnp=None, queries=keep["hT"], keys=[audT], mask="mask_bf1", mask_dtype=U8,
                w="L2_w", bias="L2_bias", out_bias="L2_bo", gate="L2_gate", gated=True, scale=DN ** -0.5, in_place=True, bias_values=False))
        narrow_attention(nc, io, keep, dict(
            name="L3a", nk=S, nan_if_masked=False, rows=True, lnp="L3_ln1p", queries=keep["hT"], keys=[keep["ctxT"]], mask="mask_bf1", mask_dtype=U8,
            w="L3_w", bias="L3_bias", out_bias="L3_bo", gate="L2_gate", gated=False, scale=DN ** -0.5, in_place=True, bias_values=False))
        mlp(nc, io, keep, dict(name="L3m", rows="x", lnp="L3_ln2p", eps=1e-5, centred=True, w="L3_wm", b1="L3_b1", b2="L3_b2",
                               gelu=ACT.Gelu_apprx_tanh, out="out", fold=False, context=None))


def kernel(**inputs):
    import concourse.bacc as bacc
    from concourse.bass_utils import run_bass_kernel_spmd as run

    a = {name: np.asarray(value) for name, value in inputs.items()}

    def tiles(w):
        return w.reshape(-1, P, w.shape[1]).transpose(1, 0, 2)

    def columns(vector):
        return vector.reshape(-1, P).T

    def padded_heads(w):
        out = np.zeros((H, 32, w.shape[1]), w.dtype)
        out[:, 0:DN] = w.reshape(H, DN, -1)
        return out.reshape(H * 32, -1)

    def narrow(q, k, v, o):
        return np.concatenate([tiles(w).reshape(P, -1, 512) for w in (q, k, v, padded_heads(o))], axis=1)

    def narrow_bias(q, k, v):
        return np.concatenate([columns(q), columns(k), columns(padded_heads(v[:, None])[:, 0])], axis=1)

    def mlp_weights(w1, w2):
        return np.concatenate([tiles(w).reshape(P, -1, 512) for w in (w1, w2)], axis=1)

    zeros = np.zeros(D, np.float32)
    t = {"x": a["x"], "ctx_2048": a["ctx_2048"], "mask_ik0": a["mask_BxS2_ik0"].reshape(1, -1),
         "mask_bf1": a["mask_BxS2_bf1"].view(np.uint8).reshape(1, -1)}
    kv, kvb = (a[f"L0_xattn_kv_{n}"].reshape(-1, H, DN, 2) for n in "wb")
    key_value = [(kv[..., i].reshape(D, D), kvb[..., i].reshape(D)) for i in range(2)]
    t["L0_w"] = narrow(a["L0_xattn_q_w"], key_value[0][0], key_value[1][0], a["L0_xattn_out_w"])
    t["L0_bias"] = narrow_bias(a["L0_xattn_q_b"], key_value[0][1], key_value[1][1])
    t["L0_bo"] = a["L0_xattn_out_b"]
    t["L0_lnp"] = np.concatenate([columns(a["L0_xattn_postnorm_w"]), columns(zeros)], axis=1)
    t["L2_w"] = narrow(*(a[f"L2_xattn_W{n}"].T for n in "qkvo"))
    t["L2_bias"], t["L2_bo"], t["L2_gate"] = narrow_bias(zeros, zeros, zeros), zeros, a["L2_xattn_gate"]
    t["L2_lnp"] = np.concatenate([columns(a["L2_xattn_ln_gamma"]), columns(a["L2_xattn_ln_beta"])], axis=1)
    t["L3_w"] = narrow(*(a[f"L3_xattn_{n}_w"] for n in ("q", "k", "v", "cproj")))
    t["L3_bias"] = narrow_bias(*(a[f"L3_xattn_{n}_b"] for n in "qkv"))
    t["L3_bo"] = a["L3_xattn_cproj_b"]
    for n in (1, 2):
        t[f"L3_ln{n}p"] = np.concatenate([columns(a[f"L3_xattn_ln{n}_w"]), columns(a[f"L3_xattn_ln{n}_b"])], axis=1)
    for out, names in (("L0", ("mlp_w1", "mlp_b1", "mlp_w2", "mlp_b2")), ("L1", ("w_fc1", "b_fc1", "w_fc2", "b_fc2")),
                       ("L3", ("fc_w", "fc_b", "proj_w", "proj_b"))):
        w1, b1, w2, b2 = (a[f"{out}_xattn_{n}"] for n in names)
        t[f"{out}_wm"], t[f"{out}_b1"], t[f"{out}_b2"] = mlp_weights(w1, w2), columns(b1), b2
    for n in ("1", "2", "_mlp"):
        t[f"L1_ln{n.replace('_mlp', 'm')}p"] = np.concatenate(
            [columns(a[f"L1_xattn_ln{n}_scale"]), columns(a[f"L1_xattn_ln{n}_offset"])], axis=1)
    for n in (1, 2):
        wq, wk, wv, wo = (a[f"L1_xattn_w{m}{n}"] for m in "qkvo")
        by_pair = [tiles(w).reshape(P, KT, PAIRS, 2 * DW).transpose(2, 0, 1, 3).reshape(PAIRS, P, -1) for w in (wq, wk, wv)]
        by_pair.append(wo.reshape(PAIRS, 2, P, D).transpose(0, 2, 1, 3).reshape(PAIRS, P, -1))
        t[f"L1_w{n}"] = np.concatenate(by_pair, axis=2)
        t[f"L1_wq{n}"], t[f"L1_wo{n}"], t[f"L1_bias_k{n}"] = wq, wo, a[f"L1_xattn_bias_k{n}"].reshape(-1)
        t[f"L1_cols{n}"] = np.stack([columns(a[f"L1_xattn_{m}{n}"].reshape(-1)) for m in ("bq", "bias_k", "bv", "bias_v")], axis=1)
        t[f"L1_bk{n}"], t[f"L1_bo{n}"] = columns(a[f"L1_xattn_bk{n}"]), a[f"L1_xattn_bo{n}"]

    nc = bacc.Bacc("TRN2", target_bir_lowering=False, num_devices=1)
    arrays, io = {}, {}
    for name, value in t.items():
        arrays[f"in_{name}"] = np.ascontiguousarray(value)
        io[name] = nc.dram_tensor(f"in_{name}", value.shape, mybir.dt.from_np(value.dtype), kind="ExternalInput").ap()
    io["out"] = nc.dram_tensor("out_x", (B, Q, D), F32, kind="ExternalOutput").ap()
    program(nc, io)
    result = run(nc, [arrays], core_ids=[0])
    return result.results[0]["out_x"]
```
